# Optimizing a Trainium2 kernel written in Bass

```python
import numpy as np
import jax
import jax.numpy as jnp

def _softmax(x, axis=-1):
    return jax.nn.softmax(x, axis=axis)

def _gelu(x):
    return jax.nn.gelu(x, approximate=True)

def _silu(x):
    return jax.nn.silu(x)

def _sigmoid(x):
    return jax.nn.sigmoid(x)

def _layernorm(x, axis=-1, eps=1e-05):
    m = jnp.mean(x, axis=axis, keepdims=True)
    v = jnp.var(x, axis=axis, keepdims=True)
    return (x - m) / jnp.sqrt(v + eps)

def _scatter_add(tgt, idx, src, axis=0):
    return tgt.at[idx].add(src)

def _segment_sum(src, seg, n):
    return jax.ops.segment_sum(src, seg, n)
kernel_name = 'mk_perceiver_d2_seqx_r4_562645'

def setup_inputs(seed: int=0):
    np.random.seed(seed)
    _w = jnp.asarray

    def _rec_inputs():
        import jax
        import jax.numpy as jnp
        _rk = jax.random.key(seed)
        x = -0.0002928 + 1 * jax.random.normal(jax.random.fold_in(_rk, 1), (16, 64, 256), jnp.float32)
        _lenS = 64 - jax.random.randint(jax.random.fold_in(_rk, 7), (16,), 0, max(1, 64 // 4) + 1, jnp.int32)
        _lenS2 = 1601 - jax.random.randint(jax.random.fold_in(_rk, 8), (16,), 0, max(1, 1601 // 4) + 1, jnp.int32)
        _ctx_1024P = jax.random.normal(jax.random.fold_in(_rk, 11), (16, 16, 256), jnp.float32)
        _ctx_1024c = jax.random.dirichlet(jax.random.fold_in(_rk, 511), 0.3 * jnp.ones((16,), jnp.float32), (16, 1601))
        _ctx_1024t = jnp.einsum('bsk,bkd->bsd', _ctx_1024c, _ctx_1024P)
        _ctx_1024t = _ctx_1024t * jax.lax.rsqrt(jnp.mean(jnp.square(_ctx_1024t)) + 1e-12) * 0.953939
        ctx_1024 = -1.39393e-06 + 0.999914 * (_ctx_1024t + 0.3 * jax.random.normal(jax.random.fold_in(_rk, 611), (16, 1601, 256), jnp.float32))
        return (x, ctx_1024)
    x, ctx_1024 = _rec_inputs()

    def _L0_xattn_setup():
        import jax, jax.numpy as jnp
        import numpy as np
        MODEL_DIM = 256
        NUM_HEADS = 16
        HEAD_DIM = MODEL_DIM // NUM_HEADS
        SCALE = HEAD_DIM ** (-0.5)
        key = jax.random.key(seed)
        ks = jax.random.split(key, 8)
        B, LQ, LC = (2, 512, 512)
        std = MODEL_DIM ** (-0.5)
        return {'query': jax.random.normal(ks[0], (B, LQ, MODEL_DIM), jnp.float32), 'context': jax.random.normal(ks[1], (B, LC, MODEL_DIM), jnp.float32), 'Wq': jax.random.normal(ks[2], (MODEL_DIM, MODEL_DIM), jnp.float32) * std, 'bq': jnp.zeros((MODEL_DIM,), jnp.float32), 'Wkv': jax.random.normal(ks[3], (MODEL_DIM, 2 * MODEL_DIM), jnp.float32) * std, 'bkv': jnp.zeros((2 * MODEL_DIM,), jnp.float32), 'Wout': jax.random.normal(ks[4], (MODEL_DIM, MODEL_DIM), jnp.float32) * std, 'bout': jnp.zeros((MODEL_DIM,), jnp.float32)}
    _L0_xattn_all = _L0_xattn_setup()
    _L0_xattn_in = {k: v for k, v in _L0_xattn_all.items() if k in ('Wq', 'bq', 'Wkv', 'bkv', 'Wout', 'bout')}
    del _L0_xattn_all

    def _L0_attn_setup():
        import jax, jax.numpy as jnp
        import numpy as np
        H = 16

        def rotate_half(x):
            x1 = x[..., ::2]
            x2 = x[..., 1::2]
            return jnp.concatenate((-x2, x1), axis=-1)

        def rope_cache(n, hd):
            freqs = 10000.0 ** (-jnp.arange(0, hd, 2, dtype=jnp.float32) / hd)
            angles = jnp.arange(n, dtype=jnp.float32)[:, None] * freqs
            sin = jnp.sin(angles)
            cos = jnp.cos(angles)
            sin = jnp.stack([sin, sin], axis=-1).reshape(n, hd)
            cos = jnp.stack([cos, cos], axis=-1).reshape(n, hd)
            return (sin, cos)
        key = jax.random.key(seed)
        k1, k2, k3 = jax.random.split(key, 3)
        dim, inner = (256, 256)
        x = jax.random.normal(k1, (2, 512, dim), dtype=jnp.float32)
        w_qkv = jax.random.normal(k2, (dim, 3 * inner), dtype=jnp.float32) * dim ** (-0.5)
        w_out = jax.random.normal(k3, (inner, dim), dtype=jnp.float32) * inner ** (-0.5)
        b_out = jnp.zeros((dim,), dtype=jnp.float32)
        return {'x': x, 'w_qkv': w_qkv, 'w_out': w_out, 'b_out': b_out}
    _L0_attn_all = _L0_attn_setup()
    _L0_attn_in = {k: v for k, v in _L0_attn_all.items() if k in ('w_qkv', 'w_out', 'b_out')}
    del _L0_attn_all

    def _L0_ffn_setup():
        import jax, jax.numpy as jnp
        import numpy as np
        B, S, D = (1, 512, 256)
        E, K, F = (8, 2, 352)
        NS = 2
        SCALE = 2.5

        def _swiglu_mlp(x, wg, wu, wd):
            return jax.nn.silu(x @ wg) * (x @ wu) @ wd
        key = jax.random.key(seed)
        ks = jax.random.split(key, 8)
        s = 0.02
        return {'hidden_states': jax.random.normal(ks[0], (B, S, D), jnp.float32), 'gate_w': jax.random.normal(ks[1], (E, D), jnp.float32) * s, 'w_gate': jax.random.normal(ks[2], (E, D, F), jnp.float32) * s, 'w_up': jax.random.normal(ks[3], (E, D, F), jnp.float32) * s, 'w_down': jax.random.normal(ks[4], (E, F, D), jnp.float32) * s, 'sw_gate': jax.random.normal(ks[5], (D, F * NS), jnp.float32) * s, 'sw_up': jax.random.normal(ks[6], (D, F * NS), jnp.float32) * s, 'sw_down': jax.random.normal(ks[7], (F * NS, D), jnp.float32) * s}
    _L0_ffn_all = _L0_ffn_setup()
    _L0_ffn_in = {k: v for k, v in _L0_ffn_all.items() if k in ('gate_w', 'w_gate', 'w_up', 'w_down', 'sw_gate', 'sw_up', 'sw_down')}
    del _L0_ffn_all

    def _L1_xattn_setup():
        import jax, jax.numpy as jnp
        import numpy as np
        D1, D2, D3 = (256, 256, 256)
        key = jax.random.key(seed)
        k1, k2, kw, kb = jax.random.split(key, 4)
        x1 = jax.random.normal(k1, (8, 512, D1), dtype=jnp.float32)
        x2 = jax.random.normal(k2, (8, 512, D2), dtype=jnp.float32)
        bound = 1.0 / np.sqrt(D1 + D2)
        W = jax.random.uniform(kw, (D3, D1 + D2), minval=-bound, maxval=bound, dtype=jnp.float32)
        b = jax.random.uniform(kb, (D3,), minval=-bound, maxval=bound, dtype=jnp.float32)
        return {'x1': x1, 'x2': x2, 'W': W, 'b': b}
    _L1_xattn_all = _L1_xattn_setup()
    _L1_xattn_in = {k: v for k, v in _L1_xattn_all.items() if k in ('W', 'b')}
    del _L1_xattn_all

    def _L1_attn_setup():
        import jax, jax.numpy as jnp
        import numpy as np
        DIM = 256
        HEADS = 8
        DIM_QK = 64
        MAX_POS = 10
        SCALE = DIM_QK ** (-0.5)
        key = jax.random.key(seed)
        ks = jax.random.split(key, 6)
        b, n = (4, 512)
        x = jax.random.normal(ks[0], (b, n, DIM), dtype=jnp.float32)
        mask = jnp.ones((b, n), dtype=bool)
        s = DIM ** (-0.5)
        W_qk = jax.random.normal(ks[1], (DIM, DIM_QK * HEADS * 2), dtype=jnp.float32) * s
        W_v = jax.random.normal(ks[2], (DIM, DIM), dtype=jnp.float32) * s
        W_out = jax.random.normal(ks[3], (DIM, DIM), dtype=jnp.float32) * s
        b_out = jnp.zeros((DIM,), dtype=jnp.float32)
        conv = jax.random.normal(ks[4], (HEADS, 2 * MAX_POS + 1), dtype=jnp.float32) * 0.02
        return {'x': x, 'mask': mask, 'W_qk': W_qk, 'W_v': W_v, 'W_out': W_out, 'b_out': b_out, 'conv': conv}
    _L1_attn_all = _L1_attn_setup()
    _L1_attn_in = {k: v for k, v in _L1_attn_all.items() if k in ('mask', 'W_qk', 'W_v', 'W_out', 'b_out', 'conv')}
    del _L1_attn_all

    def _L1_ffn_setup():
        import jax, jax.numpy as jnp
        import numpy as np
        NUM_GEMMS = 8
        HIDDEN = 256
        INTER = 1024
        key = jax.random.key(seed)
        k_x, k_w1, k_b1, k_w2, k_b2 = jax.random.split(key, 5)
        x = jax.random.normal(k_x, (8, 512, HIDDEN), dtype=jnp.float32)
        s1 = 1.0 / np.sqrt(HIDDEN)
        s2 = 1.0 / np.sqrt(INTER)
        W1 = jax.random.uniform(k_w1, (NUM_GEMMS, INTER, HIDDEN), jnp.float32, -s1, s1)
        b1 = jax.random.uniform(k_b1, (NUM_GEMMS, INTER), jnp.float32, -s1, s1)
        W2 = jax.random.uniform(k_w2, (NUM_GEMMS, HIDDEN, INTER), jnp.float32, -s2, s2)
        b2 = jax.random.uniform(k_b2, (NUM_GEMMS, HIDDEN), jnp.float32, -s2, s2)
        return {'x': x, 'W1': W1, 'b1': b1, 'W2': W2, 'b2': b2}
    _L1_ffn_all = _L1_ffn_setup()
    _L1_ffn_in = {k: v for k, v in _L1_ffn_all.items() if k in ('W1', 'b1', 'W2', 'b2')}
    del _L1_ffn_all
    return {'x': x, 'ctx_1024': ctx_1024, 'L0_xattn_Wq': _L0_xattn_in['Wq'], 'L0_xattn_bq': _L0_xattn_in['bq'], 'L0_xattn_Wkv': _L0_xattn_in['Wkv'], 'L0_xattn_bkv': _L0_xattn_in['bkv'], 'L0_xattn_Wout': _L0_xattn_in['Wout'], 'L0_xattn_bout': _L0_xattn_in['bout'], 'L0_attn_w_qkv': _L0_attn_in['w_qkv'], 'L0_attn_w_out': _L0_attn_in['w_out'], 'L0_attn_b_out': _L0_attn_in['b_out'], 'L0_ffn_gate_w': _L0_ffn_in['gate_w'], 'L0_ffn_w_gate': _L0_ffn_in['w_gate'], 'L0_ffn_w_up': _L0_ffn_in['w_up'], 'L0_ffn_w_down': _L0_ffn_in['w_down'], 'L0_ffn_sw_gate': _L0_ffn_in['sw_gate'], 'L0_ffn_sw_up': _L0_ffn_in['sw_up'], 'L0_ffn_sw_down': _L0_ffn_in['sw_down'], 'L1_xattn_W': _L1_xattn_in['W'], 'L1_xattn_b': _L1_xattn_in['b'], 'L1_attn_mask': _L1_attn_in['mask'], 'L1_attn_W_qk': _L1_attn_in['W_qk'], 'L1_attn_W_v': _L1_attn_in['W_v'], 'L1_attn_W_out': _L1_attn_in['W_out'], 'L1_attn_b_out': _L1_attn_in['b_out'], 'L1_attn_conv': _L1_attn_in['conv'], 'L1_ffn_W1': _L1_ffn_in['W1'], 'L1_ffn_b1': _L1_ffn_in['b1'], 'L1_ffn_W2': _L1_ffn_in['W2'], 'L1_ffn_b2': _L1_ffn_in['b2']}

def reference(x, ctx_1024, L0_xattn_Wq, L0_xattn_bq, L0_xattn_Wkv, L0_xattn_bkv, L0_xattn_Wout, L0_xattn_bout, L0_attn_w_qkv, L0_attn_w_out, L0_attn_b_out, L0_ffn_gate_w, L0_ffn_w_gate, L0_ffn_w_up, L0_ffn_w_down, L0_ffn_sw_gate, L0_ffn_sw_up, L0_ffn_sw_down, L1_xattn_W, L1_xattn_b, L1_attn_mask, L1_attn_W_qk, L1_attn_W_v, L1_attn_W_out, L1_attn_b_out, L1_attn_conv, L1_ffn_W1, L1_ffn_b1, L1_ffn_W2, L1_ffn_b2):
    import jax
    import jax.numpy as jnp

    def _L0_xattn_ref(query, context, Wq, bq, Wkv, bkv, Wout, bout):
        import jax, jax.numpy as jnp
        import numpy as np
        MODEL_DIM = 256
        NUM_HEADS = 16
        HEAD_DIM = MODEL_DIM // NUM_HEADS
        SCALE = HEAD_DIM ** (-0.5)
        B, LQ, _ = query.shape
        LC = context.shape[1]
        H, D = (NUM_HEADS, HEAD_DIM)
        q = query @ Wq + bq
        kv = context @ Wkv + bkv
        kv = kv.reshape(B, LC, H, D, 2)
        k = jnp.transpose(kv[..., 0], (0, 2, 1, 3))
        v = jnp.transpose(kv[..., 1], (0, 2, 1, 3))
        q = jnp.transpose(q.reshape(B, LQ, H, D), (0, 2, 1, 3))
        scores = jnp.einsum('bhid,bhjd->bhij', q, k) * SCALE
        attn = jax.nn.softmax(scores, axis=-1)
        out = jnp.einsum('bhij,bhjd->bhid', attn, v)
        out = jnp.transpose(out, (0, 2, 1, 3)).reshape(B, LQ, H * D)
        return out @ Wout + bout

    def _L0_attn_ref(x, w_qkv, w_out, b_out):
        import jax, jax.numpy as jnp
        import numpy as np
        H = 16

        def rotate_half(x):
            x1 = x[..., ::2]
            x2 = x[..., 1::2]
            return jnp.concatenate((-x2, x1), axis=-1)

        def rope_cache(n, hd):
            freqs = 10000.0 ** (-jnp.arange(0, hd, 2, dtype=jnp.float32) / hd)
            angles = jnp.arange(n, dtype=jnp.float32)[:, None] * freqs
            sin = jnp.sin(angles)
            cos = jnp.cos(angles)
            sin = jnp.stack([sin, sin], axis=-1).reshape(n, hd)
            cos = jnp.stack([cos, cos], axis=-1).reshape(n, hd)
            return (sin, cos)
        b, n, dim = x.shape
        qkv = x @ w_qkv
        q, k, v = jnp.split(qkv, 3, axis=-1)
        heads = lambda t: t.reshape(b, n, H, -1).transpose(0, 2, 1, 3)
        q, k, v = (heads(q), heads(k), heads(v))
        hd = q.shape[-1]
        sin, cos = rope_cache(n, hd)
        q = q * cos + rotate_half(q) * sin
        k = k * cos + rotate_half(k) * sin
        scale = hd ** (-0.5)
        dots = jnp.einsum('bhid,bhjd->bhij', q, k) * scale
        attn = jax.nn.softmax(dots, axis=-1)
        out = jnp.einsum('bhij,bhjd->bhid', attn, v)
        out = out.transpose(0, 2, 1, 3).reshape(b, n, H * hd)
        return out @ w_out + b_out

    def _L0_ffn_ref(hidden_states, gate_w, w_gate, w_up, w_down, sw_gate, sw_up, sw_down):
        import jax, jax.numpy as jnp
        import numpy as np
        B, S, D = (1, 512, 256)
        E, K, F = (8, 2, 352)
        NS = 2
        SCALE = 2.5

        def _swiglu_mlp(x, wg, wu, wd):
            return jax.nn.silu(x @ wg) * (x @ wu) @ wd
        identity = hidden_states
        x = hidden_states.reshape(-1, hidden_states.shape[-1])
        T = x.shape[0]
        logits = x.astype(jnp.float32) @ gate_w.astype(jnp.float32).T
        scores = jax.nn.softmax(logits, axis=-1)
        topk_w, topk_i = jax.lax.top_k(scores, K)
        topk_w = topk_w / (topk_w.sum(-1, keepdims=True) + 1e-20) * SCALE
        combine = jnp.zeros((T, E), jnp.float32).at[jnp.arange(T)[:, None], topk_i].set(topk_w)
        g = jax.nn.silu(jnp.einsum('td,edf->etf', x, w_gate)) * jnp.einsum('td,edf->etf', x, w_up)
        expert_out = jnp.einsum('etf,efd->etd', g, w_down)
        y = jnp.einsum('te,etd->td', combine, expert_out).astype(x.dtype)
        y = y.reshape(identity.shape)
        return y + _swiglu_mlp(identity, sw_gate, sw_up, sw_down)

    def _L1_xattn_ref(x1, x2, W, b):
        import jax, jax.numpy as jnp
        import numpy as np
        D1, D2, D3 = (256, 256, 256)
        d1 = x1.shape[-1]
        W1 = W[:, :d1]
        W2 = W[:, d1:]
        part1 = jnp.einsum('bld,ed->ble', x1, W1)
        part2 = jnp.einsum('bld,ed->be', x2, W2) / x2.shape[1]
        return part1 + part2[:, None, :] + b

    def _L1_attn_ref(x, mask, W_qk, W_v, W_out, b_out, conv):
        import jax, jax.numpy as jnp
        import numpy as np
        DIM = 256
        HEADS = 8
        DIM_QK = 64
        MAX_POS = 10
        SCALE = DIM_QK ** (-0.5)
        b, n, _ = x.shape
        h, dqk = (HEADS, DIM_QK)
        dv = DIM // h
        qk = x @ W_qk
        q, k = jnp.split(qk, 2, axis=-1)
        v = x @ W_v
        q = q.reshape(b, n, h, dqk).transpose(0, 2, 1, 3)
        k = k.reshape(b, n, h, dqk).transpose(0, 2, 1, 3)
        v = v.reshape(b, n, h, dv).transpose(0, 2, 1, 3)
        dots = jnp.einsum('bhid,bhjd->bhij', q, k) * SCALE
        seq = jnp.arange(n)
        dist = jnp.clip(seq[None, :] - seq[:, None], -MAX_POS, MAX_POS) + MAX_POS
        bias = conv[:, dist]
        attn = jax.nn.softmax(dots + bias[None], axis=-1)
        out = jnp.einsum('bhij,bhjd->bhid', attn, v)
        out = out.transpose(0, 2, 1, 3).reshape(b, n, h * dv)
        return out @ W_out + b_out

    def _L1_ffn_ref(x, W1, b1, W2, b2):
        import jax, jax.numpy as jnp
        import numpy as np
        NUM_GEMMS = 8
        HIDDEN = 256
        INTER = 1024
        orig_shape = x.shape
        token_num = int(np.prod(orig_shape[:-1]))
        m = token_num // NUM_GEMMS
        xg = x.reshape(NUM_GEMMS, m, HIDDEN)
        h1 = jnp.einsum('gmh,goh->gmo', xg, W1) + b1[:, None, :]
        h2 = jnp.einsum('gmo,gho->gmh', h1, W2) + b2[:, None, :]
        return h2.reshape(orig_shape)
    x = x + _L0_xattn_ref(_layernorm(x, axis=-1), ctx_1024, L0_xattn_Wq, L0_xattn_bq, L0_xattn_Wkv, L0_xattn_bkv, L0_xattn_Wout, L0_xattn_bout)
    x = x + _L0_attn_ref(_layernorm(x, axis=-1), L0_attn_w_qkv, L0_attn_w_out, L0_attn_b_out)
    x = x + _L0_ffn_ref(_layernorm(x, axis=-1), L0_ffn_gate_w, L0_ffn_w_gate, L0_ffn_w_up, L0_ffn_w_down, L0_ffn_sw_gate, L0_ffn_sw_up, L0_ffn_sw_down)
    x = x + _L1_xattn_ref(_layernorm(x, axis=-1), ctx_1024, L1_xattn_W, L1_xattn_b)
    x = x + _L1_attn_ref(_layernorm(x, axis=-1), L1_attn_mask, L1_attn_W_qk, L1_attn_W_v, L1_attn_W_out, L1_attn_b_out, L1_attn_conv)
    x = x + _L1_ffn_ref(_layernorm(x, axis=-1), L1_ffn_W1, L1_ffn_b1, L1_ffn_W2, L1_ffn_b2)
    return x

_drawn_inputs = setup_inputs


def setup_inputs(seed=0):
    import zlib

    import numpy as np

    out = dict(_drawn_inputs(seed))
    spreads = {'L0_xattn_bq': (0.0, 0.32),
     'L0_xattn_bkv': (0.0, 0.1),
     'L0_xattn_bout': (0.0, 0.1),
     'L0_attn_b_out': (0.0, 0.1),
     'L1_attn_b_out': (0.0, 0.1)}
    factors = {'L0_ffn_sw_gate': 2.713,
     'L0_ffn_sw_down': 2.681,
     'L1_xattn_b': 2.748,
     'L1_attn_conv': 39.804,
     'L1_ffn_b1': 4.131,
     'L1_ffn_b2': 4.743}
    for name, (base, spread) in spreads.items():
        noise = np.random.default_rng([zlib.crc32(name.encode()), seed]).standard_normal(out[name].shape)
        drawn = base * np.exp(spread * noise) if base else spread * noise
        out[name] = jnp.asarray(drawn.astype(out[name].dtype))
    for name, factor in factors.items():
        out[name] = (out[name] * factor).astype(out[name].dtype)
    return out
```

```python
import concourse.bass as bass
from concourse import mybir
from contextlib import ExitStack

f32 = mybir.dt.float32
f32r = mybir.dt.float32r
ALU = mybir.AluOpType
ACT = mybir.ActivationFunctionType
AX = mybir.AxisListType

P = 128
D = 256
CH = D // P
B, S = 16, 64
T = B * S // P
NK = 1601
NKP = NK + 1
KT = -(-NK // P)
KLAST = NK - P * (KT - 1)
H0, D0 = 16, 16
VW = D0 + 1
VROW = H0 * VW + D0


def ge(eng, sem, value):
    if isinstance(value, int) and value <= 0:
        return
    eng.wait_ge(sem, value)


RING = ("K", "V", "Q", "E", "W")


def xattn_phase(b, h, fill, chain, late):
    out, fill, late = [], list(fill), dict(late)
    for u in range(8):
        out.append(("mx", b, h, u))
        if u >= 1 and fill:
            out.append(fill.pop(0))
    out += fill + chain[:2] + [("mt", b, h, 0)] + chain[2:]
    for g in range(7):
        out.append(("st", b, h, g))
        if g >= 1:
            out.append(("pv", b, h, g - 1))
        out += late.get(g, [])
    return out + [("pv", b, h, 6)]


def xattn_order(first, more):
    if_more = lambda x: x if more else []
    K = lambda b, h: [("K", b, h, u) for u in range(4)]
    V = lambda b, lo, hi: [("V", b, 0, u) for u in range(lo, hi)]
    split = lambda b: {1: [("cv", b, 0, 0)], 4: [("cv", b, 0, 1)]}
    o = []
    for b in range(2):
        queries = {2: [("Q", 2, 0, 0)], 5: [("Q", 2, 0, 1)]} if b == 1 and more else {}
        late = (split(b + 1) if b == 0 or more else {}) | queries
        k = K(b, 1)
        e = [("E", b - 1, 0, 0)] if b == 1 or not first else []
        w = [("W", -2, 0, 0), ("W", -2, 0, 1)] if b == 0 and not first else []
        o += xattn_phase(b, 0, [k[0]] + e + k[1:3] + w, [k[3]] + V(b, 4, 7), late)
        ahead = b == 0 or more
        o += xattn_phase(b, 1, K(b + 1, 0) if ahead else [], V(b + 1, 0, 4) if ahead else [], {})
    return o


XATTN_FIRST = ([("cv", 0, 0, k) for k in range(2)] + [("Q", 0, 0, 0), ("Q", 0, 0, 1)]
               + [("K", 0, 0, k) for k in range(4)] + [("V", 0, 0, v) for v in range(4)])
XATTN_LAST = [("E", 1, 0, 0), ("W", 0, 0, 0), ("W", 0, 0, 1)]
KCOLS = [(0, 512), (512, 1024), (1024, 1536), (1536, NKP)]
CVCOLS = [(0, 1024), (1024, NKP)]
MXCOLS, MXN = [0, 400, 800, NK - 402], 402
DMAS_KST = 24


def xattn(nc, X, lnT, c, w, ctxT, csum):
    ctx = ExitStack()
    with ctx:
        sb = lambda n, s, d=f32: ctx.enter_context(nc.sbuf_tensor(n, s, d))
        sem = lambda n: ctx.enter_context(nc.semaphore(n))
        raw = sb("xa_raw", [P, CH, NKP])
        ctx_hi, ctx_lo = sb("xa_ctx_hi", [P, CH, NKP], f32r), sb("xa_ctx_lo", [P, CH, NKP], f32r)
        kstage_hi, kstage_lo = sb("xa_kst_hi", [P, NKP], f32r), sb("xa_kst_lo", [P, NKP], f32r)
        KS = sb("xa_keys", [98, 8, NKP], f32r)
        QS = [sb(f"xa_queries{j}", [98, 8, P], f32r) for j in range(2)]
        Q96 = sb("xa_q96", [96, 8, P], f32r)
        qtmp = sb("xa_qtmp", [96, 4, P])
        V = [sb(f"xa_values{j}", [P, KT, VROW]) for j in range(2)]
        PTN = 4
        PT = [sb(f"xa_pt{j}", [P, 2, 512]) for j in range(PTN)]
        o_sb = sb("xa_o", [P, 4, S])
        rec = sb("xa_rec", [P, 4, S])
        oN = sb("xa_on", [P, 4, P])
        mx = sb("xa_mx", [P, 4, 4])
        nm = sb("xa_nm", [P, 4, 2])
        mhi = sb("xa_mhi", [P, 512], f32r)
        wtmp = sb("xa_wtmp", [P, CH, D])
        kraw = [wtmp[:].rearrange("p c n -> p (c n)"), sb("xa_kraw", [P, 512])[:]]
        wk = [sb(f"xa_wk{j}", [P, CH, D], f32r) for j in range(2)]
        wv = [sb(f"xa_wv{j}", [P, CH, D], f32r) for j in range(2)]
        wq96 = sb("xa_wq96", [P, CH, 8, 96])
        bq96 = sb("xa_bq96", [96, 8])
        bk = sb("xa_bk", [P, CH])
        bvq = sb("xa_bv", [P, 4])
        wo = sb("xa_wo", [P, 4, D])
        bo = sb("xa_bo", [P, D])
        SC = [ctx.enter_context(nc.psum_tensor(f"xa_sc{j}", [P, 2, 512], f32)) for j in range(2)]
        OP = [ctx.enter_context(nc.psum_tensor(f"xa_op{j}", [P, 512], f32)) for j in range(2)]
        PJ = [ctx.enter_context(nc.psum_tensor(f"xa_pj{j}", [P, 512], f32)) for j in range(2)]

        w_in, wk_in, wv_in = sem("xa_w_in"), sem("xa_wk_in"), sem("xa_wv_in")
        w_split, bo_in = sem("xa_w_split"), sem("xa_bo_in")
        raw_in, hi_done, lo_done = sem("xa_raw_in"), sem("xa_hi_done"), sem("xa_lo_done")
        full = {k: sem(f"xa_{k}_full") for k in RING}
        free = {k: sem(f"xa_{k}_free") for k in RING if k != "E"}
        khi, klo = sem("xa_khi"), sem("xa_klo")
        kst_in = [sem(f"xa_kst_in{h}") for h in range(2)]
        q_in = sem("xa_q_in")
        sc_full = {k: sem(f"xa_{k}_full") for k in ("mx", "st")}
        mx_done, nm_done, mt_full, mrow = sem("xa_mx_done"), sem("xa_nm_done"), sem("xa_mt_full"), sem("xa_mrow")
        ex_done, pv_done, o_ev = sem("xa_ex_done"), sem("xa_pv_done"), sem("xa_o_ev")
        rec_done, on_done = sem("xa_rec_done"), sem("xa_on_done")
        init, dch, pch, qch = sem("xa_init"), sem("xa_dch"), sem("xa_pch"), sem("xa_qch")

        PER = {"K": 8, "V": 7, "Q": 2, "E": 1, "W": 2, "mx": 16, "st": 14, "pv": 14, "mt": 2, "cv": 2}
        INNER = {"K": 4, "mx": 8, "st": 7, "pv": 7, "mt": 1}

        def nth(step, i):
            k, b, h, n = step
            if k in ("Q", "W"):
                return PER[k] * (i + b // 2) + (n + 1)
            return (i * (2 * PER[k])) + (PER[k] * b + INNER.get(k, 0) * h + n + 1)

        def z(i):
            return 0 if i is None else i

        def ptslot(step):
            return (nth(step, 0) - 1) % PTN

        START, MIDDLE, END = xattn_order(True, True), xattn_order(False, True), xattn_order(False, False)

        def past(order, n, i, kinds):
            before = []
            if order is not XATTN_FIRST:
                before = [(x, 0) for x in XATTN_FIRST]
            if order is MIDDLE or order is END or order is XATTN_LAST:
                before += [(x, i - 1) for x in START]
            if order is XATTN_LAST:
                before += [(x, i) for x in END]
            return [x for x in before + [(x, z(i)) for x in order[:n]] if x[0][0] in kinds]

        def ring_before(order, kinds, n, i):
            before = past(order, n, i, kinds)
            return before[-2] if len(before) >= 2 else None

        def bank(order, kinds, n, i):
            return len(past(order, n, 1, kinds)) % 2

        def walk(steps):
            steps[0](XATTN_FIRST, None)
            steps[0](START, 0)
            with steps[1].Fori(1, T - 1) as i:
                steps[0](MIDDLE, i)
            steps[0](END, T - 1)
            steps[0](XATTN_LAST, T - 1)

        block = ctx.enter_context(nc.Block())

        @block.sync
        def _(sp):
            sp.dma_start(raw[:, :, 0:NK], ctxT[0]).then_inc(raw_in, 16)
            sp.dma_start(wtmp[:], w["wv"]).then_inc(wv_in, 16)
            for dst, src in ((wq96, "wq"), (bq96, "bq"), (bk, "bk"), (bvq, "bv"), (wo, "wo")):
                sp.dma_start(dst[:], w[src]).then_inc(w_in, 16)
            sp.dma_start(bo[:], w["bo"].rearrange("(a n) -> a n", a=1).to_broadcast([P, D])).then_inc(bo_in, 16)
            sp.wait_ge(w_split, 2)
            sp.dma_start(wtmp[:], w["wk"]).then_inc(wk_in, 16)
            def steps(order, i):
                for n, step in enumerate(order):
                    k, b, h, u = step
                    if (k, u) == ("V", 3) and i is None or (k, h, u) == ("st", 1, 1) and order is not END:
                        b_ = 0 if i is None else b + 1
                        ge(sp, hi_done, nth(("cv", b_, 0, 1), z(i)) * 2)
                        ge(sp, lo_done, nth(("cv", b_, 0, 1), z(i)))
                        sp.dma_start(raw[:, :, 0:NK], ctxT[2 * z(i) + (b_ + 1)]).then_inc(raw_in, 16)
                    if k == "K" and u in (1, 3):
                        lo, hi = CVCOLS[u // 2]
                        ge(sp, klo, nth(step, z(i)))
                        for r, src in ((0, kstage_hi), (1, kstage_lo), (2, kstage_hi)):
                            for q in range(4):
                                sp.dma_start(KS[32 * r:32 * r + 32, 4 * h + q, lo:hi].bitcast(f32),
                                             src[32 * q:32 * q + 32, lo:hi].bitcast(f32)).then_inc(kst_in[h], 16)

            walk((steps, sp))

        @block.gpsimd
        def _(pool):
            nc.gpsimd.memset(raw[:, :, NK:NKP], 0.0).then_inc(init, 1)
            for j in range(2):
                nc.gpsimd.memset(V[j][:], 1.0).then_inc(init, 1)
            pool.wait_ge(bo_in, 16)
            for t in range(T):
                nc.gpsimd.tensor_tensor(X[:, t], X[:, t], bo[:], ALU.add).then_inc(init, 1)
            pool.wait_ge(w_in, 16 * 5)
            chain = [0]

            def steps(order, i):
                for n, step in enumerate(order):
                    k, b, h, u = step
                    if k == "cv":
                        ge(pool, hi_done, nth(step, z(i)) * 2)
                        lo, hi = CVCOLS[u]
                        nc.gpsimd.tensor_tensor(ctx_lo[:, :, lo:hi], raw[:, :, lo:hi],
                                                ctx_hi[:, :, lo:hi].bitcast(f32), ALU.subtract).then_inc(lo_done, 1)
                    if k == "K":
                        lo, hi = KCOLS[u]
                        ge(pool, khi, nth(step, z(i)))
                        nc.gpsimd.tensor_tensor(kstage_lo[:, lo:hi], kraw[u % 2][:, 0:hi - lo],
                                                kstage_hi[:, lo:hi].bitcast(f32), ALU.subtract).then_inc(klo, 1)
                    if (k, h, u) == ("mx", 0, 7) or (k, u) == ("Q", 1):
                        if k == "Q":
                            pair, tile_, want = 0, None, nth(step, z(i))
                            bat = 0 if i is None else 2 * (i + 1)
                        elif b == 0:
                            pair, want = 1, nth(("Q", 0, 0, 1), i)
                            bat = 2 * i + 1
                        else:
                            continue
                        ge(pool, free["Q"], want)
                        if not (i is None or (isinstance(i, int) and i == 0 and pair == 1)):
                            rel = 0 if pair == 0 else -1
                            ge(pool, sc_full["st"], nth(("st", rel, 1, 6), i))
                        for e in range(2):
                            nc.gpsimd.tensor_tensor(QS[pair][0:96, :, e * S:(e + 1) * S],
                                                    Q96[:, :, pair * S:(pair + 1) * S].bitcast(f32),
                                                    c["hmask"][0:96, e:e + 1].unsqueeze(1).to_broadcast([96, 8, S]),
                                                    ALU.mult).then_inc(q_in, 1)
                    if k == "E":
                        ge(pool, rec_done, nth(step, i))
                        if b == 0:
                            ge(pool, full["W"], nth(("W", -2, 0, 1), i))
                        nc.gpsimd.tensor_tensor(o_sb[:], o_sb[:], rec[:], ALU.mult).then_inc(pch, 1)
                        pool.wait_ge(pch, nth(step, i))
                        nc.gpsimd.tensor_tensor(oN[:, :, (b % 2) * S:(b % 2 + 1) * S], o_sb[:],
                                                bvq[:].unsqueeze(2).to_broadcast([P, 4, S]), ALU.add).then_inc(on_done, 1)

            walk((steps, pool))

        @block.scalar
        def _(act):
            act.wait_ge(w_in, 16 * 5)

            def steps(order, i):
                for n, step in enumerate(order):
                    k, b, h, u = step
                    if k == "cv":
                        lo, hi = CVCOLS[u]
                        ge(act, raw_in, 16 * (nth(("E", b, 0, 0), z(i))))
                        if i is None:
                            act.wait_ge(init, 1)
                        else:
                            ge(act, full["K"], nth(("K", b - 1, 1, 2 * u + 1), i))
                            if u == 1:
                                ge(act, full["V"], nth(("V", b - 1, 0, 6), i))
                        for ch in range(CH):
                            bat = 0 if i is None else 2 * i + b
                            nc.scalar.activation(ctx_hi[:, ch, lo:hi], raw[:, ch, lo:hi], ACT.Copy,
                                                 accum_out=csum[:, ch, u, bass.ds(bat, 1)]).then_inc(hi_done, 1)
                    elif k == "K":
                        lo, hi = KCOLS[u]
                        ge(act, full["K"], nth(step, z(i)))
                        if i is not None and u in (0, 2):
                            ph = (b - 1, 1) if h == 0 else (b, 0)
                            done = nth(("E", ph[0], 0, 0), i) * (16 * DMAS_KST)
                            ge(act, kst_in[ph[1]], done)
                        kr = kraw[u % 2]
                        ge(act, klo, nth(step, z(i)) - 2)
                        nc.scalar.activation(kr[:, 0:hi - lo], PJ[bank(order, RING, n, i)][:, 0:hi - lo],
                                             ACT.Identity, bias=bk[:, h:h + 1]).then_inc(free["K"], 1)
                        ge(act, free["K"], nth(step, z(i)))
                        nc.scalar.activation(kstage_hi[:, lo:hi], kr[:, 0:hi - lo], ACT.Copy).then_inc(khi, 1)
                    elif k == "V":
                        nt = 2 if u < 6 else 1
                        rows = P if u < 6 else KLAST
                        ge(act, full["V"], nth(step, z(i)))
                        if u == 0 and i is not None and not (isinstance(i, int) and i == 0 and b == 1):
                            ge(act, pv_done, nth(("pv", b - 2, 1, 6), i))
                        if i is None and u == 0:
                            act.wait_ge(init, 3)
                        vdst = V[b % 2][0:rows, 2 * u:2 * u + nt, 0:H0 * VW].rearrange("p k (h s) -> p k h s", s=VW)[:, :, :, 0:D0]
                        vsrc = PJ[bank(order, RING, n, i)][0:rows, 0:nt * D].rearrange("p (k h s) -> p k h s", k=nt, s=D0)
                        for kk in range(nt):
                            ins = nc.scalar.activation(vdst[:, kk], vsrc[:, kk], ACT.Copy)
                        ins.then_inc(free["V"], 1)
                    elif k == "st":
                        nt = 2 if u < 6 else 1
                        rows = P if u < 6 else KLAST
                        ge(act, sc_full["st"], nth(step, i))
                        j = nth(step, 0) - 1
                        ge(act, pv_done, nth(step, i) - PTN)
                        nc.scalar.activation(PT[ptslot(step)][0:rows, 0:nt], SC[bank(order, ("mx", "st"), n, i)][0:rows, 0:nt],
                                             ACT.Exp, scale=float(D0) ** -0.5).then_inc(ex_done, 1)

            walk((steps, act))

        @block.vector
        def _(dve):
            for src, dst in ((wv_in, wv), (wk_in, wk)):
                dve.wait_ge(src, 16)
                nc.vector.tensor_copy(dst[0][:], wtmp[:]).then_inc(w_split, 1)
                dve.wait_ge(w_split, 1 if dst is wv else 3)
                nc.vector.tensor_tensor(dst[1][:], wtmp[:], dst[0][:].bitcast(f32), ALU.subtract).then_inc(w_split, 1)
                dve.wait_ge(w_split, 2 if dst is wv else 4)
            nc.vector.memset(KS[96:98].bitcast(f32), 1.0).then_inc(w_split, 1)
            dve.wait_ge(w_in, 16 * 5)

            def steps(order, i):
                for n, step in enumerate(order):
                    k, b, h, u = step
                    if k == "mx":
                        ge(dve, sc_full["mx"], nth(step, i))
                        if u == 0:
                            ge(dve, nm_done, nth(("mt", b, h, 0), i) * 2 - 2)
                        nc.vector.tensor_reduce(mx[:, u // 2, 2 * (u % 2):2 * (u % 2) + 2],
                                                SC[bank(order, ("mx", "st"), n, i)][:, :, 0:MXN], AX.X, ALU.max).then_inc(mx_done, 1)
                        if u == 7:
                            dve.wait_ge(mx_done, nth(step, i))
                            ge(dve, mt_full, nth(("mt", b, h, 0), i) - 1)
                            for e in range(2):
                                nc.vector.tensor_reduce(nm[:, :, e:e + 1], mx[:], AX.X, ALU.max, negate=True).then_inc(nm_done, 1)
                    elif k == "mt":
                        ge(dve, mt_full, nth(step, i))
                        ge(dve, mrow, nth(step, i) - 1)
                        nc.vector.tensor_copy(mhi[96:98], OP[h][96:98]).then_inc(dch, 1)
                        dve.wait_ge(dch, nth(step, i))
                        nc.vector.scalar_tensor_tensor(QS[b % 2][96:98, 4 * h:4 * h + 4, :], mhi[96:98].bitcast(f32).rearrange("p (a n) -> p a n", a=4),
                                                       c["mrow"][96:98, 0:1], OP[h][96:98].rearrange("p (a n) -> p a n", a=4),
                                                       ALU.mult, ALU.add).then_inc(mrow, 1)
                    elif k == "Q":
                        ge(dve, full["Q"], nth(step, z(i)))
                        qs = slice(4 * u, 4 * u + 4)
                        q0 = nth(step, z(i))
                        ge(dve, free["Q"], q0 - 1)
                        nc.vector.tensor_tensor(qtmp[:], PJ[bank(order, RING, n, i)][0:96].rearrange("p (a n) -> p a n", a=4),
                                                bq96[:, qs].unsqueeze(2).to_broadcast([96, 4, P]), ALU.add).then_inc(qch, 1)
                        dve.wait_ge(qch, q0 * 2 - 1)
                        if i is not None:
                            ge(dve, q_in, (i + 1) * 4)
                        nc.vector.tensor_copy(Q96[:, qs], qtmp[:]).then_inc(qch, 1)
                        dve.wait_ge(qch, q0 * 2)
                        nc.vector.tensor_tensor(Q96[64:96, qs], qtmp[64:96], Q96[64:96, qs].bitcast(f32), ALU.subtract).then_inc(free["Q"], 1)
                    elif k == "E":
                        ge(dve, full["E"], nth(step, i))
                        ge(dve, on_done, nth(step, i) - 1)
                        nc.vector.reciprocal(rec[:], PJ[bank(order, RING, n, i)][:, 0:4 * S].rearrange("p (a n) -> p a n", a=4)).then_inc(rec_done, 1)
                    elif k == "W":
                        ge(dve, full["W"], nth(step, i))
                        dve.wait_ge(init, 3 + T)
                        xs = X[:, bass.ds(i + b // 2, 1), u * P:(u + 1) * P].rearrange("p a n -> p (a n)")
                        nc.vector.tensor_tensor(xs, xs, PJ[bank(order, RING, n, i)][:, 0:P], ALU.add).then_inc(free["W"], 1)
                    elif k == "pv" and u == 6:
                        ge(dve, pv_done, nth(step, i))
                        ge(dve, on_done, nth(("E", b, 0, 0), i) - 1)
                        nc.vector.tensor_copy(o_sb[:, 2 * h:2 * h + 2], OP[h][:, 0:2 * S].rearrange("p (a n) -> p a n", a=2)).then_inc(o_ev, 1)

            walk((steps, dve))

        @block.tensor
        def _(pe):
            mm = nc.tensor.matmul
            pe.wait_ge(w_split, 5)
            pe.wait_ge(w_in, 16 * 5)

            def split_product(out, lh, rh):
                terms = [(a, b_) for a, b_ in zip(lh, rh)]
                todo = []
                for l, r in terms:
                    todo += [(l[0], r[0]), (l[0], r[1]), (l[1], r[0])]
                for n_, (l, r) in enumerate(todo):
                    last = mm(out, l, r, start=n_ == 0, stop=n_ == len(todo) - 1)
                return last

            def steps(order, i):
                for n, step in enumerate(order):
                    k, b, h, u = step
                    if k in RING:
                        before = ring_before(order, RING, n, i)
                        if before:
                            (bk_, j) = before
                            ge(pe, free_of(bk_[0]), nth(bk_, j))
                        dst = PJ[bank(order, RING, n, i)]
                    if k == "K":
                        lo, hi = KCOLS[u]
                        if u in (0, 2) and h == 0:
                            ge(pe, hi_done, nth(("cv", b, 0, u // 2), z(i)) * 2)
                            ge(pe, lo_done, nth(("cv", b, 0, u // 2), z(i)))
                        hs = slice(h * P, (h + 1) * P)
                        split_product(dst[:, 0:hi - lo], [(wk[0][:, ch, hs], wk[1][:, ch, hs]) for ch in range(CH)],
                                      [(ctx_hi[:, ch, lo:hi], ctx_lo[:, ch, lo:hi]) for ch in range(CH)]).then_inc(full["K"], 1)
                    elif k == "V":
                        for kk in range(2 if u < 6 else 1):
                            kt = 2 * u + kk
                            rows = P if kt < KT - 1 else KLAST
                            cs = slice(kt * P, kt * P + rows)
                            last = split_product(dst[0:rows, kk * D:(kk + 1) * D], [(ctx_hi[:, ch, cs], ctx_lo[:, ch, cs]) for ch in range(CH)],
                                                 [(wv[0][:, ch, :], wv[1][:, ch, :]) for ch in range(CH)])
                        last.then_inc(full["V"], 1)
                    elif k == "Q":
                        for a in range(4):
                            for ch in range(CH):
                                tok = bass.ds(0, P) if i is None else bass.ds((i + 1) * P, P)
                                last = mm(dst[0:96, a * P:(a + 1) * P], wq96[:, ch, 4 * u + a], lnT[:, ch, tok], start=ch == 0, stop=ch == CH - 1)
                        last.then_inc(full["Q"], 1)
                    elif k == "E":
                        ge(pe, o_ev, nth(step, i) * 2)
                        mm(dst[:, 0:4 * S], c["spread"][:], o_sb[:].rearrange("p a n -> p (a n)"), start=True, stop=True).then_inc(full["E"], 1)
                    elif k == "W":
                        if u == 0:
                            ge(pe, on_done, nth(("E", b + 1, 0, 0), i))
                        for q in range(4):
                            last = mm(dst[:, 0:P], oN[:, q], wo[:, q, u * P:(u + 1) * P], start=q == 0, stop=q == 3)
                        last.then_inc(full["W"], 1)
                    elif k == "mx":
                        wait_slot(order, n, i)
                        if u == 0:
                            ge(pe, kst_in[h], nth(("E", b, 0, 0), i) * (16 * DMAS_KST))
                            if h == 0:
                                ge(pe, q_in, nth(("E", b, 0, 0), i) * 2)
                        pr = 4 * h + u // 2
                        for kk in range(2):
                            lo = MXCOLS[2 * (u % 2) + kk]
                            last = mm(SC[bank(order, ("mx", "st"), n, i)][:, kk, 0:MXN], QS[b % 2][0:96, pr, :], KS[0:96, pr, lo:lo + MXN], start=True, stop=True)
                        last.then_inc(sc_full["mx"], 1)
                    elif k == "mt":
                        ge(pe, nm_done, nth(step, i) * 2)
                        ge(pe, o_ev, nth(step, i) - 2)
                        for a in range(4):
                            last = mm(OP[h][96:98, a * P:(a + 1) * P], nm[:, a, :], c["ident"][:], start=True, stop=True, tile_position=(0, 96))
                        last.then_inc(mt_full, 1)
                    elif k == "st":
                        wait_slot(order, n, i)
                        if u == 0:
                            ge(pe, mrow, nth(("mt", b, h, 0), i))
                        for kk in range(2 if u < 6 else 1):
                            kt = 2 * u + kk
                            rows = P if kt < KT - 1 else KLAST
                            for a in range(4):
                                last = mm(SC[bank(order, ("mx", "st"), n, i)][0:rows, kk, a * P:(a + 1) * P],
                                          KS[:, 4 * h + a, kt * P:kt * P + rows], QS[b % 2][:, 4 * h + a, :], start=True, stop=True)
                        last.then_inc(sc_full["st"], 1)
                    elif k == "pv":
                        ge(pe, ex_done, nth(("st", b, h, u), i))
                        for kk in range(2 if u < 6 else 1):
                            kt = 2 * u + kk
                            rows = P if kt < KT - 1 else KLAST
                            for a in range(2):
                                for j in range(4):
                                    hd = 8 * h + 4 * a + j
                                    last = mm(OP[h][32 * j:32 * j + 32, a * S:(a + 1) * S],
                                              V[b % 2][0:rows, kt, hd * VW:hd * VW + 32],
                                              PT[ptslot(("st", b, h, u))][0:rows, kk, (4 * a + j) * S:(4 * a + j + 1) * S],
                                              start=kt == 0 and a == 0, stop=kt == KT - 1, tile_position=(0, 32 * j), skip_group_check=True)
                        last.then_inc(pv_done, 1)

            def free_of(kind):
                return free[kind] if kind != "E" else rec_done

            def wait_slot(order, n, i):
                before = ring_before(order, ("mx", "st"), n, i)
                if isinstance(i, int) and i == 0 and sum(x[0] in ("mx", "st") for x in order[:n]) < 2:
                    return
                (x, j) = before
                ge(pe, mx_done if x[0] == "mx" else ex_done, nth(x, j))

            walk((steps, pe))


LN_SEMS = ("stat", "var", "std", "norm", "tr", "ev_dve", "ev_act", "row_in", "row_added", "hi", "lo")


def layer_norm(nc, k, sems, X, lnT, c, bias=None, row=16, lnH=None, lnL=None):
    ctx = ExitStack()
    with ctx:
        sb = lambda n, s, d=f32: ctx.enter_context(nc.sbuf_tensor(f"ln{k}_{n}", s, d))
        stat, var_done, std_done, norm, tr, ev_dve, ev_act, row_in, row_added, hi_done, lo_done = [sems[n] for n in LN_SEMS]
        s0, n0, t0, e0 = k * (2 * T + 1), k * T, 4 * k, 2 * k
        stats, mv = sb("stats", [P, T, 6]), sb("mv", [P, T, 2])
        var, std, rstd = sb("var", [P, T]), sb("std", [P, T]), sb("rstd", [P, T])
        y = sb("y", [P, T, D])
        brow = sb("brow", [P, D])
        PS = [ctx.enter_context(nc.psum_tensor(f"ln{k}_ps{j}", [P, 512], f32)) for j in range(4)]
        block = ctx.enter_context(nc.Block())

        @block.sync
        def _(sp):
            if bias is not None:
                sp.dma_start(brow[:], bias.rearrange("(a n) -> a n", a=1).to_broadcast([P, D])).then_inc(row_in, 16)

        @block.vector
        def _(dve):
            for t in range(T):
                nc.vector.bn_stats(stats[:, t], X[:, t]).then_inc(stat, 1)
            for t in range(T):
                dve.wait_ge(stat, s0 + t + 1)
                nc.vector.bn_aggr(mv[:, t], stats[:, t]).then_inc(stat, 1)
            dve.wait_ge(stat, s0 + 2 * T)
            nc.vector.tensor_scalar(var[:], mv[:, :, 1], 1e-5, None, ALU.add).then_inc(var_done, 1)
            dve.wait_ge(std_done, k + 1)
            nc.vector.reciprocal(rstd[:], std[:]).then_inc(stat, 1)
            dve.wait_ge(stat, s0 + 2 * T + 1)
            for t in range(T):
                nc.vector.tensor_scalar(y[:, t], X[:, t], mv[:, t, 0:1], rstd[:, t:t + 1], ALU.subtract, ALU.mult).then_inc(norm, 1)
            for g in (1, 3):
                dve.wait_ge(tr, t0 + g + 1)
                nc.vector.tensor_copy(lnT[:, g % 2, (g // 2) * 512:(g // 2) * 512 + 512], PS[g][:]).then_inc(ev_dve, 1)

        @block.scalar
        def _(act):
            act.wait_ge(var_done, k + 1)
            nc.scalar.activation(std[:], var[:], ACT.Sqrt).then_inc(std_done, 1)
            for g in (0, 2):
                act.wait_ge(tr, t0 + g + 1)
                nc.scalar.activation(lnT[:, g % 2, (g // 2) * 512:(g // 2) * 512 + 512], PS[g][:], ACT.Copy).then_inc(ev_act, 1)
            if lnH is not None:
                act.wait_ge(ev_act, e0 + 2)
                act.wait_ge(ev_dve, e0 + 2)
                for ch in range(CH):
                    nc.scalar.activation(lnH[:, ch], lnT[:, ch], ACT.Copy).then_inc(hi_done, 1)

        @block.tensor
        def _(pe):
            for g in range(4):
                for a in range(4):
                    t = 4 * (g // 2) + a
                    pe.wait_ge(norm, n0 + t + 1)
                    last = nc.tensor.transpose(PS[g][:, a * P:(a + 1) * P], y[:, t, (g % 2) * P:(g % 2 + 1) * P], c["ident"])
                last.then_inc(tr, 1)

        @block.gpsimd
        def _(pool):
            if bias is not None:
                pool.wait_ge(row_in, row)
                for t in range(T):
                    pool.wait_ge(norm, n0 + t + 1)
                    nc.gpsimd.tensor_tensor(X[:, t], X[:, t], brow[:], ALU.add).then_inc(row_added, 1)
            if lnH is not None:
                for ch in range(CH):
                    pool.wait_ge(hi_done, ch + 1)
                    nc.gpsimd.tensor_tensor(lnL[:, ch], lnT[:, ch], lnH[:, ch].bitcast(f32), ALU.subtract).then_inc(lo_done, 1)


def self_attention(nc, tag, X, lnT, c, w, heads, dk, dv, rope=False, conv_bias=None):
    NCH = heads * dk // P
    HC = P // dk
    NP = heads // 2
    NB = heads // 4
    VC = D + 32 - dv
    N = NP * 2 * S
    ctx = ExitStack()
    with ctx:
        sb = lambda n, s, d=f32: ctx.enter_context(nc.sbuf_tensor(f"{tag}_{n}", s, d))
        sem = lambda n: ctx.enter_context(nc.semaphore(f"{tag}_{n}"))
        names = ["q", "k"] + (["qr", "kr"] if rope else [])
        W = {n: sb("w" + n, [P, CH, heads * dk]) for n in names}
        wv, wo = sb("wv", [P, CH, D]), sb("wo", [P, NB, D])
        QT, KTt = sb("QT", [P, NCH, T * P]), sb("KT", [P, NCH, T * P])
        rot = sb("rot", [P, 512])
        Vall = sb("Vall", [P, T, D])
        Kt, Vt = sb("Kt", [P, NCH, P]), sb("Vt", [P, VC])
        Qm = sb("Qm", [P, NCH, 2, HC, S])
        Sc, Pr = sb("Sc", [P, NP, 2, S]), sb("Pr", [P, NP, 2, S])
        PT = sb("PT", [P, NP, P])
        mxt, sm, rs = sb("mx", [P, NP, 2]), sb("sm", [P, NP, 2]), sb("rs", [P, NP, 2])
        oS = sb("oS", [P, NB, P])
        bank = lambda n: ctx.enter_context(nc.psum_tensor(f"{tag}_{n}", [P, 512], f32))
        SP_ = ctx.enter_context(nc.psum_tensor(f"{tag}_SP", [P, NP, 2, S], f32))
        TP = ctx.enter_context(nc.psum_tensor(f"{tag}_TP", [P, NP, P], f32))
        OP = [bank(f"OP{j}") for j in range(2)]
        WP = bank("WP")
        PJ = [OP[0], OP[1]]
        w_in, cb_in, pj, pj_free, v_done = sem("w_in"), sem("cb_in"), sem("pj"), sem("pj_free"), sem("v_done")
        dch, kv_in, q_in = sem("dch"), sem("kv_in"), sem("q_in")
        s_full, exp_done, p_done, bias_done = sem("s_full"), sem("exp_done"), sem("p_done"), sem("bias_done")
        mx_done, sub_done, sum_done, rcp_done = sem("mx_done"), sem("sub_done"), sem("sum_done"), sem("rcp_done")
        t_full, t_ev, o_full, o_ev, y_full, y_ev = [sem(x) for x in ("t_full", "t_ev", "o_full", "o_ev", "y_full", "y_ev")]
        v_pad = sem("v_pad")
        if conv_bias is not None:
            conv, scratch = conv_bias
            ext = sb("ext", [heads, 2 * S - 1])
            CB = sb("CB", [P, NP, S])
            ext_done, ext_out = sem("ext_done"), sem("ext_out")
            NPOS = conv.shape[1]
            E0 = S - 1 - NPOS // 2
        nproj = len(names) * NCH * 2
        if rope:
            order = [(n + r, ch, g) for n in "qk" for ch in range(NCH) for g in range(2) for r in ("", "r")]
        else:
            order = [(n, ch, g) for n in "qk" for ch in range(NCH) for g in range(2)]
        block = ctx.enter_context(nc.Block())

        @block.sync
        def _(sp):
            for n in names:
                sp.dma_start(W[n][:], w[n]).then_inc(w_in, 16)
            sp.dma_start(wv[:], w["v"]).then_inc(w_in, 16)
            sp.dma_start(wo[:], w["o"]).then_inc(w_in, 16)
            if conv_bias is not None:
                sp.dma_start(ext[:, E0:E0 + NPOS], conv).then_inc(cb_in, 16)
                sp.wait_ge(ext_done, 2)
                L = 2 * S - 1
                sp.dma_start(scratch.rearrange("h (r l) -> h r l", l=L), ext[:].unsqueeze(1).to_broadcast([heads, S, L])).then_inc(ext_out, 16)
                sp.wait_ge(ext_out, 16)
                for h in range(heads):
                    e, pr = h % 2, h // 2
                    src = scratch[h, S - 1:S - 1 + S * (L - 1)].rearrange("(r l) -> r l", l=L - 1)[:, 0:S]
                    sp.dma_start(CB[e * S:(e + 1) * S, pr, :], src).then_inc(cb_in, 16)

        @block.tensor
        def _(pe):
            mm = nc.tensor.matmul
            pe.wait_ge(w_in, 16 * (len(names) + 2))
            for n, (name, ch, g) in enumerate(order):
                if n >= 2:
                    pe.wait_ge(pj_free, n - 1)
                for k in range(CH):
                    last = mm(PJ[n % 2][:], W[name][:, k, ch * P:(ch + 1) * P], lnT[:, k, g * 512:(g + 1) * 512], start=k == 0, stop=k == CH - 1)
                last.then_inc(pj, 1)
            for t in range(T):
                n = nproj + t
                if t >= 2:
                    pe.wait_ge(v_done, t - 1)
                else:
                    pe.wait_ge(pj_free, n - 1)
                for k in range(CH):
                    last = mm(PJ[n % 2][:, 0:D], lnT[:, k, t * P:(t + 1) * P], wv[:, k, :], start=k == 0, stop=k == CH - 1)
                last.then_inc(pj, 1)
            pe.wait_ge(v_done, T)

            def scores(t):
                pe.wait_ge(kv_in, t * 2 + 1)
                pe.wait_ge(q_in, t * (HC * NCH) + HC * NCH)
                if conv_bias is None:
                    ge(pe, sub_done, t)
                else:
                    ge(pe, bias_done, t * 2)
                for pr in range(NP):
                    ch, q = 2 * pr // HC, 2 * pr % HC
                    for b in range(2):
                        last = mm(SP_[:, pr, b, :], Qm[:, ch, b, q:q + 2].rearrange("p e s -> p (e s)"), Kt[:, ch, b * S:(b + 1) * S],
                                  start=True, stop=True)
                last.then_inc(s_full, 1)

            def weigh(t):
                pe.wait_ge(p_done, t + 1)
                ge(pe, t_ev, t)
                pe.wait_ge(kv_in, t * 2 + 2)
                ge(pe, o_ev, t * 2)
                for pr in range(NP):
                    last = nc.tensor.transpose(TP[:, pr, :], Pr[:, pr].rearrange("p b s -> p (b s)"), c["ident"])
                last.then_inc(t_full, 1)
                pe.wait_ge(v_pad, 1)
                pe.wait_ge(t_ev, t + 1)
                for b in range(2):
                    for h in range(heads):
                        j, blk = h % 4, h // 4
                        last = mm(OP[b][32 * j:32 * j + 32, blk * S:(blk + 1) * S], Vt[b * S:(b + 1) * S, h * dv:h * dv + 32],
                                  PT[b * S:(b + 1) * S, h // 2, (h % 2) * S:(h % 2 + 1) * S], start=True, stop=True,
                                  tile_position=(b * S, 32 * j))
                last.then_inc(o_full, 1)
                pe.wait_ge(o_ev, t * 2 + 2)
                ge(pe, y_ev, t)
                for blk in range(NB):
                    last = mm(WP[:, 0:D], oS[:, blk, :], wo[:, blk, :], start=blk == 0, stop=blk == NB - 1)
                last.then_inc(y_full, 1)

            scores(0)
            with pe.Fori(1, T) as t:
                scores(t)
                weigh(t - 1)
            weigh(T - 1)

        @block.gpsimd
        def _(pool):
            nc.gpsimd.memset(Vt[:], 0.0).then_inc(v_pad, 1)
            pool.wait_ge(v_pad, 1)
            pool.wait_ge(pj_free, nproj)
            pool.wait_ge(v_done, T)

            def tile_in(t):
                tok = bass.ds(t * P, P)
                ge(pool, s_full, t)
                nc.gpsimd.tensor_copy(Kt[:], KTt[:, :, tok]).then_inc(kv_in, 1)
                for e in range(HC):
                    for ch in range(NCH):
                        nc.gpsimd.tensor_tensor(Qm[:, ch, :, e, :], QT[:, ch, tok].rearrange("p (b s) -> p b s", b=2),
                                                w["mask"][:, e:e + 1].unsqueeze(1).to_broadcast([P, 2, S]),
                                                ALU.mult).then_inc(q_in, 1)
                ge(pool, o_full, t)
                nc.gpsimd.tensor_copy(Vt[:, 0:D], Vall[:, bass.ds(t, 1), :].rearrange("p a n -> p (a n)")).then_inc(kv_in, 1)

            tile_in(0)
            with pool.Fori(1, T) as t:
                tile_in(t)

        @block.vector
        def _(dve):
            if conv_bias is not None:
                dve.wait_ge(cb_in, 16)
                nc.vector.tensor_copy(ext[:, 0:E0], ext[:, E0:E0 + 1].to_broadcast([heads, E0])).then_inc(ext_done, 1)
                nc.vector.tensor_copy(ext[:, E0 + NPOS:], ext[:, E0 + NPOS - 1:E0 + NPOS].to_broadcast([heads, E0])).then_inc(ext_done, 1)
            links = 0
            for n, (name, ch, g) in enumerate(order):
                dst = (QT if name[0] == "q" else KTt)[:, ch, g * 512:(g + 1) * 512]
                dve.wait_ge(pj, n + 1)
                if not rope:
                    nc.vector.tensor_copy(dst, PJ[n % 2][:]).then_inc(pj_free, 1)
                    continue
                wide = lambda a: a.rearrange("p (b s) -> p b s", s=S)
                table = c["sin" if name[1:] else "cos"].unsqueeze(1).to_broadcast([P, 512 // S, S])
                if not name[1:]:
                    nc.vector.tensor_tensor(wide(dst), wide(PJ[n % 2][:]), table, ALU.mult).then_inc(pj_free, 1)
                else:
                    ge(dve, dch, links)
                    nc.vector.tensor_tensor(wide(rot[:]), wide(PJ[n % 2][:]), table, ALU.mult).then_inc(pj_free, 1)
                    dve.wait_ge(pj_free, n + 1)
                    nc.vector.tensor_tensor(dst, dst, rot[:], ALU.add).then_inc(dch, 1)
                    links += 1
            for t in range(T):
                dve.wait_ge(pj, nproj + t + 1)
                nc.vector.tensor_copy(Vall[:, t], PJ[(nproj + t) % 2][:, 0:D]).then_inc(v_done, 1)
            if conv_bias is not None:
                dve.wait_ge(cb_in, 16 * (heads + 1))
            flat = lambda a: a.rearrange("p a b s -> p (a b) s")
            rows = lambda a: a.rearrange("p a b -> p (a b)")
            spread = lambda a: rows(a).unsqueeze(2).to_broadcast([P, NP * 2, S])

            def softmax(t):
                dve.wait_ge(s_full, t + 1)
                ge(dve, exp_done, t)
                src = SP_
                if conv_bias is not None:
                    for b in range(2):
                        nc.vector.scalar_tensor_tensor(Sc[:, :, b, :], SP_[:, :, b, :], float(dk) ** -0.5, CB[:],
                                                       ALU.mult, ALU.add).then_inc(bias_done, 1)
                    dve.wait_ge(bias_done, t * 2 + 2)
                    src = Sc
                nc.vector.tensor_reduce(rows(mxt[:]), flat(src[:]), AX.X, ALU.max).then_inc(mx_done, 1)
                dve.wait_ge(mx_done, t + 1)
                nc.vector.tensor_tensor(flat(Sc[:]), flat(src[:]), spread(mxt[:]), ALU.subtract).then_inc(sub_done, 1)
                dve.wait_ge(exp_done, t + 1)
                nc.vector.tensor_reduce(rows(sm[:]), flat(Pr[:]), AX.X, ALU.add).then_inc(sum_done, 1)
                dve.wait_ge(sum_done, t + 1)
                ge(dve, p_done, t)
                nc.vector.reciprocal(rs[:], sm[:]).then_inc(rcp_done, 1)
                dve.wait_ge(rcp_done, t + 1)
                nc.vector.tensor_tensor(flat(Pr[:]), flat(Pr[:]), spread(rs[:]), ALU.mult).then_inc(p_done, 1)

            def finish(t):
                dve.wait_ge(o_full, t + 1)
                ge(dve, y_full, t)
                for b in range(2):
                    nc.vector.tensor_copy(oS[:, :, b * S:(b + 1) * S], OP[b][:, 0:NB * S].rearrange("p (a s) -> p a s", s=S)).then_inc(o_ev, 1)
                dve.wait_ge(y_full, t + 1)
                xs = X[:, bass.ds(t, 1), :].rearrange("p a n -> p (a n)")
                nc.vector.tensor_tensor(xs, xs, WP[:, 0:D], ALU.add).then_inc(y_ev, 1)

            softmax(0)
            with dve.Fori(1, T) as t:
                softmax(t)
                finish(t - 1)
            finish(T - 1)

        @block.scalar
        def _(act):
            def exps(t):
                act.wait_ge(sub_done, t + 1)
                ge(act, t_full, t)
                nc.scalar.activation(Pr[:], Sc[:], ACT.Exp, scale=float(dk) ** -0.5 if conv_bias is None else 1.0).then_inc(exp_done, 1)

            def turned(t):
                act.wait_ge(t_full, t + 1)
                ge(act, o_full, t)
                nc.scalar.activation(PT[:], TP[:], ACT.Copy).then_inc(t_ev, 1)

            exps(0)
            with act.Fori(1, T) as t:
                exps(t)
                turned(t - 1)
            turned(T - 1)


FE = 352
NE = 8
NX = NE + 2
TOPK = 2
ROUTED_SCALE = 2.5
FCH = [(0, P), (P, 2 * P), (2 * P, FE)]


def experts(nc, tag, X, lnT, lnH, lnL, c, w):
    ctx = ExitStack()
    with ctx:
        sb = lambda n, s, d=f32: ctx.enter_context(nc.sbuf_tensor(f"{tag}_{n}", s, d))
        sem = lambda n: ctx.enter_context(nc.semaphore(f"{tag}_{n}"))
        gate = sb("gate", [P, CH, NE])
        lg, sc8, pk, t8 = [sb(n, [P, T, NE]) for n in ("lg", "sc8", "pk", "t8")]
        g1, g2 = sb("g1", [P, T * NE, NE]), sb("g2", [P, T * NE, NE])
        m8, s8 = sb("m8", [P, T]), sb("s8", [P, T])
        comb = sb("comb", [P, T, NX])
        gu_raw = [sb(f"gu_raw{j}", [P, CH, 2, FE]) for j in range(2)]
        dn_raw = [sb(f"dn_raw{j}", [P, 3, D]) for j in range(2)]
        gu = [[sb(f"gu{j}{k}", [P, CH, 2, FE], f32r) for k in range(2)] for j in range(2)]
        dn = [[sb(f"dn{j}{k}", [P, 3, D], f32r) for k in range(2)] for j in range(2)]
        h = [[sb(f"h{j}{k}", [P, 3, T * P], f32r) for k in range(2)] for j in range(2)]
        sg = [sb(f"sg{j}", [P, 512]) for j in range(2)]
        h32 = [sb(f"h32{j}", [P, 512]) for j in range(2)]
        GU = [ctx.enter_context(nc.psum_tensor(f"{tag}_GU{j}", [P, 2, 512], f32)) for j in range(2)]
        DN = [ctx.enter_context(nc.psum_tensor(f"{tag}_DN{j}", [P, 2, D], f32)) for j in range(2)]
        LG = ctx.enter_context(nc.psum_tensor(f"{tag}_LG", [P, T, NE], f32))
        gate_in, lg_full, r, rexp = sem("gate_in"), sem("lg_full"), sem("r"), sem("rexp")
        gu_in, dn_in = [[sem(f"{n}{j}") for j in range(2)] for n in ("gu_in", "dn_in")]
        gu_hi, gu_lo, dn_hi, dn_lo = sem("gu_hi"), sem("gu_lo"), sem("dn_hi"), sem("dn_lo")
        gu_full, silu_done, mul_done, hhi_done, hlo_done = [sem(x) for x in ("gu_full", "silu", "mul", "hhi", "hlo")]
        dn_full, dn_read = sem("dn_full"), sem("dn_read")
        UN = [(f, g) for f in range(3) for g in range(2)]
        NU, ND = len(UN), T // 2
        block = ctx.enter_context(nc.Block())

        def over_experts(eng, ahead, behind):
            def two(i):
                ahead(i * 2 + 1, 1)
                behind(i * 2, 0)
                ahead(i * 2 + 2, 0)
                behind(i * 2 + 1, 1)

            ahead(0, 0)
            two(0)
            with eng.Fori(1, NX // 2 - 1) as i:
                two(i)
            ahead(NX - 1, 1)
            behind(NX - 2, 0)
            behind(NX - 1, 1)

        def over_splits(eng, units, split_gu, split_dn):
            def two(i, last=False):
                for j in range(2):
                    e = i * 2 + j
                    units(e, j)
                    if not (last and j == 1):
                        split_dn(e + 1, 1 - j)
                    if not last:
                        split_gu(e + 2, j)

            split_gu(0, 0)
            split_gu(1, 1)
            split_dn(0, 0)
            two(0)
            with eng.Fori(1, NX // 2 - 1) as i:
                two(i)
            two(NX // 2 - 1, last=True)

        @block.sync
        def _(sp):
            sp.dma_start(gate[:], w["gate"]).then_inc(gate_in, 16)

            def load(e, j):
                ge(sp, gu_lo, e - 1)
                sp.dma_start(gu_raw[j][:], w["gu"][e]).then_inc(gu_in[j], 16)
                ge(sp, dn_lo, e - 1)
                sp.dma_start(dn_raw[j][:], w["down"][e]).then_inc(dn_in[j], 16)

            load(0, 0)
            load(1, 1)
            with sp.Fori(1, NX // 2) as i:
                load(i * 2, 0)
                load(i * 2 + 1, 1)

        @block.tensor
        def _(pe):
            mm = nc.tensor.matmul
            pe.wait_ge(gate_in, 16)
            for t in range(T):
                for k in range(CH):
                    last = mm(LG[:, t, :], lnT[:, k, t * P:(t + 1) * P], gate[:, k, :], start=k == 0, stop=k == CH - 1)
            last.then_inc(lg_full, 1)

            def split_product(out, pairs):
                todo = [x for (lh, ll), (rh, rl) in pairs for x in ((lh, rh), (lh, rl), (ll, rh))]
                for n, (l, r_) in enumerate(todo):
                    last = mm(out, l, r_, start=n == 0, stop=n == len(todo) - 1)
                return last

            def up(e, j):
                pe.wait_ge(gu_lo, e + 1)
                for n, (f, g) in enumerate(UN):
                    lo, hi = FCH[f]
                    ge(pe, mul_done, e * NU + (n - 1))
                    for x in range(2):
                        last = split_product(GU[n % 2][0:hi - lo, x, :], [
                            ((gu[j][0][:, k, x, lo:hi], gu[j][1][:, k, x, lo:hi]),
                             (lnH[:, k, g * 512:(g + 1) * 512], lnL[:, k, g * 512:(g + 1) * 512])) for k in range(CH)])
                    last.then_inc(gu_full, 1)

            def down(e, j):
                pe.wait_ge(hlo_done, e * NU + NU)
                pe.wait_ge(dn_lo, e + 1)
                for n in range(ND):
                    ge(pe, dn_read, e * T + (2 * n - 2))
                    for a in range(2):
                        tok = slice((2 * n + a) * P, (2 * n + a + 1) * P)
                        last = split_product(DN[n % 2][:, a, :], [
                            ((h[j][0][0:hi - lo, f, tok], h[j][1][0:hi - lo, f, tok]), (dn[j][0][0:hi - lo, f, :], dn[j][1][0:hi - lo, f, :]))
                            for f, (lo, hi) in enumerate(FCH)])
                    last.then_inc(dn_full, 1)

            over_experts(pe, up, down)

        @block.scalar
        def _(act):
            def split_gu(e, j):
                act.wait_ge(gu_in[j], e * 8 + (16 - 8 * j))
                if not (isinstance(e, int) and e < 2):
                    act.wait_ge(gu_full, e * NU - NU)
                nc.scalar.activation(gu[j][0][:], gu_raw[j][:], ACT.Copy).then_inc(gu_hi, 1)

            def split_dn(e, j):
                act.wait_ge(dn_in[j], e * 8 + (16 - 8 * j))
                if not (isinstance(e, int) and e < 2):
                    act.wait_ge(dn_full, e * ND - ND)
                nc.scalar.activation(dn[j][0][:], dn_raw[j][:], ACT.Copy).then_inc(dn_hi, 1)

            def units(e, j):
                for n, (f, g) in enumerate(UN):
                    lo, hi = FCH[f]
                    act.wait_ge(gu_full, e * NU + (n + 1))
                    ge(act, mul_done, e * NU + (n - 1))
                    nc.scalar.activation(sg[n % 2][0:hi - lo], GU[n % 2][0:hi - lo, 0, :], ACT.Silu).then_inc(silu_done, 1)
                    if n >= 1:
                        hi_part(e, j, n - 1)
                hi_part(e, j, NU - 1)

            def hi_part(e, j, n):
                f, g = UN[n]
                lo, hi = FCH[f]
                act.wait_ge(mul_done, e * NU + (n + 1))
                if n == 0 and not (isinstance(e, int) and e < 2):
                    act.wait_ge(dn_full, e * ND - ND)
                nc.scalar.activation(h[j][0][0:hi - lo, f, g * 512:(g + 1) * 512], h32[n % 2][0:hi - lo], ACT.Copy).then_inc(hhi_done, 1)

            act.wait_ge(lg_full, 1)
            act.wait_ge(r, 2)
            nc.scalar.activation(sc8[:], lg[:], ACT.Exp).then_inc(rexp, 1)
            over_splits(act, units, split_gu, split_dn)

        @block.gpsimd
        def _(pool):
            def lower(e, j, part, raw, hi, lo):
                pool.wait_ge(hi, e + 1)
                nc.gpsimd.tensor_tensor(part[j][1][:], raw[j][:], part[j][0][:].bitcast(f32), ALU.subtract).then_inc(lo, 1)

            def split_gu(e, j):
                lower(e, j, gu, gu_raw, gu_hi, gu_lo)

            def split_dn(e, j):
                lower(e, j, dn, dn_raw, dn_hi, dn_lo)

            def units(e, j):
                for n, (f, g) in enumerate(UN):
                    lo, hi = FCH[f]
                    pool.wait_ge(hhi_done, e * NU + (n + 1))
                    s_ = slice(g * 512, (g + 1) * 512)
                    nc.gpsimd.tensor_tensor(h[j][1][0:hi - lo, f, s_], h32[n % 2][0:hi - lo], h[j][0][0:hi - lo, f, s_].bitcast(f32),
                                            ALU.subtract).then_inc(hlo_done, 1)

            over_splits(pool, units, split_gu, split_dn)

        @block.vector
        def _(dve):
            n_ = [0]

            def step(ins):
                n_[0] += 1
                ins.then_inc(r, 1)
                dve.wait_ge(r, n_[0])

            over8 = lambda a: a.unsqueeze(2).to_broadcast([P, T, NE])
            V = nc.vector
            dve.wait_ge(lg_full, 1)
            step(V.tensor_reduce(m8[:], LG[:], AX.X, ALU.max))
            step(V.tensor_tensor(lg[:], LG[:], over8(m8[:]), ALU.subtract))
            dve.wait_ge(rexp, 1)
            step(V.tensor_reduce(s8[:], sc8[:], AX.X, ALU.add))
            step(V.reciprocal(m8[:], s8[:]))
            step(V.tensor_tensor(sc8[:], sc8[:], over8(m8[:]), ALU.mult))
            for t in range(T):
                ts = slice(t * NE, (t + 1) * NE)
                mine = sc8[:, t].unsqueeze(2).to_broadcast([P, NE, NE])
                other = sc8[:, t].unsqueeze(1).to_broadcast([P, NE, NE])
                V.tensor_tensor(g1[:, ts], other, mine, ALU.is_gt).then_inc(r, 1)
                V.tensor_tensor(g2[:, ts], other, mine, ALU.is_equal).then_inc(r, 1)
                n_[0] += 2
            dve.wait_ge(r, n_[0])
            g2v = g2[:].rearrange("p (t e) j -> p t (e j)", t=T)
            step(V.tensor_tensor(g2v, g2v, c["lower"].unsqueeze(1).to_broadcast([P, T, NE * NE]), ALU.mult))
            step(V.tensor_tensor(g1[:], g1[:], g2[:], ALU.add))
            step(V.tensor_reduce(pk[:].rearrange("p t e -> p (t e)"), g1[:], AX.X, ALU.add))
            step(V.tensor_scalar(t8[:], pk[:], float(TOPK), None, ALU.is_lt))
            step(V.tensor_tensor(pk[:], sc8[:], t8[:], ALU.mult))
            step(V.tensor_reduce(s8[:], pk[:], AX.X, ALU.add))
            step(V.tensor_scalar(m8[:], s8[:], 1e-20, None, ALU.add))
            step(V.reciprocal(s8[:], m8[:]))
            step(V.tensor_scalar(m8[:], s8[:], ROUTED_SCALE, None, ALU.mult))
            step(V.tensor_tensor(comb[:, :, 0:NE], pk[:], over8(m8[:]), ALU.mult))
            step(V.memset(comb[:, :, NE:NX], 1.0))

            def units(e, j):
                for n, (f, g) in enumerate(UN):
                    lo, hi = FCH[f]
                    dve.wait_ge(silu_done, e * NU + (n + 1))
                    ge(dve, hlo_done, e * NU + (n - 1))
                    V.tensor_tensor(h32[n % 2][0:hi - lo], sg[n % 2][0:hi - lo], GU[n % 2][0:hi - lo, 1, :], ALU.mult).then_inc(mul_done, 1)

            def add(e, j):
                for n in range(ND):
                    dve.wait_ge(dn_full, e * ND + (n + 1))
                    for a in range(2):
                        t = 2 * n + a
                        ge(dve, dn_read, e * T + (t - T + 1))
                        V.scalar_tensor_tensor(X[:, t], DN[n % 2][:, a, :], comb[:, t, bass.ds(e, 1)], X[:, t], ALU.mult, ALU.add).then_inc(dn_read, 1)

            over_experts(dve, units, add)


def mean_context(nc, tag, X, lnT, c, w, csum):
    ctx = ExitStack()
    with ctx:
        sb = lambda n, s, d=f32: ctx.enter_context(nc.sbuf_tensor(f"{tag}_{n}", s, d))
        sem = lambda n: ctx.enter_context(nc.semaphore(f"{tag}_{n}"))
        w1, w2 = sb("w1", [P, CH, D]), sb("w2", [P, CH, D])
        mean = sb("mean", [P, CH, B])
        wide = sb("wide", [P, CH, B, S])
        PS = [ctx.enter_context(nc.psum_tensor(f"{tag}_ps{j}", [P, 512], f32)) for j in range(2)]
        w_in, m, mdone, full, read = sem("w_in"), sem("m"), sem("mdone"), sem("full"), sem("read")
        block = ctx.enter_context(nc.Block())

        @block.sync
        def _(sp):
            sp.dma_start(w1[:], w["w1"]).then_inc(w_in, 16)
            sp.dma_start(w2[:], w["w2"]).then_inc(w_in, 16)

        @block.gpsimd
        def _(pool):
            nc.gpsimd.tensor_tensor(mean[:], csum[:, :, 0], csum[:, :, 1], ALU.add).then_inc(m, 1)
            pool.wait_ge(m, 1)
            for k in range(CH):
                nc.gpsimd.tensor_scalar(wide[:, k], mean[:, k].unsqueeze(2).to_broadcast([P, B, S]), 1.0 / NK, None, ALU.mult).then_inc(mdone, 1)

        @block.tensor
        def _(pe):
            pe.wait_ge(w_in, 32)
            pe.wait_ge(mdone, CH)
            wv = wide[:].rearrange("p c b s -> p c (b s)")
            for t in range(T):
                ge(pe, read, t - 1)
                tok = slice(t * P, (t + 1) * P)
                for n in range(2 * CH):
                    l, r_ = (lnT[:, n, tok], w1[:, n, :]) if n < CH else (wv[:, n - CH, tok], w2[:, n - CH, :])
                    last = nc.tensor.matmul(PS[t % 2][:, 0:D], l, r_, start=n == 0, stop=n == 2 * CH - 1)
                last.then_inc(full, 1)

        @block.vector
        def _(dve):
            for t in range(T):
                dve.wait_ge(full, t + 1)
                nc.vector.tensor_tensor(X[:, t], X[:, t], PS[t % 2][:, 0:D], ALU.add).then_inc(read, 1)


def grouped_ffn(nc, tag, X, lnT, c, w, out):
    F = 1024
    NF = F // P
    ctx = ExitStack()
    with ctx:
        sb = lambda n, s, d=f32: ctx.enter_context(nc.sbuf_tensor(f"{tag}_{n}", s, d))
        sem = lambda n: ctx.enter_context(nc.semaphore(f"{tag}_{n}"))
        w1 = [sb(f"w1{j}", [P, CH, F]) for j in range(2)]
        w2 = [sb(f"w2{j}", [P, NF, D]) for j in range(2)]
        b1 = sb("b1", [P, T, NF])
        b2 = [sb(f"b2{j}", [P, D]) for j in range(2)]
        h = [sb(f"h{j}", [P, NF, P]) for j in range(2)]
        xo = [sb(f"xo{j}", [P, D]) for j in range(2)]
        HP = [ctx.enter_context(nc.psum_tensor(f"{tag}_hp{j}", [P, 4, P], f32)) for j in range(4)]
        YP = [ctx.enter_context(nc.psum_tensor(f"{tag}_yp{j}", [P, 512], f32)) for j in range(2)]
        b_in, w_in = sem("b_in"), [sem(f"w_in{j}") for j in range(2)]
        h_full, h_ev, y_full, y_ev = sem("h_full"), sem("h_ev"), sem("y_full"), sem("y_ev")
        r_done, out_done = sem("r_done"), [sem(f"out_done{j}") for j in range(2)]
        block = ctx.enter_context(nc.Block())

        @block.sync
        def _(sp):
            sp.dma_start(b1[:], w["b1"]).then_inc(b_in, 16)

            def load(i, j):
                t = i * 2 + j
                if not isinstance(i, int):
                    sp.wait_ge(y_full, t - 1)
                    sp.wait_ge(r_done, t - 1)
                sp.dma_start(w1[j][:], w["w1"][t]).then_inc(w_in[j], 16)
                sp.dma_start(w2[j][:], w["w2"][t]).then_inc(w_in[j], 16)
                sp.dma_start(b2[j][:], w["b2"][bass.ds(t, 1), :].to_broadcast([P, D])).then_inc(w_in[j], 16)

            for j in range(2):
                load(0, j)
            with sp.Fori(1, T // 2) as i:
                for j in range(2):
                    load(i, j)

        @block.tensor
        def _(pe):
            mm = nc.tensor.matmul

            def two(i):
                for j in range(2):
                    t = i * 2 + j
                    pe.wait_ge(w_in[j], i * 48 + 48)
                    for g in range(2):
                        for f in range(4):
                            for k in range(CH):
                                last = mm(HP[2 * j + g][:, f, :], w1[j][:, k, (4 * g + f) * P:(4 * g + f + 1) * P], lnT[:, k, bass.ds(t * P, P)],
                                          start=k == 0, stop=k == CH - 1)
                        last.then_inc(h_full, 1)
                    ge(pe, y_ev, t - 1)
                    for g in range(2):
                        pe.wait_ge(h_ev, t * 2 + (g + 1))
                        for f in range(4):
                            last = mm(YP[j][:, 0:D], h[j][:, 4 * g + f, :], w2[j][:, 4 * g + f, :], start=g + f == 0, stop=g + f == 4)
                    last.then_inc(y_full, 1)

            two(0)
            with pe.Fori(1, T // 2) as i:
                two(i)

        @block.vector
        def _(dve):
            dve.wait_ge(b_in, 16)
            def two(i):
                for j in range(2):
                    t = i * 2 + j
                    for g in range(2):
                        dve.wait_ge(h_full, t * 2 + (g + 1))
                        nc.vector.tensor_tensor(h[j][:, 4 * g:4 * g + 4, :], HP[2 * j + g][:],
                                                b1[:, bass.ds(t, 1), 4 * g:4 * g + 4].rearrange("p a f -> p (a f)").unsqueeze(2).to_broadcast([P, 4, P]),
                                                ALU.add).then_inc(h_ev, 1)
                    dve.wait_ge(y_full, t + 1)
                    ge(dve, out_done[j], i * 16)
                    nc.vector.tensor_tensor(xo[j][:], X[:, bass.ds(t, 1), :].rearrange("p a n -> p (a n)"), YP[j][:, 0:D], ALU.add).then_inc(y_ev, 1)
                    dve.wait_ge(y_ev, t + 1)
                    nc.vector.tensor_tensor(xo[j][:], xo[j][:], b2[j][:], ALU.add).then_inc(r_done, 1)

            two(0)
            with dve.Fori(1, T // 2) as i:
                two(i)

        @block.scalar
        def _(act):
            with act.Fori(0, T // 2) as i:
                for j in range(2):
                    t = i * 2 + j
                    act.wait_ge(r_done, t + 1)
                    act.dma_start(out[t], xo[j][:]).then_inc(out_done[j], 16)
            for j in range(2):
                act.wait_ge(out_done[j], 16 * (T // 2))


CONST = {"ident": P, "spread": P, "hmask": 2, "mrow": 1, "cos": S, "sin": S, "lower": NE * NE, "half": 2, "eighth": 8}
H1, DQK1, DV1 = 8, 64, 32


def program(nc, a, out):
    ctx = ExitStack()
    with ctx:
        sb = lambda n, s, d=f32: ctx.enter_context(nc.sbuf_tensor(n, s, d))
        X = sb("X", [P, T, D])
        lnT = sb("lnT", [P, CH, T * P])
        consts = sb("consts", [P, sum(CONST.values())])
        csum = sb("csum", [P, CH, 2, B])
        first_in = ctx.enter_context(nc.semaphore("first_in"))
        ln = {n: ctx.enter_context(nc.semaphore(f"ln_{n}")) for n in LN_SEMS}
        c, at = {}, 0
        for name, width in CONST.items():
            c[name] = consts[:, at:at + width]
            at += width

        with nc.Block() as block:
            @block.sync
            def _(sp):
                sp.dma_start(X[:], a["x"].rearrange("(t p) n -> p t n", p=P)).then_inc(first_in, 16)
                sp.dma_start(consts[:], a["consts"]).then_inc(first_in, 16)
                sp.wait_ge(first_in, 32)

        layer_norm(nc, 0, ln, X, lnT, c)
        xattn(nc, X, lnT, c, {k: a["xa_" + k] for k in ("wq", "bq", "wk", "bk", "wv", "bv", "wo", "bo")}, a["ctxT"], csum)

        layer_norm(nc, 1, ln, X, lnT, c, bias=a["sa_bo"], row=16)
        w = {k: a["sa_" + k] for k in ("q", "qr", "k", "kr", "v", "o")} | {"mask": c["eighth"]}
        self_attention(nc, "sa", X, lnT, c, w, H0, D0, D0, rope=True)

        with ExitStack() as parts:
            lnH = parts.enter_context(nc.sbuf_tensor("lnH", [P, CH, T * P], f32r))
            lnL = parts.enter_context(nc.sbuf_tensor("lnL", [P, CH, T * P], f32r))
            layer_norm(nc, 2, ln, X, lnT, c, lnH=lnH, lnL=lnL)
            experts(nc, "moe", X, lnT, lnH, lnL, c, {k: a["moe_" + k] for k in ("gate", "gu", "down")})

        layer_norm(nc, 3, ln, X, lnT, c, bias=a["mc_b"], row=32)
        mean_context(nc, "mc", X, lnT, c, {k: a["mc_" + k] for k in ("w1", "w2")}, csum)

        layer_norm(nc, 4, ln, X, lnT, c, bias=a["sb_bo"], row=48)
        w = {k: a["sb_" + k] for k in ("q", "k", "v", "o")} | {"mask": c["half"]}
        scratch = nc.dram_tensor("bias_scratch", (H1, S * (2 * S - 1)), f32, kind="Internal").ap()
        self_attention(nc, "sb", X, lnT, c, w, H1, DQK1, DV1, conv_bias=(a["sb_conv"], scratch))

        layer_norm(nc, 5, ln, X, lnT, c)
        grouped_ffn(nc, "gf", X, lnT, c, {k: a["gf_" + k] for k in ("w1", "b1", "w2", "b2")}, out)


def shape_constants():
    import numpy as np

    p = np.arange(P)
    d = p % D0
    spread = np.zeros((P, P), np.float32)
    spread[32 * (p // 32) + D0, p] = 1.0
    freqs = (np.float32(10000.0) ** (-np.arange(0, D0, 2, dtype=np.float32) / np.float32(D0))).astype(np.float32)
    angles = (np.arange(S, dtype=np.float32)[:, None] * freqs).astype(np.float32)
    sign = np.where(d < D0 // 2, -1.0, 1.0).astype(np.float32)[:, None]
    e, j = np.divmod(np.arange(NE * NE), NE)
    parts = {
        "ident": np.eye(P),
        "spread": spread,
        "hmask": np.stack([d.astype(int) * 0 + ((p % 32) // D0 == h) for h in range(2)], 1),
        "mrow": np.where(p == 97, -1.0, 0.0)[:, None],
        "cos": np.cos(angles)[:, d // 2].T,
        "sin": np.sin(angles)[:, d // 2].T * sign,
        "lower": np.tile((j < e)[None], (P, 1)),
        "eighth": np.stack([p // D0 == h for h in range(8)], 1),
        "half": np.stack([p // (P // 2) == h for h in range(2)], 1),
    }
    return np.ascontiguousarray(np.concatenate([parts[k] for k in CONST], 1).astype(np.float32))


def kernel(**inputs):
    import numpy as np
    import concourse.bacc as bacc
    from concourse.bass_utils import run_bass_kernel_spmd

    i = {k: np.asarray(v) for k, v in inputs.items()}

    def rows(w):
        return w.reshape(-1, P, w.shape[-1]).transpose(1, 0, 2)

    def quads(w):
        n = w.size // D
        o = np.zeros((4, 32, 4, n), w.dtype)
        o[:, :D0] = w.reshape(4, 4, D0, n).transpose(1, 2, 0, 3)
        return o.reshape(P, 4, n)

    wq, wkv, bkv = i["L0_xattn_Wq"], i["L0_xattn_Wkv"], i["L0_xattn_bkv"]
    pairs = rows(wq).reshape(P, CH, 8, 1, 32)
    w_q, w_k, w_v = np.split(i["L0_attn_w_qkv"], 3, axis=1)
    turn = (np.arange(H0)[:, None] * D0 + np.concatenate([np.arange(1, D0, 2), np.arange(0, D0, 2)])).ravel()
    qk = i["L1_attn_W_qk"]
    halves = lambda w: w.reshape(D, 2, FE).transpose(1, 0, 2)
    gate_w = np.concatenate([i["L0_ffn_w_gate"], halves(i["L0_ffn_sw_gate"])])
    up_w = np.concatenate([i["L0_ffn_w_up"], halves(i["L0_ffn_sw_up"])])
    down_w = np.concatenate([i["L0_ffn_w_down"], i["L0_ffn_sw_down"].reshape(2, FE, D)])
    down = np.zeros((NX, 3 * P, D), down_w.dtype)
    down[:, :FE] = down_w
    W = i["L1_xattn_W"]
    arrays = {
        "x": i["x"].reshape(T * P, D),
        "consts": shape_constants(),
        "ctxT": i["ctx_1024"].transpose(0, 2, 1).reshape(B, CH, P, NK).transpose(0, 2, 1, 3),
        "xa_wq": np.broadcast_to(pairs, (P, CH, 8, 3, 32)).reshape(P, CH, 8, 96),
        "xa_bq": np.tile(i["L0_xattn_bq"].reshape(8, 32).T, (3, 1)),
        "xa_wk": rows(wkv[:, 0::2]),
        "xa_bk": bkv[0::2].reshape(CH, P).T,
        "xa_wv": rows(wkv[:, 1::2]),
        "xa_bv": quads(bkv[1::2])[:, :, 0],
        "xa_wo": quads(i["L0_xattn_Wout"]),
        "xa_bo": i["L0_xattn_bout"],
        "sa_q": rows(w_q), "sa_qr": rows(w_q[:, turn]), "sa_k": rows(w_k), "sa_kr": rows(w_k[:, turn]),
        "sa_v": rows(w_v), "sa_o": quads(i["L0_attn_w_out"]), "sa_bo": i["L0_attn_b_out"],
        "moe_gate": rows(i["L0_ffn_gate_w"].T),
        "moe_gu": np.stack([gate_w, up_w], 2).reshape(NX, CH, P, 2, FE).transpose(0, 2, 1, 3, 4),
        "moe_down": down.reshape(NX, 3, P, D).transpose(0, 2, 1, 3),
        "mc_w1": rows(W[:, :D].T), "mc_w2": rows(W[:, D:].T), "mc_b": i["L1_xattn_b"],
        "sb_q": rows(qk[:, :H1 * DQK1]), "sb_k": rows(qk[:, H1 * DQK1:]), "sb_v": rows(i["L1_attn_W_v"]),
        "sb_o": rows(i["L1_attn_W_out"]), "sb_bo": i["L1_attn_b_out"], "sb_conv": i["L1_attn_conv"],
        "gf_w1": i["L1_ffn_W1"].transpose(0, 2, 1).reshape(T, CH, P, 1024).transpose(0, 2, 1, 3),
        "gf_b1": i["L1_ffn_b1"].reshape(T, 8, P).transpose(2, 0, 1),
        "gf_w2": i["L1_ffn_W2"].transpose(0, 2, 1).reshape(T, 8, P, D).transpose(0, 2, 1, 3),
        "gf_b2": i["L1_ffn_b2"],
    }
    arrays = {k: np.ascontiguousarray(v) for k, v in arrays.items()}
    nc = bacc.Bacc("TRN2", target_bir_lowering=False, num_devices=1)
    a = {k: nc.dram_tensor("in_" + k, v.shape, mybir.dt.from_np(v.dtype), kind="ExternalInput").ap() for k, v in arrays.items()}
    out = nc.dram_tensor("out_x", (T, P, D), f32, kind="ExternalOutput").ap()
    program(nc, a, out)
    done = run_bass_kernel_spmd(nc, [{"in_" + k: v for k, v in arrays.items()}], core_ids=[0])
    return done.results[0]["out_x"].reshape(B, S, D)
```

```python
import concourse.bass as bass
from concourse import mybir
from contextlib import ExitStack

f32 = mybir.dt.float32
f32r = mybir.dt.float32r
ALU = mybir.AluOpType
ACT = mybir.ActivationFunctionType
AX = mybir.AxisListType

P = 128
D = 256
CH = D // P
B, S = 16, 64
T = B * S // P
NK = 1601
NKP = NK + 1
KT = -(-NK // P)
KLAST = NK - P * (KT - 1)
H0, D0 = 16, 16
VW = D0 + 1
VROW = H0 * VW + D0


def ge(eng, sem, value):
    if isinstance(value, int) and value <= 0:
        return
    eng.wait_ge(sem, value)


RING = ("K", "V", "Q", "E", "W")


def xattn_phase(b, h, fill, chain, late):
    out, fill, late = [], list(fill), dict(late)
    for u in range(8):
        out.append(("mx", b, h, u))
        if fill and (u in (1, 3, 4, 6) or u >= 1 and len(fill) > 4):
            out.append(fill.pop(0))
    out += fill + chain[:2] + [("mt", b, h, 0)] + chain[2:3]
    for g in range(7):
        out.append(("st", b, h, g))
        if g == 0:
            out += chain[3:]
        if g >= 1:
            out.append(("pv", b, h, g - 1))
        out += late.get(g, [])
    return out + [("pv", b, h, 6)]


def xattn_order(first, more):
    if_more = lambda x: x if more else []
    K = lambda b, h: [("K", b, h, u) for u in range(4)]
    V = lambda b, lo, hi: [("V", b, 0, u) for u in range(lo, hi)]
    split = lambda b: {1: [("cv", b, 0, 0)], 4: [("cv", b, 0, 1)]}
    o = []
    for b in range(2):
        queries = {2: [("Q", 2, 0, 0)], 5: [("Q", 2, 0, 1)]} if b == 1 and more else {}
        late = (split(b + 1) if b == 0 or more else {}) | queries
        k = K(b, 1)
        e = [("E", b - 1, 0, 0)] if b == 1 or not first else []
        w = [("W", -2, 0, 0), ("W", -2, 0, 1)] if b == 0 and not first else []
        o += xattn_phase(b, 0, [k[0]] + e + k[1:3] + w, [k[3]] + V(b, 4, 7), late)
        ahead = b == 0 or more
        o += xattn_phase(b, 1, K(b + 1, 0) if ahead else [], V(b + 1, 0, 4) if ahead else [], {})
    return o


XATTN_FIRST = ([("cv", 0, 0, k) for k in range(2)] + [("Q", 0, 0, 0), ("Q", 0, 0, 1)]
               + [("K", 0, 0, k) for k in range(4)] + [("V", 0, 0, v) for v in range(4)])
XATTN_LAST = [("E", 1, 0, 0), ("W", 0, 0, 0), ("W", 0, 0, 1)]
KCOLS = [(0, 512), (512, 1024), (1024, 1536), (1536, NKP)]
CVCOLS = [(0, 1024), (1024, NKP)]
MXCOLS, MXN = [0, 400, 800, NK - 402], 402
DMAS_KST = 12


def xattn_buffers(nc, ctx):
    sb = lambda n, s, d=f32: ctx.enter_context(nc.sbuf_tensor("xa_" + n, s, d))
    E = {
        "raw": sb("raw", [P, CH, NKP]),
        "KS": sb("keys", [98, 8, NKP], f32r),
        "V": [sb(f"values{j}", [P, KT, VROW]) for j in range(2)],
        "wv": sb("wv", [P, CH, D]), "wk": sb("wk", [P, CH, D]),
        "wq": sb("wq96", [P, CH, 8, 96]), "bq": sb("bq96", [96, 8]), "bk": sb("bk", [P, CH]),
        "bv": sb("bv", [P, 4]), "wo": sb("wo", [P, 4, D]), "bo": sb("bo", [P, D]),
    }
    for n in ("wv_in", "wk_in", "raw_in", "w_in", "init", "ones"):
        E[n] = ctx.enter_context(nc.semaphore("xa_" + n))
    return E


def xattn_loads(sp, E, w, ctxT):
    sp.dma_start(E["wk"][:], w["wk"]).then_inc(E["wk_in"], 16)
    sp.dma_start(E["raw"][:, :, 0:NK], ctxT[0]).then_inc(E["raw_in"], 16)
    sp.dma_start(E["wv"][:], w["wv"]).then_inc(E["wv_in"], 16)
    for n in ("wq", "bq", "bk", "bv", "wo"):
        sp.dma_start(E[n][:], w[n]).then_inc(E["w_in"], 16)
    sp.dma_start(E["bo"][:], w["bo"].rearrange("(a n) -> a n", a=1).to_broadcast([P, D])).then_inc(E["w_in"], 16)


def xattn_ones(nc, eng, E, half):
    eng.memset(E["KS"][96:98, 4 * half:4 * half + 4].bitcast(f32), 1.0).then_inc(E["ones"], 1)


def xattn_fill(nc, pool, E):
    nc.gpsimd.memset(E["raw"][:, :, NK:NKP], 0.0).then_inc(E["init"], 1)
    for j in range(2):
        nc.gpsimd.memset(E["V"][j][:], 1.0).then_inc(E["init"], 1)


def xattn(nc, X, lnT, c, E, ctxT, csum):
    ctx = ExitStack()
    with ctx:
        sb = lambda n, s, d=f32: ctx.enter_context(nc.sbuf_tensor(n, s, d))
        sem = lambda n: ctx.enter_context(nc.semaphore(n))
        raw, KS, V, wo, bo = E["raw"], E["KS"], E["V"], E["wo"], E["bo"]
        wq96, bq96, bk, bvq = E["wq"], E["bq"], E["bk"], E["bv"]
        wk_in, wv_in, w_in, raw_in, init = [E[n] for n in ("wk_in", "wv_in", "w_in", "raw_in", "init")]
        ctx_hi, ctx_lo = sb("xa_ctx_hi", [P, CH, NKP], f32r), sb("xa_ctx_lo", [P, CH, NKP], f32r)
        kstage_hi, kstage_lo = sb("xa_kst_hi", [P, NKP], f32r), sb("xa_kst_lo", [P, NKP], f32r)
        QS = [sb(f"xa_queries{j}", [98, 8, P], f32r) for j in range(2)]
        Q96 = sb("xa_q96", [96, 8, P], f32r)
        qtmp = sb("xa_qtmp", [96, 4, P])
        PTN = 4
        PT = [sb(f"xa_pt{j}", [P, 2, 512]) for j in range(PTN)]
        o_sb = sb("xa_o", [P, 4, S])
        rec = sb("xa_rec", [P, 4, S])
        oN = sb("xa_on", [P, 4, P])
        mx = sb("xa_mx", [P, 4, 4])
        nm = sb("xa_nm", [P, 4, 2])
        mhi = sb("xa_mhi", [P, 512], f32r)
        kraw = [E[n][:].rearrange("p c n -> p (c n)") for n in ("wk", "wv")]
        wk = [sb(f"xa_wk{j}", [P, CH, D], f32r) for j in range(2)]
        wv = [sb(f"xa_wv{j}", [P, CH, D], f32r) for j in range(2)]
        SC = [ctx.enter_context(nc.psum_tensor(f"xa_sc{j}", [P, 2, 512], f32)) for j in range(2)]
        OP = [ctx.enter_context(nc.psum_tensor(f"xa_op{j}", [P, 512], f32)) for j in range(2)]
        PJ = [ctx.enter_context(nc.psum_tensor(f"xa_pj{j}", [P, 512], f32)) for j in range(2)]

        w_split, bo_added = sem("xa_w_split"), sem("xa_bo_added")
        hi_done, lo_done, csum_done = sem("xa_hi_done"), sem("xa_lo_done"), sem("xa_csum_done")
        full = {k: sem(f"xa_{k}_full") for k in RING}
        free = {k: sem(f"xa_{k}_free") for k in RING if k != "E"}
        khi, klo = sem("xa_khi"), sem("xa_klo")
        kst_in = [sem(f"xa_kst_in{h}") for h in range(2)]
        q_in = sem("xa_q_in")
        sc_full = {k: sem(f"xa_{k}_full") for k in ("mx", "st")}
        mx_done, nm_done, mt_full, mrow = sem("xa_mx_done"), sem("xa_nm_done"), sem("xa_mt_full"), sem("xa_mrow")
        ex_done, pv_done, o_ev = sem("xa_ex_done"), sem("xa_pv_done"), sem("xa_o_ev")
        rec_done, on_done = sem("xa_rec_done"), sem("xa_on_done")
        dch, pch, qch = sem("xa_dch"), sem("xa_pch"), sem("xa_qch")

        PER = {"K": 8, "V": 7, "Q": 2, "E": 1, "W": 2, "mx": 16, "st": 14, "pv": 14, "mt": 2, "cv": 2}
        INNER = {"K": 4, "mx": 8, "st": 7, "pv": 7, "mt": 1}

        def nth(step, i):
            k, b, h, n = step
            if k in ("Q", "W"):
                return PER[k] * (i + b // 2) + (n + 1)
            return (i * (2 * PER[k])) + (PER[k] * b + INNER.get(k, 0) * h + n + 1)

        def z(i):
            return 0 if i is None else i

        def ptslot(step):
            return (nth(step, 0) - 1) % PTN

        START, MIDDLE, END = xattn_order(True, True), xattn_order(False, True), xattn_order(False, False)

        def past(order, n, i, kinds):
            before = []
            if order is not XATTN_FIRST:
                before = [(x, 0) for x in XATTN_FIRST]
            if order is MIDDLE or order is END or order is XATTN_LAST:
                before += [(x, i - 1) for x in START]
            if order is XATTN_LAST:
                before += [(x, i) for x in END]
            return [x for x in before + [(x, z(i)) for x in order[:n]] if x[0][0] in kinds]

        def ring_before(order, kinds, n, i):
            before = past(order, n, i, kinds)
            return before[-2] if len(before) >= 2 else None

        def bank(order, kinds, n, i):
            return len(past(order, n, 1, kinds)) % 2

        def walk(steps):
            steps[0](XATTN_FIRST, None)
            steps[0](START, 0)
            with steps[1].Fori(1, T - 1) as i:
                steps[0](MIDDLE, i)
            steps[0](END, T - 1)
            steps[0](XATTN_LAST, T - 1)

        block = ctx.enter_context(nc.Block())

        @block.sync
        def _(sp):
            def steps(order, i):
                for n, step in enumerate(order):
                    k, b, h, u = step
                    if (k, u) == ("V", 3) and i is None or (k, h, u) == ("st", 1, 1) and order is not END:
                        b_ = 0 if i is None else b + 1
                        ge(sp, csum_done, nth(("cv", b_, 0, 1), z(i)) * 2)
                        ge(sp, lo_done, nth(("cv", b_, 0, 1), z(i)))
                        sp.dma_start(raw[:, :, 0:NK], ctxT[2 * z(i) + (b_ + 1)]).then_inc(raw_in, 16)
                    if k == "K" and u == 3:
                        ge(sp, klo, nth(step, z(i)))
                        for r, src in ((0, kstage_hi), (1, kstage_lo), (2, kstage_hi)):
                            for q in range(4):
                                sp.dma_start(KS[32 * r:32 * r + 32, 4 * h + q, :].bitcast(f32),
                                             src[32 * q:32 * q + 32].bitcast(f32)).then_inc(kst_in[h], 16)

            walk((steps, sp))

        @block.gpsimd
        def _(pool):
            def steps(order, i):
                for n, step in enumerate(order):
                    k, b, h, u = step
                    if k == "cv":
                        ge(pool, hi_done, nth(step, z(i)) * 2)
                        lo, hi = CVCOLS[u]
                        nc.gpsimd.tensor_tensor(ctx_lo[:, :, lo:hi], raw[:, :, lo:hi],
                                                ctx_hi[:, :, lo:hi].bitcast(f32), ALU.subtract).then_inc(lo_done, 1)
                    if k == "K":
                        lo, hi = KCOLS[u]
                        ge(pool, khi, nth(step, z(i)))
                        nc.gpsimd.tensor_tensor(kstage_lo[:, lo:hi], kraw[u % 2][:, 0:hi - lo],
                                                kstage_hi[:, lo:hi].bitcast(f32), ALU.subtract).then_inc(klo, 1)
                    if (k, h, u) == ("mx", 0, 7) or (k, u) == ("Q", 1):
                        if k == "Q":
                            pair, tile_, want = 0, None, nth(step, z(i))
                            bat = 0 if i is None else 2 * (i + 1)
                        elif b == 0:
                            pair, want = 1, nth(("Q", 0, 0, 1), i)
                            bat = 2 * i + 1
                        else:
                            continue
                        ge(pool, free["Q"], want)
                        if not (i is None or (isinstance(i, int) and i == 0 and pair == 1)):
                            rel = 0 if pair == 0 else -1
                            ge(pool, sc_full["st"], nth(("st", rel, 1, 6), i))
                        for e in range(2):
                            nc.gpsimd.tensor_tensor(QS[pair][0:96, :, e * S:(e + 1) * S],
                                                    Q96[:, :, pair * S:(pair + 1) * S].bitcast(f32),
                                                    c["hmask"][0:96, e:e + 1].unsqueeze(1).to_broadcast([96, 8, S]),
                                                    ALU.mult).then_inc(q_in, 1)
                    if k == "E":
                        ge(pool, rec_done, nth(step, i))
                        if b == 0:
                            ge(pool, full["W"], nth(("W", -2, 0, 1), i))
                        nc.gpsimd.tensor_tensor(o_sb[:], o_sb[:], rec[:], ALU.mult).then_inc(pch, 1)
                        pool.wait_ge(pch, nth(step, i))
                        nc.gpsimd.tensor_tensor(oN[:, :, (b % 2) * S:(b % 2 + 1) * S], o_sb[:],
                                                bvq[:].unsqueeze(2).to_broadcast([P, 4, S]), ALU.add).then_inc(on_done, 1)

            def first_steps(order, i):
                steps(order, i)
                if order is XATTN_FIRST:
                    pool.wait_ge(w_in, 16 * 6)
                    for t in range(T):
                        nc.gpsimd.tensor_tensor(X[:, t], X[:, t], bo[:], ALU.add).then_inc(bo_added, 1)

            walk((first_steps, pool))

        @block.scalar
        def _(act):
            act.wait_ge(w_in, 16 * 6)

            def steps(order, i):
                for n, step in enumerate(order):
                    k, b, h, u = step
                    if k == "K":
                        lo, hi = KCOLS[u]
                        ge(act, full["K"], nth(step, z(i)))
                        if i is not None and u in (0, 2):
                            ph = (b - 1, 1) if h == 0 else (b, 0)
                            done = nth(("E", ph[0], 0, 0), i) * (16 * DMAS_KST)
                            ge(act, kst_in[ph[1]], done)
                        kr = kraw[u % 2]
                        ge(act, klo, nth(step, z(i)) - 2)
                        nc.scalar.activation(kr[:, 0:hi - lo], PJ[bank(order, RING, n, i)][:, 0:hi - lo],
                                             ACT.Identity, bias=bk[:, h:h + 1]).then_inc(free["K"], 1)
                        ge(act, free["K"], nth(step, z(i)))
                        nc.scalar.activation(kstage_hi[:, lo:hi], kr[:, 0:hi - lo], ACT.Copy).then_inc(khi, 1)
                    elif k == "V":
                        nt = 2 if u < 6 else 1
                        rows = P if u < 6 else KLAST
                        ge(act, full["V"], nth(step, z(i)))
                        if u == 0 and i is not None and not (isinstance(i, int) and i == 0 and b == 1):
                            ge(act, pv_done, nth(("pv", b - 2, 1, 6), i))
                        if i is None and u == 0:
                            act.wait_ge(init, 3)
                        vdst = V[b % 2][0:rows, 2 * u:2 * u + nt, 0:H0 * VW].rearrange("p k (h s) -> p k h s", s=VW)[:, :, :, 0:D0]
                        vsrc = PJ[bank(order, RING, n, i)][0:rows, 0:nt * D].rearrange("p (k h s) -> p k h s", k=nt, s=D0)
                        for kk in range(nt):
                            ins = nc.scalar.activation(vdst[:, kk], vsrc[:, kk], ACT.Copy)
                        ins.then_inc(free["V"], 1)
                    elif k == "st":
                        nt = 2 if u < 6 else 1
                        rows = P if u < 6 else KLAST
                        ge(act, sc_full["st"], nth(step, i))
                        j = nth(step, 0) - 1
                        ge(act, pv_done, nth(step, i) - PTN)
                        nc.scalar.activation(PT[ptslot(step)][0:rows, 0:nt], SC[bank(order, ("mx", "st"), n, i)][0:rows, 0:nt],
                                             ACT.Exp, scale=float(D0) ** -0.5).then_inc(ex_done, 1)

            walk((steps, act))

        @block.vector
        def _(dve):
            for n, (src, raw_w, dst) in enumerate(((wk_in, E["wk"], wk), (wv_in, E["wv"], wv))):
                dve.wait_ge(src, 16)
                nc.vector.tensor_copy(dst[0][:], raw_w[:]).then_inc(w_split, 1)
                dve.wait_ge(w_split, 2 * n + 1)
                nc.vector.tensor_tensor(dst[1][:], raw_w[:], dst[0][:].bitcast(f32), ALU.subtract).then_inc(w_split, 1)
            dve.wait_ge(w_in, 16 * 6)

            def steps(order, i):
                for n, step in enumerate(order):
                    k, b, h, u = step
                    if k == "cv":
                        lo, hi = CVCOLS[u]
                        ge(dve, raw_in, 16 * (nth(("E", b, 0, 0), z(i))))
                        if i is None:
                            dve.wait_ge(init, 1)
                        else:
                            ge(dve, full["K"], nth(("K", b - 1, 1, 2 * u + 1), i))
                            if u == 1:
                                ge(dve, full["V"], nth(("V", b - 1, 0, 6), i))
                        bat = 0 if i is None else 2 * i + b
                        for ch in range(CH):
                            nc.vector.tensor_copy(ctx_hi[:, ch, lo:hi], raw[:, ch, lo:hi]).then_inc(hi_done, 1)
                        for ch in range(CH):
                            nc.vector.tensor_reduce(csum[:, ch, u, bass.ds(bat, 1)], raw[:, ch, lo:hi], AX.X, ALU.add).then_inc(csum_done, 1)
                    elif k == "mx":
                        ge(dve, sc_full["mx"], nth(step, i))
                        if u == 0:
                            ge(dve, nm_done, nth(("mt", b, h, 0), i) * 2 - 2)
                        nc.vector.tensor_reduce(mx[:, u // 2, 2 * (u % 2):2 * (u % 2) + 2],
                                                SC[bank(order, ("mx", "st"), n, i)][:, :, 0:MXN], AX.X, ALU.max).then_inc(mx_done, 1)
                        if u == 7:
                            dve.wait_ge(mx_done, nth(step, i))
                            ge(dve, mt_full, nth(("mt", b, h, 0), i) - 1)
                            for e in range(2):
                                nc.vector.tensor_reduce(nm[:, :, e:e + 1], mx[:], AX.X, ALU.max, negate=True).then_inc(nm_done, 1)
                    elif k == "mt":
                        ge(dve, mt_full, nth(step, i))
                        ge(dve, mrow, nth(step, i) - 1)
                        nc.vector.tensor_copy(mhi[96:98], OP[h][96:98]).then_inc(dch, 1)
                        dve.wait_ge(dch, nth(step, i))
                        nc.vector.scalar_tensor_tensor(QS[b % 2][96:98, 4 * h:4 * h + 4, :], mhi[96:98].bitcast(f32).rearrange("p (a n) -> p a n", a=4),
                                                       c["mrow"][96:98, 0:1], OP[h][96:98].rearrange("p (a n) -> p a n", a=4),
                                                       ALU.mult, ALU.add).then_inc(mrow, 1)
                    elif k == "Q":
                        ge(dve, full["Q"], nth(step, z(i)))
                        qs = slice(4 * u, 4 * u + 4)
                        q0 = nth(step, z(i))
                        ge(dve, free["Q"], q0 - 1)
                        nc.vector.tensor_tensor(qtmp[:], PJ[bank(order, RING, n, i)][0:96].rearrange("p (a n) -> p a n", a=4),
                                                bq96[:, qs].unsqueeze(2).to_broadcast([96, 4, P]), ALU.add).then_inc(qch, 1)
                        dve.wait_ge(qch, q0 * 2 - 1)
                        if i is not None:
                            ge(dve, q_in, (i + 1) * 4)
                        nc.vector.tensor_copy(Q96[:, qs], qtmp[:]).then_inc(qch, 1)
                        dve.wait_ge(qch, q0 * 2)
                        nc.vector.tensor_tensor(Q96[64:96, qs], qtmp[64:96], Q96[64:96, qs].bitcast(f32), ALU.subtract).then_inc(free["Q"], 1)
                    elif k == "E":
                        ge(dve, full["E"], nth(step, i))
                        ge(dve, on_done, nth(step, i) - 1)
                        nc.vector.reciprocal(rec[:], PJ[bank(order, RING, n, i)][:, 0:4 * S].rearrange("p (a n) -> p a n", a=4)).then_inc(rec_done, 1)
                    elif k == "W":
                        ge(dve, full["W"], nth(step, i))
                        dve.wait_ge(bo_added, T)
                        xs = X[:, bass.ds(i + b // 2, 1), u * P:(u + 1) * P].rearrange("p a n -> p (a n)")
                        nc.vector.tensor_tensor(xs, xs, PJ[bank(order, RING, n, i)][:, 0:P], ALU.add).then_inc(free["W"], 1)
                    elif k == "pv" and u == 6:
                        ge(dve, pv_done, nth(step, i))
                        ge(dve, on_done, nth(("E", b, 0, 0), i) - 1)
                        nc.vector.tensor_copy(o_sb[:, 2 * h:2 * h + 2], OP[h][:, 0:2 * S].rearrange("p (a n) -> p a n", a=2)).then_inc(o_ev, 1)

            walk((steps, dve))

        @block.tensor
        def _(pe):
            mm = nc.tensor.matmul
            pe.wait_ge(w_split, 4)
            pe.wait_ge(w_in, 16 * 6)

            def split_product(out, lh, rh):
                terms = [(a, b_) for a, b_ in zip(lh, rh)]
                todo = []
                for l, r in terms:
                    todo += [(l[0], r[0]), (l[0], r[1]), (l[1], r[0])]
                for n_, (l, r) in enumerate(todo):
                    last = mm(out, l, r, start=n_ == 0, stop=n_ == len(todo) - 1)
                return last

            def steps(order, i):
                for n, step in enumerate(order):
                    k, b, h, u = step
                    if k in RING:
                        before = ring_before(order, RING, n, i)
                        if before:
                            (bk_, j) = before
                            ge(pe, free_of(bk_[0]), nth(bk_, j))
                        dst = PJ[bank(order, RING, n, i)]
                    if k == "K":
                        lo, hi = KCOLS[u]
                        if u in (0, 2) and h == 0:
                            ge(pe, hi_done, nth(("cv", b, 0, u // 2), z(i)) * 2)
                            ge(pe, lo_done, nth(("cv", b, 0, u // 2), z(i)))
                        hs = slice(h * P, (h + 1) * P)
                        split_product(dst[:, 0:hi - lo], [(wk[0][:, ch, hs], wk[1][:, ch, hs]) for ch in range(CH)],
                                      [(ctx_hi[:, ch, lo:hi], ctx_lo[:, ch, lo:hi]) for ch in range(CH)]).then_inc(full["K"], 1)
                    elif k == "V":
                        for kk in range(2 if u < 6 else 1):
                            kt = 2 * u + kk
                            rows = P if kt < KT - 1 else KLAST
                            cs = slice(kt * P, kt * P + rows)
                            last = split_product(dst[0:rows, kk * D:(kk + 1) * D], [(ctx_hi[:, ch, cs], ctx_lo[:, ch, cs]) for ch in range(CH)],
                                                 [(wv[0][:, ch, :], wv[1][:, ch, :]) for ch in range(CH)])
                        last.then_inc(full["V"], 1)
                    elif k == "Q":
                        for a in range(4):
                            for ch in range(CH):
                                tok = bass.ds(0, P) if i is None else bass.ds((i + 1) * P, P)
                                last = mm(dst[0:96, a * P:(a + 1) * P], wq96[:, ch, 4 * u + a], lnT[:, ch, tok], start=ch == 0, stop=ch == CH - 1)
                        last.then_inc(full["Q"], 1)
                    elif k == "E":
                        ge(pe, o_ev, nth(step, i) * 2)
                        mm(dst[:, 0:4 * S], c["spread"][:], o_sb[:].rearrange("p a n -> p (a n)"), start=True, stop=True).then_inc(full["E"], 1)
                    elif k == "W":
                        if u == 0:
                            ge(pe, on_done, nth(("E", b + 1, 0, 0), i))
                        for q in range(4):
                            last = mm(dst[:, 0:P], oN[:, q], wo[:, q, u * P:(u + 1) * P], start=q == 0, stop=q == 3)
                        last.then_inc(full["W"], 1)
                    elif k == "mx":
                        wait_slot(order, n, i)
                        if u == 0:
                            ge(pe, kst_in[h], nth(("E", b, 0, 0), i) * (16 * DMAS_KST))
                            if h == 0:
                                ge(pe, q_in, nth(("E", b, 0, 0), i) * 2)
                        pr = 4 * h + u // 2
                        for kk in range(2):
                            lo = MXCOLS[2 * (u % 2) + kk]
                            last = mm(SC[bank(order, ("mx", "st"), n, i)][:, kk, 0:MXN], QS[b % 2][0:96, pr, :], KS[0:96, pr, lo:lo + MXN], start=True, stop=True)
                        last.then_inc(sc_full["mx"], 1)
                    elif k == "mt":
                        ge(pe, nm_done, nth(step, i) * 2)
                        ge(pe, o_ev, nth(step, i) - 2)
                        for a in range(4):
                            last = mm(OP[h][96:98, a * P:(a + 1) * P], nm[:, a, :], c["ident"][:], start=True, stop=True, tile_position=(0, 96))
                        last.then_inc(mt_full, 1)
                    elif k == "st":
                        wait_slot(order, n, i)
                        pe.wait_ge(E["ones"], 2)
                        if u == 0:
                            ge(pe, mrow, nth(("mt", b, h, 0), i))
                        for kk in range(2 if u < 6 else 1):
                            kt = 2 * u + kk
                            rows = P if kt < KT - 1 else KLAST
                            for a in range(4):
                                last = mm(SC[bank(order, ("mx", "st"), n, i)][0:rows, kk, a * P:(a + 1) * P],
                                          KS[:, 4 * h + a, kt * P:kt * P + rows], QS[b % 2][:, 4 * h + a, :], start=True, stop=True)
                        last.then_inc(sc_full["st"], 1)
                    elif k == "pv":
                        ge(pe, ex_done, nth(("st", b, h, u), i))
                        for kk in range(2 if u < 6 else 1):
                            kt = 2 * u + kk
                            rows = P if kt < KT - 1 else KLAST
                            for a in range(2):
                                for j in range(4):
                                    hd = 8 * h + 4 * a + j
                                    last = mm(OP[h][32 * j:32 * j + 32, a * S:(a + 1) * S],
                                              V[b % 2][0:rows, kt, hd * VW:hd * VW + 32],
                                              PT[ptslot(("st", b, h, u))][0:rows, kk, (4 * a + j) * S:(4 * a + j + 1) * S],
                                              start=kt == 0 and a == 0, stop=kt == KT - 1, tile_position=(0, 32 * j), skip_group_check=True)
                        last.then_inc(pv_done, 1)

            def free_of(kind):
                return free[kind] if kind != "E" else rec_done

            def wait_slot(order, n, i):
                before = ring_before(order, ("mx", "st"), n, i)
                if isinstance(i, int) and i == 0 and sum(x[0] in ("mx", "st") for x in order[:n]) < 2:
                    return
                (x, j) = before
                ge(pe, mx_done if x[0] == "mx" else ex_done, nth(x, j))

            walk((steps, pe))


def stage_weights(nc, ctx, tag, sources, **shapes):
    W = {n: ctx.enter_context(nc.sbuf_tensor(f"{tag}_w_{n}", s, f32)) for n, s in shapes.items()}
    w_in = ctx.enter_context(nc.semaphore(f"{tag}_w_in"))
    return W, w_in, [(W[n][:], sources[n], w_in) for n in shapes]


LN_SEMS = ("stat", "var", "std", "norm", "tr", "ev_dve", "ev_act")


def layer_norm(nc, k, sems, X, lnT, c, loads=(), also={}):
    ctx = ExitStack()
    with ctx:
        sb = lambda n, s, d=f32: ctx.enter_context(nc.sbuf_tensor(f"ln{k}_{n}", s, d))
        stat, var_done, std_done, norm, tr, ev_dve, ev_act = [sems[n] for n in LN_SEMS]
        s0, n0, t0 = k * (2 * T + 1), k * T, 4 * k
        stats, mv = sb("stats", [P, T, 6]), sb("mv", [P, T, 2])
        var, std, rstd = sb("var", [P, T]), sb("std", [P, T]), sb("rstd", [P, T])
        y = sb("y", [P, T, D])
        PS = [ctx.enter_context(nc.psum_tensor(f"ln{k}_ps{j}", [P, 512], f32)) for j in range(4)]
        block = ctx.enter_context(nc.Block())

        @block.sync
        def _(sp):
            for dst, src, counted in loads:
                sp.dma_start(dst, src).then_inc(counted, 16)

        @block.vector
        def _(dve):
            for t in range(T):
                nc.vector.bn_stats(stats[:, t], X[:, t]).then_inc(stat, 1)
            for t in range(T):
                dve.wait_ge(stat, s0 + t + 1)
                nc.vector.bn_aggr(mv[:, t], stats[:, t]).then_inc(stat, 1)
            dve.wait_ge(stat, s0 + 2 * T)
            nc.vector.tensor_scalar(var[:], mv[:, :, 1], 1e-5, None, ALU.add).then_inc(var_done, 1)
            dve.wait_ge(std_done, k + 1)
            nc.vector.reciprocal(rstd[:], std[:]).then_inc(stat, 1)
            dve.wait_ge(stat, s0 + 2 * T + 1)
            for t in range(T):
                nc.vector.tensor_scalar(y[:, t], X[:, t], mv[:, t, 0:1], rstd[:, t:t + 1], ALU.subtract, ALU.mult).then_inc(norm, 1)
            for g in (1, 3):
                dve.wait_ge(tr, t0 + g + 1)
                nc.vector.tensor_copy(lnT[:, g % 2, (g // 2) * 512:(g // 2) * 512 + 512], PS[g][:]).then_inc(ev_dve, 1)

        @block.scalar
        def _(act):
            if "act" in also:
                also["act"](act)
            act.wait_ge(var_done, k + 1)
            nc.scalar.activation(std[:], var[:], ACT.Sqrt).then_inc(std_done, 1)
            for g in (0, 2):
                act.wait_ge(tr, t0 + g + 1)
                nc.scalar.activation(lnT[:, g % 2, (g // 2) * 512:(g // 2) * 512 + 512], PS[g][:], ACT.Copy).then_inc(ev_act, 1)

        @block.tensor
        def _(pe):
            for g in range(4):
                for a in range(4):
                    t = 4 * (g // 2) + a
                    pe.wait_ge(norm, n0 + t + 1)
                    last = nc.tensor.transpose(PS[g][:, a * P:(a + 1) * P], y[:, t, (g % 2) * P:(g % 2 + 1) * P], c["ident"])
                last.then_inc(tr, 1)

        @block.gpsimd
        def _(pool):
            if "pool" in also:
                also["pool"](pool)


def bias_row(nc, ctx, tag, source):
    row, row_in = ctx.enter_context(nc.sbuf_tensor(f"{tag}_brow", [P, D], f32)), ctx.enter_context(nc.semaphore(f"{tag}_row_in"))
    return row, row_in, [(row[:], source.rearrange("(a n) -> a n", a=1).to_broadcast([P, D]), row_in)]


def add_bias(nc, pool, X, row, row_in, added):
    pool.wait_ge(row_in, 16)
    for t in range(T):
        nc.gpsimd.tensor_tensor(X[:, t], X[:, t], row[:], ALU.add).then_inc(added, 1)


def self_attention(nc, tag, X, lnT, c, W, w_in, bias, heads, dk, dv, mask, rope=False, conv_bias=None, loads=()):
    NCH = heads * dk // P
    HC = P // dk
    NP = heads // 2
    VW2 = 2 * (dv + 1)
    OT0 = 512 - P
    ctx = ExitStack()
    with ctx:
        sb = lambda n, s, d=f32: ctx.enter_context(nc.sbuf_tensor(f"{tag}_{n}", s, d))
        sem = lambda n: ctx.enter_context(nc.semaphore(f"{tag}_{n}"))
        names = ["q", "k"] + (["qr", "kr"] if rope else [])
        QT, KTt = sb("QT", [P, NCH, T * P]), sb("KT", [P, NCH, T * P])
        rot = sb("rot", [P, 512])
        Vall = sb("Vall", [P, T, NP * VW2])
        Vt = [sb(f"Vt{j}", [P, NP * VW2]) for j in range(2)]
        Qm = [sb(f"Qm{j}", [P, NCH, 2, HC, S]) for j in range(2)]
        Sc, Pr = sb("Sc", [P, NP, 2, S]), sb("Pr", [P, NP, 2, S])
        PT = sb("PT", [P, NP, P])
        mxt, rs = sb("mx", [P, NP, 2]), sb("rs", [P, 2, NP])
        oN, oT = sb("oN", [P, 2, NP, dv]), sb("oT", [P, 2, P])
        bank = lambda n, k=1: ctx.enter_context(nc.psum_tensor(f"{tag}_{n}", [P, k, 512], f32))
        SC = ctx.enter_context(nc.psum_tensor(f"{tag}_SC", [P, NP, 2, S], f32))
        TP = ctx.enter_context(nc.psum_tensor(f"{tag}_TP", [P, NP, P], f32))
        OV, WP = bank("OV", 2), bank("WP")
        PJ = [OV[:, 0], OV[:, 1]]
        outs = OV[:, :, 0:NP * VW2].rearrange("p b (a v) -> p b a v", v=VW2)
        cb_in, pj, pj_free, rot_done, ones = [sem(x) for x in ("cb_in", "pj", "pj_free", "rot", "ones")]
        bias_added = sem("bias_added")
        q_in, v_in = sem("q_in"), sem("v_in")
        s_full, t_full, o_full, ot_full, y_full = [sem(x) for x in ("s_full", "t_full", "o_full", "ot_full", "y_full")]
        bias_done, mx_done, sub_done, exp_done = [sem(x) for x in ("bias", "mx", "sub", "exp")]
        t_ev, rcp_done, norm_done, ot_ev, y_ev = [sem(x) for x in ("t_ev", "rcp", "norm", "ot_ev", "y_ev")]
        if conv_bias is not None:
            conv, scratch = conv_bias
            ext = sb("ext", [heads, 2 * S - 1])
            CB = sb("CB", [P, NP, S])
            ext_done, ext_out = sem("ext_done"), sem("ext_out")
            NPOS = conv.shape[1]
            E0 = S - 1 - NPOS // 2
        turned = ("", "r") if rope else ("",)
        order = [(n + r, ch, g) for n in "qk" for ch in range(NCH) for g in range(2) for r in turned]
        nproj = len(order)
        QS_ = HC * NCH
        block = ctx.enter_context(nc.Block())

        def over_tiles(eng, step, before, after):
            before()
            for t in range(2):
                step(t, t, t > 0, True)
            with eng.Fori(1, T // 2 - 1) as i:
                for j in range(2):
                    step(i * 2 + j, j, True, True)
            for t in range(T - 2, T):
                step(t, t % 2, True, t < T - 1)
            after()

        @block.sync
        def _(sp):
            if conv_bias is not None:
                sp.dma_start(ext[:, E0:E0 + NPOS], conv).then_inc(cb_in, 16)
                sp.wait_ge(ext_done, 2)
                L = 2 * S - 1
                sp.dma_start(scratch.rearrange("h (r l) -> h r l", l=L), ext[:].unsqueeze(1).to_broadcast([heads, S, L])).then_inc(ext_out, 16)
                sp.wait_ge(ext_out, 16)
                for h in range(heads):
                    e, pr = h % 2, h // 2
                    src = scratch[h, S - 1:S - 1 + S * (L - 1)].rearrange("(r l) -> r l", l=L - 1)[:, 0:S]
                    sp.dma_start(CB[e * S:(e + 1) * S, pr, :], src).then_inc(cb_in, 16)
            for dst, src, counted in loads:
                sp.dma_start(dst, src).then_inc(counted, 16)

        @block.tensor
        def _(pe):
            mm = nc.tensor.matmul
            pe.wait_ge(w_in, 16 * (len(names) + 2))
            for n, (name, ch, g) in enumerate(order):
                if n >= 2:
                    pe.wait_ge(pj_free, n - 1)
                for k in range(CH):
                    last = mm(PJ[n % 2], W[name][:, k, ch * P:(ch + 1) * P], lnT[:, k, g * 512:(g + 1) * 512], start=k == 0, stop=k == CH - 1)
                last.then_inc(pj, 1)
            for t in range(T):
                n = nproj + t
                pe.wait_ge(pj_free, n - 1)
                for k in range(CH):
                    last = mm(PJ[n % 2][:, 0:D], lnT[:, k, t * P:(t + 1) * P], W["v"][:, k, :], start=k == 0, stop=k == CH - 1)
                last.then_inc(pj, 1)

            def scores(t, j):
                pe.wait_ge(q_in, t * QS_ + QS_)
                if conv_bias is None:
                    ge(pe, sub_done, t)
                else:
                    ge(pe, bias_done, t * 2)
                for pr in range(NP):
                    ch, q = 2 * pr // HC, 2 * pr % HC
                    for b in range(2):
                        last = mm(SC[:, pr, b, :], Qm[j][:, ch, b, q:q + 2].rearrange("p e s -> p (e s)"),
                                  KTt[:, ch, bass.ds(t * P + b * S, S)], start=True, stop=True)
                last.then_inc(s_full, 1)

            def turn(t):
                ge(pe, t_ev, t)
                pe.wait_ge(exp_done, t + 1)
                for pr in range(NP):
                    last = nc.tensor.transpose(TP[:, pr, :], Pr[:, pr].rearrange("p b s -> p (b s)"), c["ident"])
                last.then_inc(t_full, 1)

            def weigh(t, j):
                ge(pe, ot_ev, t)
                pe.wait_ge(v_in, t + 1)
                pe.wait_ge(t_ev, t + 1)
                for pr in range(NP):
                    for b in range(2):
                        last = mm(outs[:, b, pr], PT[b * S:(b + 1) * S, pr, :], Vt[j][b * S:(b + 1) * S, pr * VW2:(pr + 1) * VW2],
                                  start=True, stop=True, tile_position=(b * S, 0))
                last.then_inc(o_full, 1)

            def turn_out(t):
                pe.wait_ge(norm_done, t * 2 + 2)
                for b in range(2):
                    last = nc.tensor.transpose(OV[:, b, OT0:512], oN[:, b].rearrange("p a d -> p (a d)"), c["ident"])
                last.then_inc(ot_full, 1)

            def project(t):
                ge(pe, y_ev, t)
                pe.wait_ge(ot_ev, t + 1)
                for b in range(2):
                    for e in range(2):
                        last = mm(WP[b * S:(b + 1) * S, 0, 0:D], oT[:, b, e * S:(e + 1) * S], W["o"][:, e, :],
                                  start=e == 0, stop=e == 1, tile_position=(0, b * S))
                last.then_inc(y_full, 1)

            def step(t, j, behind, ahead):
                turn(t)
                if behind:
                    turn_out(t - 1)
                if ahead:
                    scores(t + 1, 1 - j)
                weigh(t, j)
                if behind:
                    project(t - 1)

            def before():
                pe.wait_ge(ones, 1)
                pe.wait_ge(pj_free, nproj + T)
                scores(0, 0)

            def after():
                turn_out(T - 1)
                project(T - 1)

            over_tiles(pe, step, before, after)

        @block.gpsimd
        def _(pool):
            nc.gpsimd.memset(Vall[:], 1.0).then_inc(ones, 1)
            add_bias(nc, pool, X, *bias, bias_added)
            if rope:
                pool.wait_ge(rot_done, nproj // 4)
            else:
                pool.wait_ge(pj_free, nproj // 2)

            def queries(t, j):
                tok = bass.ds(t * P, P)
                ge(pool, s_full, t - 1)
                for e in range(HC):
                    for ch in range(NCH):
                        nc.gpsimd.tensor_tensor(Qm[j][:, ch, :, e, :], QT[:, ch, tok].rearrange("p (b s) -> p b s", b=2),
                                                mask[:, e:e + 1].unsqueeze(1).to_broadcast([P, 2, S]),
                                                ALU.mult).then_inc(q_in, 1)
                pool.wait_ge(pj_free, nproj + T)
                ge(pool, o_full, t - 1)
                nc.gpsimd.tensor_copy(Vt[j][:], Vall[:, bass.ds(t, 1), :].rearrange("p a n -> p (a n)")).then_inc(v_in, 1)

            for t in range(2):
                queries(t, t)
            with pool.Fori(1, T // 2) as i:
                for j in range(2):
                    queries(i * 2 + j, j)

        @block.vector
        def _(dve):
            if conv_bias is not None:
                dve.wait_ge(cb_in, 16)
                nc.vector.tensor_copy(ext[:, 0:E0], ext[:, E0:E0 + 1].to_broadcast([heads, E0])).then_inc(ext_done, 1)
                nc.vector.tensor_copy(ext[:, E0 + NPOS:], ext[:, E0 + NPOS - 1:E0 + NPOS].to_broadcast([heads, E0])).then_inc(ext_done, 1)
            turns = 0
            for n, (name, ch, g) in enumerate(order):
                dst = (QT if name[0] == "q" else KTt)[:, ch, g * 512:(g + 1) * 512]
                dve.wait_ge(pj, n + 1)
                if not rope:
                    nc.vector.tensor_copy(dst, PJ[n % 2]).then_inc(pj_free, 1)
                    continue
                wide = lambda a: a.rearrange("p (b s) -> p b s", s=S)
                table = c["sin" if name[1:] else "cos"].unsqueeze(1).to_broadcast([P, 512 // S, S])
                if not name[1:]:
                    nc.vector.tensor_tensor(wide(dst), wide(PJ[n % 2]), table, ALU.mult).then_inc(pj_free, 1)
                else:
                    ge(dve, rot_done, turns)
                    nc.vector.tensor_tensor(wide(rot[:]), wide(PJ[n % 2]), table, ALU.mult).then_inc(pj_free, 1)
                    dve.wait_ge(pj_free, n + 1)
                    nc.vector.tensor_tensor(dst, dst, rot[:], ALU.add).then_inc(rot_done, 1)
                    turns += 1
            dve.wait_ge(ones, 1)
            for t in range(T):
                dve.wait_ge(pj, nproj + t + 1)
                nc.vector.tensor_copy(Vall[:, t].rearrange("p (h v) -> p h v", v=dv + 1)[:, :, 0:dv],
                                      PJ[(nproj + t) % 2][:, 0:D].rearrange("p (h v) -> p h v", v=dv)).then_inc(pj_free, 1)
            if conv_bias is not None:
                dve.wait_ge(cb_in, 16 * (heads + 1))
            flat = lambda a: a.rearrange("p a b s -> p (a b) s")
            rows = lambda a: a.rearrange("p a b -> p (a b)")
            spread = lambda a: rows(a).unsqueeze(2).to_broadcast([P, NP * 2, S])

            def less_max(t):
                dve.wait_ge(s_full, t + 1)
                ge(dve, exp_done, t)
                src = SC
                if conv_bias is not None:
                    for b in range(2):
                        nc.vector.scalar_tensor_tensor(Sc[:, :, b, :], SC[:, :, b, :], float(dk) ** -0.5, CB[:],
                                                       ALU.mult, ALU.add).then_inc(bias_done, 1)
                    dve.wait_ge(bias_done, t * 2 + 2)
                    src = Sc
                nc.vector.tensor_reduce(rows(mxt[:]), flat(src[:]), AX.X, ALU.max).then_inc(mx_done, 1)
                dve.wait_ge(mx_done, t + 1)
                nc.vector.tensor_tensor(flat(Sc[:]), flat(src[:]), spread(mxt[:]), ALU.subtract).then_inc(sub_done, 1)

            def normalise(t):
                dve.wait_ge(o_full, t + 1)
                ge(dve, norm_done, t * 2)
                ge(dve, ot_full, t)
                for e in range(2):
                    r_ = slice(e * S, (e + 1) * S)
                    v0 = e * (dv + 1)
                    nc.vector.reciprocal(rs[r_], outs[r_, :, :, v0 + dv]).then_inc(rcp_done, 1)
                for e in range(2):
                    r_ = slice(e * S, (e + 1) * S)
                    v0 = e * (dv + 1)
                    dve.wait_ge(rcp_done, t * 2 + (e + 1))
                    nc.vector.tensor_tensor(oN[r_], outs[r_, :, :, v0:v0 + dv], rs[r_].unsqueeze(3).to_broadcast([S, 2, NP, dv]),
                                            ALU.mult).then_inc(norm_done, 1)

            def add(t):
                dve.wait_ge(bias_added, T)
                dve.wait_ge(y_full, t + 1)
                xs = X[:, bass.ds(t, 1), :].rearrange("p a n -> p (a n)")
                nc.vector.tensor_tensor(xs, xs, WP[:, 0, 0:D], ALU.add).then_inc(y_ev, 1)

            def step(t, j, behind, ahead):
                if ahead:
                    less_max(t + 1)
                normalise(t)
                if behind:
                    add(t - 1)

            over_tiles(dve, step, lambda: less_max(0), lambda: add(T - 1))

        @block.scalar
        def _(act):
            def exps(t):
                act.wait_ge(sub_done, t + 1)
                ge(act, t_full, t)
                nc.scalar.activation(Pr[:], Sc[:], ACT.Exp, scale=float(dk) ** -0.5 if conv_bias is None else 1.0).then_inc(exp_done, 1)

            def turned_in(t):
                act.wait_ge(t_full, t + 1)
                ge(act, o_full, t)
                nc.scalar.activation(PT[:], TP[:], ACT.Copy).then_inc(t_ev, 1)

            def turned_out(t):
                act.wait_ge(ot_full, t + 1)
                ge(act, y_full, t)
                nc.scalar.activation(oT[:], OV[:, :, OT0:512], ACT.Copy).then_inc(ot_ev, 1)

            def step(t, j, behind, ahead):
                turned_in(t)
                if behind:
                    turned_out(t - 1)
                if ahead:
                    exps(t + 1)

            over_tiles(act, step, lambda: exps(0), lambda: turned_out(T - 1))


FE = 352
NE = 8
NX = NE + 2
TOPK = 2
ROUTED_SCALE = 2.5
FCH = [(0, P), (P, 2 * P), (2 * P, FE)]


def expert_buffers(nc, ctx, w):
    sb = lambda n, s: [ctx.enter_context(nc.sbuf_tensor(f"moe_{n}{j}", s, f32)) for j in range(2)]
    sem = lambda n: ctx.enter_context(nc.semaphore("moe_" + n))
    gate, gate_in = ctx.enter_context(nc.sbuf_tensor("moe_gate", [P, CH, NE], f32)), sem("gate_in")
    gu, dn = sb("gu_raw", [P, CH, 2, FE]), sb("dn_raw", [P, 3, D])
    gu_in, dn_in = [[sem(f"{n}{j}") for j in range(2)] for n in ("gu_in", "dn_in")]
    loads = [(gate[:], w["gate"], gate_in)]
    loads += [(gu[j][:], w["gu"][j], gu_in[j]) for j in range(2)] + [(dn[j][:], w["down"][j], dn_in[j]) for j in range(2)]
    return (gate, gate_in, gu, dn, gu_in, dn_in), loads


def experts(nc, tag, X, lnT, c, w, buffers):
    ctx = ExitStack()
    with ctx:
        sb = lambda n, s, d=f32: ctx.enter_context(nc.sbuf_tensor(f"{tag}_{n}", s, d))
        sem = lambda n: ctx.enter_context(nc.semaphore(f"{tag}_{n}"))
        gate, gate_in, gu_raw, dn_raw, gu_in, dn_in = buffers
        lg, sc8, pk, t8 = [sb(n, [P, T, NE]) for n in ("lg", "sc8", "pk", "t8")]
        g1, g2 = sb("g1", [P, T * NE, NE]), sb("g2", [P, T * NE, NE])
        m8, s8 = sb("m8", [P, T]), sb("s8", [P, T])
        comb = sb("comb", [P, T, NX])
        gu = [[sb(f"gu{j}{k}", [P, CH, 2, FE], f32r) for k in range(2)] for j in range(2)]
        dn = [[sb(f"dn{j}{k}", [P, 3, D], f32r) for k in range(2)] for j in range(2)]
        h = [[sb(f"h{j}{k}", [P, 3, T * P], f32r) for k in range(2)] for j in range(2)]
        sg = [sb(f"sg{j}", [P, 512]) for j in range(2)]
        h32 = [sb(f"h32{j}", [P, 512]) for j in range(2)]
        GU = [ctx.enter_context(nc.psum_tensor(f"{tag}_GU{j}", [P, 2, 512], f32)) for j in range(2)]
        DN = [ctx.enter_context(nc.psum_tensor(f"{tag}_DN{j}", [P, 2, D], f32)) for j in range(2)]
        LG = ctx.enter_context(nc.psum_tensor(f"{tag}_LG", [P, T, NE], f32))
        lnH, lnL = sb("lnH", [P, CH, T * P], f32r), sb("lnL", [P, CH, T * P], f32r)
        ln_hi, ln_lo = sem("ln_hi"), sem("ln_lo")
        lg_full, r, rexp = sem("lg_full"), sem("r"), sem("rexp")
        gu_hi, gu_lo, dn_hi, dn_lo = sem("gu_hi"), sem("gu_lo"), sem("dn_hi"), sem("dn_lo")
        gu_full, silu_done, mul_done, hhi_done, hlo_done = [sem(x) for x in ("gu_full", "silu", "mul", "hhi", "hlo")]
        dn_full, dn_read = sem("dn_full"), sem("dn_read")
        UN = [(f, g) for f in range(3) for g in range(2)]
        NU, ND = len(UN), T // 2
        block = ctx.enter_context(nc.Block())

        def over_experts(eng, ahead, behind):
            def two(i):
                ahead(i * 2 + 1, 1)
                behind(i * 2, 0)
                ahead(i * 2 + 2, 0)
                behind(i * 2 + 1, 1)

            ahead(0, 0)
            two(0)
            with eng.Fori(1, NX // 2 - 1) as i:
                two(i)
            ahead(NX - 1, 1)
            behind(NX - 2, 0)
            behind(NX - 1, 1)

        def over_splits(eng, units, split_gu, split_dn, then=lambda: None):
            def two(i, last=False):
                for j in range(2):
                    e = i * 2 + j
                    units(e, j)
                    if not (last and j == 1):
                        split_dn(e + 1, 1 - j)
                    if not last:
                        split_gu(e + 2, j)

            split_gu(0, 0)
            split_gu(1, 1)
            split_dn(0, 0)
            then()
            two(0)
            with eng.Fori(1, NX // 2 - 1) as i:
                two(i)
            two(NX // 2 - 1, last=True)

        @block.sync
        def _(sp):
            def load(e, j):
                ge(sp, gu_lo, e - 1)
                sp.dma_start(gu_raw[j][:], w["gu"][e]).then_inc(gu_in[j], 16)
                ge(sp, dn_lo, e - 1)
                sp.dma_start(dn_raw[j][:], w["down"][e]).then_inc(dn_in[j], 16)

            with sp.Fori(1, NX // 2) as i:
                load(i * 2, 0)
                load(i * 2 + 1, 1)

        @block.tensor
        def _(pe):
            mm = nc.tensor.matmul
            pe.wait_ge(gate_in, 16)
            for t in range(T):
                for k in range(CH):
                    last = mm(LG[:, t, :], lnT[:, k, t * P:(t + 1) * P], gate[:, k, :], start=k == 0, stop=k == CH - 1)
            last.then_inc(lg_full, 1)

            def split_product(out, pairs):
                todo = [x for (lh, ll), (rh, rl) in pairs for x in ((lh, rh), (lh, rl), (ll, rh))]
                for n, (l, r_) in enumerate(todo):
                    last = mm(out, l, r_, start=n == 0, stop=n == len(todo) - 1)
                return last

            def up(e, j):
                pe.wait_ge(gu_lo, e + 1)
                for n, (f, g) in enumerate(UN):
                    lo, hi = FCH[f]
                    ge(pe, mul_done, e * NU + (n - 1))
                    for x in range(2):
                        last = split_product(GU[n % 2][0:hi - lo, x, :], [
                            ((gu[j][0][:, k, x, lo:hi], gu[j][1][:, k, x, lo:hi]),
                             (lnH[:, k, g * 512:(g + 1) * 512], lnL[:, k, g * 512:(g + 1) * 512])) for k in range(CH)])
                    last.then_inc(gu_full, 1)

            def down(e, j):
                pe.wait_ge(hlo_done, e * NU + NU)
                pe.wait_ge(dn_lo, e + 1)
                for n in range(ND):
                    ge(pe, dn_read, e * T + (2 * n - 2))
                    for a in range(2):
                        tok = slice((2 * n + a) * P, (2 * n + a + 1) * P)
                        last = split_product(DN[n % 2][:, a, :], [
                            ((h[j][0][0:hi - lo, f, tok], h[j][1][0:hi - lo, f, tok]), (dn[j][0][0:hi - lo, f, :], dn[j][1][0:hi - lo, f, :]))
                            for f, (lo, hi) in enumerate(FCH)])
                    last.then_inc(dn_full, 1)

            pe.wait_ge(ln_lo, CH)
            over_experts(pe, up, down)

        @block.scalar
        def _(act):
            def split_gu(e, j):
                act.wait_ge(gu_in[j], e * 8 + (16 - 8 * j))
                if not (isinstance(e, int) and e < 2):
                    act.wait_ge(gu_full, e * NU - NU)
                nc.scalar.activation(gu[j][0][:], gu_raw[j][:], ACT.Copy).then_inc(gu_hi, 1)

            def split_dn(e, j):
                act.wait_ge(dn_in[j], e * 8 + (16 - 8 * j))
                if not (isinstance(e, int) and e < 2):
                    act.wait_ge(dn_full, e * ND - ND)
                nc.scalar.activation(dn[j][0][:], dn_raw[j][:], ACT.Copy).then_inc(dn_hi, 1)

            def units(e, j):
                for n, (f, g) in enumerate(UN):
                    lo, hi = FCH[f]
                    act.wait_ge(gu_full, e * NU + (n + 1))
                    ge(act, mul_done, e * NU + (n - 1))
                    nc.scalar.activation(sg[n % 2][0:hi - lo], GU[n % 2][0:hi - lo, 0, :], ACT.Silu).then_inc(silu_done, 1)
                    if n >= 1:
                        hi_part(e, j, n - 1)
                hi_part(e, j, NU - 1)

            def hi_part(e, j, n):
                f, g = UN[n]
                lo, hi = FCH[f]
                act.wait_ge(mul_done, e * NU + (n + 1))
                if n == 0 and not (isinstance(e, int) and e < 2):
                    act.wait_ge(dn_full, e * ND - ND)
                nc.scalar.activation(h[j][0][0:hi - lo, f, g * 512:(g + 1) * 512], h32[n % 2][0:hi - lo], ACT.Copy).then_inc(hhi_done, 1)

            for k in range(CH):
                nc.scalar.activation(lnH[:, k], lnT[:, k], ACT.Copy).then_inc(ln_hi, 1)

            def routing():
                act.wait_ge(r, 2)
                nc.scalar.activation(sc8[:], lg[:], ACT.Exp).then_inc(rexp, 1)

            over_splits(act, units, split_gu, split_dn, routing)

        @block.gpsimd
        def _(pool):
            def lower(e, j, part, raw, hi, lo):
                pool.wait_ge(hi, e + 1)
                nc.gpsimd.tensor_tensor(part[j][1][:], raw[j][:], part[j][0][:].bitcast(f32), ALU.subtract).then_inc(lo, 1)

            def split_gu(e, j):
                lower(e, j, gu, gu_raw, gu_hi, gu_lo)

            def split_dn(e, j):
                lower(e, j, dn, dn_raw, dn_hi, dn_lo)

            def units(e, j):
                for n, (f, g) in enumerate(UN):
                    lo, hi = FCH[f]
                    pool.wait_ge(hhi_done, e * NU + (n + 1))
                    s_ = slice(g * 512, (g + 1) * 512)
                    nc.gpsimd.tensor_tensor(h[j][1][0:hi - lo, f, s_], h32[n % 2][0:hi - lo], h[j][0][0:hi - lo, f, s_].bitcast(f32),
                                            ALU.subtract).then_inc(hlo_done, 1)

            over_splits(pool, units, split_gu, split_dn)

        @block.vector
        def _(dve):
            n_ = [0]

            def step(ins):
                n_[0] += 1
                ins.then_inc(r, 1)
                dve.wait_ge(r, n_[0])

            over8 = lambda a: a.unsqueeze(2).to_broadcast([P, T, NE])
            V = nc.vector
            for k in range(CH):
                dve.wait_ge(ln_hi, k + 1)
                V.tensor_tensor(lnL[:, k], lnT[:, k], lnH[:, k].bitcast(f32), ALU.subtract).then_inc(ln_lo, 1)
            dve.wait_ge(lg_full, 1)
            step(V.tensor_reduce(m8[:], LG[:], AX.X, ALU.max))
            step(V.tensor_tensor(lg[:], LG[:], over8(m8[:]), ALU.subtract))
            dve.wait_ge(rexp, 1)
            step(V.tensor_reduce(s8[:], sc8[:], AX.X, ALU.add))
            step(V.reciprocal(m8[:], s8[:]))
            step(V.tensor_tensor(sc8[:], sc8[:], over8(m8[:]), ALU.mult))
            for t in range(T):
                ts = slice(t * NE, (t + 1) * NE)
                mine = sc8[:, t].unsqueeze(2).to_broadcast([P, NE, NE])
                other = sc8[:, t].unsqueeze(1).to_broadcast([P, NE, NE])
                V.tensor_tensor(g1[:, ts], other, mine, ALU.is_gt).then_inc(r, 1)
                V.tensor_tensor(g2[:, ts], other, mine, ALU.is_equal).then_inc(r, 1)
                n_[0] += 2
            dve.wait_ge(r, n_[0])
            g2v = g2[:].rearrange("p (t e) j -> p t (e j)", t=T)
            step(V.tensor_tensor(g2v, g2v, c["lower"].unsqueeze(1).to_broadcast([P, T, NE * NE]), ALU.mult))
            step(V.tensor_tensor(g1[:], g1[:], g2[:], ALU.add))
            step(V.tensor_reduce(pk[:].rearrange("p t e -> p (t e)"), g1[:], AX.X, ALU.add))
            step(V.tensor_scalar(t8[:], pk[:], float(TOPK), None, ALU.is_lt))
            step(V.tensor_tensor(pk[:], sc8[:], t8[:], ALU.mult))
            step(V.tensor_reduce(s8[:], pk[:], AX.X, ALU.add))
            step(V.tensor_scalar(m8[:], s8[:], 1e-20, None, ALU.add))
            step(V.reciprocal(s8[:], m8[:]))
            step(V.tensor_scalar(m8[:], s8[:], ROUTED_SCALE, None, ALU.mult))
            step(V.tensor_tensor(comb[:, :, 0:NE], pk[:], over8(m8[:]), ALU.mult))
            step(V.memset(comb[:, :, NE:NX], 1.0))

            def units(e, j):
                for n, (f, g) in enumerate(UN):
                    lo, hi = FCH[f]
                    dve.wait_ge(silu_done, e * NU + (n + 1))
                    ge(dve, hlo_done, e * NU + (n - 1))
                    V.tensor_tensor(h32[n % 2][0:hi - lo], sg[n % 2][0:hi - lo], GU[n % 2][0:hi - lo, 1, :], ALU.mult).then_inc(mul_done, 1)

            def add(e, j):
                for n in range(ND):
                    dve.wait_ge(dn_full, e * ND + (n + 1))
                    for a in range(2):
                        t = 2 * n + a
                        ge(dve, dn_read, e * T + (t - T + 1))
                        V.scalar_tensor_tensor(X[:, t], DN[n % 2][:, a, :], comb[:, t, bass.ds(e, 1)], X[:, t], ALU.mult, ALU.add).then_inc(dn_read, 1)

            over_experts(dve, units, add)


def context_means(nc, csum, mean, wide, mean_done, wide_done):
    def add_parts(pool):
        nc.gpsimd.tensor_tensor(mean[:], csum[:, :, 0], csum[:, :, 1], ALU.add).then_inc(mean_done, 1)

    def widen(act):
        act.wait_ge(mean_done, 1)
        for k in range(CH):
            nc.scalar.activation(wide[:, k], mean[:, k].unsqueeze(2).to_broadcast([P, B, S]), ACT.Copy, scale=1.0 / NK).then_inc(wide_done, 1)

    return {"pool": add_parts, "act": widen}


def mean_context(nc, tag, X, lnT, W, w_in, bias, wide, wide_done):
    ctx = ExitStack()
    with ctx:
        sem = lambda n: ctx.enter_context(nc.semaphore(f"{tag}_{n}"))
        PS = [ctx.enter_context(nc.psum_tensor(f"{tag}_ps{j}", [P, 512], f32)) for j in range(2)]
        full, read, bias_added = sem("full"), sem("read"), sem("bias_added")
        block = ctx.enter_context(nc.Block())

        @block.gpsimd
        def _(pool):
            add_bias(nc, pool, X, *bias, bias_added)

        @block.tensor
        def _(pe):
            pe.wait_ge(w_in, 32)
            pe.wait_ge(wide_done, CH)
            means = wide[:].rearrange("p c b s -> p c (b s)")
            for t in range(T):
                ge(pe, read, t - 1)
                tok = slice(t * P, (t + 1) * P)
                for n in range(2 * CH):
                    l, r_ = (lnT[:, n, tok], W["w1"][:, n, :]) if n < CH else (means[:, n - CH, tok], W["w2"][:, n - CH, :])
                    last = nc.tensor.matmul(PS[t % 2][:, 0:D], l, r_, start=n == 0, stop=n == 2 * CH - 1)
                last.then_inc(full, 1)

        @block.vector
        def _(dve):
            for t in range(T):
                dve.wait_ge(bias_added, t + 1)
                dve.wait_ge(full, t + 1)
                nc.vector.tensor_tensor(X[:, t], X[:, t], PS[t % 2][:, 0:D], ALU.add).then_inc(read, 1)


FG = 1024
NF = FG // P
NG = 4


def group_loads(w, W, t):
    return [(W["w1"][:], w["w1"][t]), (W["w2"][:], w["w2"][t]), (W["b2"][:], w["b2"][t:t + 1, :].to_broadcast([P, D]))]


def grouped_ffn(nc, tag, X, lnT, c, w, W, w_in, out):
    ctx = ExitStack()
    with ctx:
        sb = lambda n, s, d=f32: ctx.enter_context(nc.sbuf_tensor(f"{tag}_{n}", s, d))
        sem = lambda n: ctx.enter_context(nc.semaphore(f"{tag}_{n}"))
        w1, w2, b2 = [[W[j][n] for j in range(NG)] for n in ("w1", "w2", "b2")]
        b1 = sb("b1", [P, T, NF])
        h = [sb(f"h{j}", [P, NF, P]) for j in range(2)]
        xo = [sb(f"xo{j}", [P, D]) for j in range(2)]
        HP = [ctx.enter_context(nc.psum_tensor(f"{tag}_hp{j}", [P, 4, P], f32)) for j in range(4)]
        YP = [ctx.enter_context(nc.psum_tensor(f"{tag}_yp{j}", [P, 512], f32)) for j in range(2)]
        b_in = sem("b_in")
        h_full, h_ev, y_full, y_ev = sem("h_full"), sem("h_ev"), sem("y_full"), sem("y_ev")
        r_done, out_done = sem("r_done"), [sem(f"out_done{j}") for j in range(2)]
        block = ctx.enter_context(nc.Block())

        @block.sync
        def _(sp):
            sp.dma_start(b1[:], w["b1"]).then_inc(b_in, 16)

            for t in range(NG, T):
                sp.wait_ge(y_full, t - NG + 1)
                sp.wait_ge(r_done, t - NG + 1)
                for dst, src in group_loads(w, W[t % NG], t):
                    sp.dma_start(dst, src).then_inc(w_in[t % NG], 16)

        @block.tensor
        def _(pe):
            mm = nc.tensor.matmul

            for t in range(T):
                j, wj = t % 2, t % NG
                pe.wait_ge(w_in[wj], (t // NG + 1) * 48)
                for g in range(2):
                    ge(pe, h_ev, t * 2 + (g - 3))
                    for f in range(4):
                        for k in range(CH):
                            last = mm(HP[2 * j + g][:, f, :], w1[wj][:, k, (4 * g + f) * P:(4 * g + f + 1) * P], lnT[:, k, t * P:(t + 1) * P],
                                      start=k == 0, stop=k == CH - 1)
                    last.then_inc(h_full, 1)
                ge(pe, y_ev, t - 1)
                for g in range(2):
                    pe.wait_ge(h_ev, t * 2 + (g + 1))
                    for f in range(4):
                        last = mm(YP[j][:, 0:D], h[j][:, 4 * g + f, :], w2[wj][:, 4 * g + f, :], start=g + f == 0, stop=g + f == 4)
                last.then_inc(y_full, 1)

        @block.vector
        def _(dve):
            dve.wait_ge(b_in, 16)
            for t in range(T):
                j = t % 2
                for g in range(2):
                    dve.wait_ge(h_full, t * 2 + (g + 1))
                    ge(dve, y_full, t - 1)
                    nc.vector.tensor_tensor(h[j][:, 4 * g:4 * g + 4, :], HP[2 * j + g][:],
                                            b1[:, t, 4 * g:4 * g + 4].unsqueeze(2).to_broadcast([P, 4, P]), ALU.add).then_inc(h_ev, 1)
                dve.wait_ge(y_full, t + 1)
                ge(dve, out_done[j], (t // 2) * 16)
                nc.vector.tensor_tensor(xo[j][:], X[:, t], YP[j][:, 0:D], ALU.add).then_inc(y_ev, 1)
                dve.wait_ge(y_ev, t + 1)
                nc.vector.tensor_tensor(xo[j][:], xo[j][:], b2[t % NG][:], ALU.add).then_inc(r_done, 1)

        @block.scalar
        def _(act):
            for t in range(T):
                act.wait_ge(r_done, t + 1)
                act.dma_start(out[t], xo[t % 2][:]).then_inc(out_done[t % 2], 16)
            for j in range(2):
                act.wait_ge(out_done[j], 16 * (T // 2))


CONST = {"ident": P, "spread": P, "hmask": 2, "mrow": 1, "cos": S, "sin": S, "lower": NE * NE, "half": 2, "eighth": 8}
H1, DQK1, DV1 = 8, 64, 32


def program(nc, a, out):
    ctx = ExitStack()
    with ctx:
        sb = lambda n, s, d=f32: ctx.enter_context(nc.sbuf_tensor(n, s, d))
        X = sb("X", [P, T, D])
        lnT = sb("lnT", [P, CH, T * P])
        consts = sb("consts", [P, sum(CONST.values())])
        csum = sb("csum", [P, CH, 2, B])
        first_in = ctx.enter_context(nc.semaphore("first_in"))
        ln = {n: ctx.enter_context(nc.semaphore(f"ln_{n}")) for n in LN_SEMS}
        c, at = {}, 0
        for name, width in CONST.items():
            c[name] = consts[:, at:at + width]
            at += width

        xa_parts = ExitStack()
        E = xattn_buffers(nc, xa_parts)

        with nc.Block() as block:
            @block.sync
            def _(sp):
                sp.dma_start(X[:], a["x"].rearrange("(t p) n -> p t n", p=P)).then_inc(first_in, 16)
                sp.dma_start(consts[:], a["consts"]).then_inc(first_in, 16)
                xattn_loads(sp, E, {k: a["xa_" + k] for k in ("wq", "bq", "wk", "bk", "wv", "bv", "wo", "bo")}, a["ctxT"])
                sp.wait_ge(first_in, 32)

            @block.vector
            def _(dve):
                xattn_ones(nc, nc.vector, E, 0)

            @block.gpsimd
            def _(pool):
                xattn_ones(nc, nc.gpsimd, E, 1)

        layer_norm(nc, 0, ln, X, lnT, c, also={"pool": lambda pool: xattn_fill(nc, pool, E)})
        xattn(nc, X, lnT, c, E, a["ctxT"], csum)
        xa_parts.close()

        with ExitStack() as parts:
            wide = [P, CH, H0 * D0]
            W, w_in, loads = stage_weights(nc, parts, "sa", {k: a["sa_" + k] for k in ("q", "qr", "k", "kr", "v", "o")},
                                           q=wide, qr=wide, k=wide, kr=wide, v=[P, CH, D], o=[P, 2, D])
            row, row_in, row_load = bias_row(nc, parts, "sa", a["sa_bo"])
            layer_norm(nc, 1, ln, X, lnT, c, loads=loads + row_load)
            self_attention(nc, "sa", X, lnT, c, W, w_in, (row, row_in), H0, D0, D0, c["eighth"], rope=True)

        with ExitStack() as parts:
            moe = {k: a["moe_" + k] for k in ("gate", "gu", "down")}
            buffers, loads = expert_buffers(nc, parts, moe)
            layer_norm(nc, 2, ln, X, lnT, c, loads=loads)
            experts(nc, "moe", X, lnT, c, moe, buffers)

        with ExitStack() as parts:
            W, w_in, loads = stage_weights(nc, parts, "mc", {k: a["mc_" + k] for k in ("w1", "w2")}, w1=[P, CH, D], w2=[P, CH, D])
            row, row_in, row_load = bias_row(nc, parts, "mc", a["mc_b"])
            mean = parts.enter_context(nc.sbuf_tensor("mc_mean", [P, CH, B], f32))
            wide = parts.enter_context(nc.sbuf_tensor("mc_wide", [P, CH, B, S], f32))
            mean_done, wide_done = [parts.enter_context(nc.semaphore(f"mc_{n}_done")) for n in ("mean", "wide")]
            layer_norm(nc, 3, ln, X, lnT, c, loads=loads + row_load, also=context_means(nc, csum, mean, wide, mean_done, wide_done))
            mean_context(nc, "mc", X, lnT, W, w_in, (row, row_in), wide, wide_done)

        gf = ExitStack()
        gf_W = [{n: gf.enter_context(nc.sbuf_tensor(f"gf_{n}{j}", s_, f32))
                 for n, s_ in (("w1", [P, CH, FG]), ("w2", [P, NF, D]), ("b2", [P, D]))} for j in range(NG)]
        gf_in = [gf.enter_context(nc.semaphore(f"gf_w_in{j}")) for j in range(NG)]
        gf_dram = {k: a["gf_" + k] for k in ("w1", "b1", "w2", "b2")}
        gf_loads = [(dst, src, gf_in[t]) for t in range(NG) for dst, src in group_loads(gf_dram, gf_W[t], t)]

        with ExitStack() as parts:
            wide = [P, CH, H1 * DQK1]
            W, w_in, loads = stage_weights(nc, parts, "sb", {k: a["sb_" + k] for k in ("q", "k", "v", "o")},
                                           q=wide, k=wide, v=[P, CH, D], o=[P, 2, D])
            row, row_in, row_load = bias_row(nc, parts, "sb", a["sb_bo"])
            layer_norm(nc, 4, ln, X, lnT, c, loads=loads + row_load)
            scratch = nc.dram_tensor("bias_scratch", (H1, S * (2 * S - 1)), f32, kind="Internal").ap()
            self_attention(nc, "sb", X, lnT, c, W, w_in, (row, row_in), H1, DQK1, DV1, c["half"], conv_bias=(a["sb_conv"], scratch), loads=gf_loads)

        layer_norm(nc, 5, ln, X, lnT, c)
        with gf:
            grouped_ffn(nc, "gf", X, lnT, c, gf_dram, gf_W, gf_in, out)


def shape_constants():
    import numpy as np

    p = np.arange(P)
    d = p % D0
    spread = np.zeros((P, P), np.float32)
    spread[32 * (p // 32) + D0, p] = 1.0
    freqs = (np.float32(10000.0) ** (-np.arange(0, D0, 2, dtype=np.float32) / np.float32(D0))).astype(np.float32)
    angles = (np.arange(S, dtype=np.float32)[:, None] * freqs).astype(np.float32)
    sign = np.where(d < D0 // 2, -1.0, 1.0).astype(np.float32)[:, None]
    e, j = np.divmod(np.arange(NE * NE), NE)
    parts = {
        "ident": np.eye(P),
        "spread": spread,
        "hmask": np.stack([d.astype(int) * 0 + ((p % 32) // D0 == h) for h in range(2)], 1),
        "mrow": np.where(p == 97, -1.0, 0.0)[:, None],
        "cos": np.cos(angles)[:, d // 2].T,
        "sin": np.sin(angles)[:, d // 2].T * sign,
        "lower": np.tile((j < e)[None], (P, 1)),
        "eighth": np.stack([p // D0 == h for h in range(8)], 1),
        "half": np.stack([p // (P // 2) == h for h in range(2)], 1),
    }
    return np.ascontiguousarray(np.concatenate([parts[k] for k in CONST], 1).astype(np.float32))


def kernel(**inputs):
    import numpy as np
    import concourse.bacc as bacc
    from concourse.bass_utils import run_bass_kernel_spmd

    i = {k: np.asarray(v) for k, v in inputs.items()}

    def rows(w):
        return w.reshape(-1, P, w.shape[-1]).transpose(1, 0, 2)

    def quads(w):
        n = w.size // D
        o = np.zeros((4, 32, 4, n), w.dtype)
        o[:, :D0] = w.reshape(4, 4, D0, n).transpose(1, 2, 0, 3)
        return o.reshape(P, 4, n)

    def pairs_rows(w, heads):
        return w.reshape(heads // 2, 2, -1, w.shape[-1]).transpose(0, 2, 1, 3).reshape(P, 2, -1)

    wq, wkv, bkv = i["L0_xattn_Wq"], i["L0_xattn_Wkv"], i["L0_xattn_bkv"]
    pairs = rows(wq).reshape(P, CH, 8, 1, 32)
    w_q, w_k, w_v = np.split(i["L0_attn_w_qkv"], 3, axis=1)
    turn = (np.arange(H0)[:, None] * D0 + np.concatenate([np.arange(1, D0, 2), np.arange(0, D0, 2)])).ravel()
    qk = i["L1_attn_W_qk"]
    halves = lambda w: w.reshape(D, 2, FE).transpose(1, 0, 2)
    gate_w = np.concatenate([i["L0_ffn_w_gate"], halves(i["L0_ffn_sw_gate"])])
    up_w = np.concatenate([i["L0_ffn_w_up"], halves(i["L0_ffn_sw_up"])])
    down_w = np.concatenate([i["L0_ffn_w_down"], i["L0_ffn_sw_down"].reshape(2, FE, D)])
    down = np.zeros((NX, 3 * P, D), down_w.dtype)
    down[:, :FE] = down_w
    W = i["L1_xattn_W"]
    arrays = {
        "x": i["x"].reshape(T * P, D),
        "consts": shape_constants(),
        "ctxT": i["ctx_1024"].transpose(0, 2, 1).reshape(B, CH, P, NK).transpose(0, 2, 1, 3),
        "xa_wq": np.broadcast_to(pairs, (P, CH, 8, 3, 32)).reshape(P, CH, 8, 96),
        "xa_bq": np.tile(i["L0_xattn_bq"].reshape(8, 32).T, (3, 1)),
        "xa_wk": rows(wkv[:, 0::2]),
        "xa_bk": bkv[0::2].reshape(CH, P).T,
        "xa_wv": rows(wkv[:, 1::2]),
        "xa_bv": quads(bkv[1::2])[:, :, 0],
        "xa_wo": quads(i["L0_xattn_Wout"]),
        "xa_bo": i["L0_xattn_bout"],
        "sa_q": rows(w_q), "sa_qr": rows(w_q[:, turn]), "sa_k": rows(w_k), "sa_kr": rows(w_k[:, turn]),
        "sa_v": rows(w_v), "sa_o": pairs_rows(i["L0_attn_w_out"], H0), "sa_bo": i["L0_attn_b_out"],
        "moe_gate": rows(i["L0_ffn_gate_w"].T),
        "moe_gu": np.stack([gate_w, up_w], 2).reshape(NX, CH, P, 2, FE).transpose(0, 2, 1, 3, 4),
        "moe_down": down.reshape(NX, 3, P, D).transpose(0, 2, 1, 3),
        "mc_w1": rows(W[:, :D].T), "mc_w2": rows(W[:, D:].T), "mc_b": i["L1_xattn_b"],
        "sb_q": rows(qk[:, :H1 * DQK1]), "sb_k": rows(qk[:, H1 * DQK1:]), "sb_v": rows(i["L1_attn_W_v"]),
        "sb_o": pairs_rows(i["L1_attn_W_out"], H1), "sb_bo": i["L1_attn_b_out"], "sb_conv": i["L1_attn_conv"],
        "gf_w1": i["L1_ffn_W1"].transpose(0, 2, 1).reshape(T, CH, P, 1024).transpose(0, 2, 1, 3),
        "gf_b1": i["L1_ffn_b1"].reshape(T, 8, P).transpose(2, 0, 1),
        "gf_w2": i["L1_ffn_W2"].transpose(0, 2, 1).reshape(T, 8, P, D).transpose(0, 2, 1, 3),
        "gf_b2": i["L1_ffn_b2"],
    }
    arrays = {k: np.ascontiguousarray(v) for k, v in arrays.items()}
    nc = bacc.Bacc("TRN2", target_bir_lowering=False, num_devices=1)
    a = {k: nc.dram_tensor("in_" + k, v.shape, mybir.dt.from_np(v.dtype), kind="ExternalInput").ap() for k, v in arrays.items()}
    out = nc.dram_tensor("out_x", (T, P, D), f32, kind="ExternalOutput").ap()
    program(nc, a, out)
    done = run_bass_kernel_spmd(nc, [{"in_" + k: v for k, v in arrays.items()}], core_ids=[0])
    return done.results[0]["out_x"].reshape(B, S, D)
```

```python
import concourse.bass as bass
from concourse import mybir
from contextlib import ExitStack

f32 = mybir.dt.float32
f32r = mybir.dt.float32r
ALU = mybir.AluOpType
ACT = mybir.ActivationFunctionType
AX = mybir.AxisListType

P = 128
D = 256
CH = D // P
B, S = 16, 64
T = B * S // P
NK = 1601
NKP = NK + 1
KT = -(-NK // P)
KLAST = NK - P * (KT - 1)
H0, D0 = 16, 16
VW = D0 + 1
VROW = H0 * VW + D0


def ge(eng, sem, value):
    if isinstance(value, int) and value <= 0:
        return
    eng.wait_ge(sem, value)


RING = ("K", "V", "Q", "E", "W")


def xattn_phase(b, h, fill, chain, late):
    out, fill, late = [], list(fill), dict(late)
    for u in range(8):
        out.append(("mx", b, h, u))
        if fill and (u in (1, 3, 4, 6) or u >= 1 and len(fill) > 4):
            out.append(fill.pop(0))
    out += fill + chain[:2] + [("mt", b, h, 0)] + chain[2:3]
    for g in range(7):
        out.append(("st", b, h, g))
        if g == 0:
            out += chain[3:]
        if g >= 1:
            out.append(("pv", b, h, g - 1))
        out += late.get(g, [])
    return out + [("pv", b, h, 6)]


def xattn_order(first, more):
    K = lambda b, h: [("K", b, h, u) for u in range(4)]
    V = lambda b, lo, hi: [("V", b, 0, u) for u in range(lo, hi)]
    split = lambda b: {1: [("cv", b, 0, 0)], 4: [("cv", b, 0, 1)]}
    o = []
    for b in range(2):
        queries = {2: [("Q", 2, 0, 0)], 5: [("Q", 2, 0, 1)]} if b == 1 and more else {}
        late = (split(b + 1) if b == 0 or more else {}) | queries
        k = K(b, 1)
        e = [("E", b - 1, 0, 0)] if b == 1 or not first else []
        w = [("W", -2, 0, 0), ("W", -2, 0, 1)] if b == 0 and not first else []
        o += xattn_phase(b, 0, [k[0]] + e + k[1:3] + w, [k[3]] + V(b, 4, 7), late)
        ahead = b == 0 or more
        o += xattn_phase(b, 1, K(b + 1, 0) if ahead else [], V(b + 1, 0, 4) if ahead else [], {})
    return o


XATTN_FIRST = ([("cv", 0, 0, k) for k in range(2)] + [("K", 0, 0, k) for k in range(4)]
               + [("Q", 0, 0, 0), ("Q", 0, 0, 1)] + [("V", 0, 0, v) for v in range(4)])
XATTN_LAST = [("E", 1, 0, 0), ("W", 0, 0, 0), ("W", 0, 0, 1)]
KCOLS = [(0, 512), (512, 1024), (1024, 1536), (1536, NKP)]
CVCOLS = [(0, 1024), (1024, NKP)]
MXCOLS, MXN = [0, 400, 800, NK - 402], 402
DMAS_KST = 12


def xattn_buffers(nc, ctx):
    sb = lambda n, s, d=f32: ctx.enter_context(nc.sbuf_tensor("xa_" + n, s, d))
    E = {
        "raw": sb("raw", [P, CH, NKP]),
        "KS": sb("keys", [98, 8, NKP], f32r),
        "V": [sb(f"values{j}", [P, KT, VROW]) for j in range(2)],
        "wv": sb("wv", [P, CH, D]), "wk": sb("wk", [P, CH, D]),
        "wq": sb("wq96", [P, CH, 8, 96]), "bq": sb("bq96", [96, 8]), "bk": sb("bk", [P, CH]),
        "bv": sb("bv", [P, 4]), "wo": sb("wo", [P, 4, D]), "bo": sb("bo", [P, D]),
    }
    for n in ("wv_in", "wk_in", "raw_in", "w_in", "init", "ones"):
        E[n] = ctx.enter_context(nc.semaphore("xa_" + n))
    return E


def xattn_loads(sp, E, w, ctxT):
    sp.dma_start(E["wk"][:], w["wk"]).then_inc(E["wk_in"], 16)
    sp.dma_start(E["raw"][:, :, 0:NK], ctxT[0]).then_inc(E["raw_in"], 16)
    sp.dma_start(E["wv"][:], w["wv"]).then_inc(E["wv_in"], 16)
    for n in ("wq", "bq", "bk", "bv", "wo"):
        sp.dma_start(E[n][:], w[n]).then_inc(E["w_in"], 16)
    sp.dma_start(E["bo"][:], w["bo"].rearrange("(a n) -> a n", a=1).to_broadcast([P, D])).then_inc(E["w_in"], 16)


def xattn_ones(nc, eng, E, half):
    eng.memset(E["KS"][96:98, 4 * half:4 * half + 4].bitcast(f32), 1.0).then_inc(E["ones"], 1)


def xattn_fill(nc, pool, E):
    nc.gpsimd.memset(E["raw"][:, :, NK:NKP], 0.0).then_inc(E["init"], 1)
    for j in range(2):
        nc.gpsimd.memset(E["V"][j][:], 1.0).then_inc(E["init"], 1)


def xattn(nc, X, stats, lnT, c, E, ctxT, csum):
    ctx = ExitStack()
    with ctx:
        sb = lambda n, s, d=f32: ctx.enter_context(nc.sbuf_tensor(n, s, d))
        sem = lambda n: ctx.enter_context(nc.semaphore(n))
        raw, KS, V, wo, bo = E["raw"], E["KS"], E["V"], E["wo"], E["bo"]
        wq96, bq96, bk, bvq = E["wq"], E["bq"], E["bk"], E["bv"]
        wk_in, wv_in, w_in, raw_in, init = [E[n] for n in ("wk_in", "wv_in", "w_in", "raw_in", "init")]
        ctx_hi, ctx_lo = sb("xa_ctx_hi", [P, CH, NKP], f32r), sb("xa_ctx_lo", [P, CH, NKP], f32r)
        kstage_hi, kstage_lo = sb("xa_kst_hi", [P, NKP], f32r), sb("xa_kst_lo", [P, NKP], f32r)
        QS = [sb(f"xa_queries{j}", [98, 8, P], f32r) for j in range(2)]
        Q96 = sb("xa_q96", [96, 8, P], f32r)
        qtmp = sb("xa_qtmp", [96, 4, P])
        PTN = 4
        PT = [sb(f"xa_pt{j}", [P, 2, 512]) for j in range(PTN)]
        o_sb = sb("xa_o", [P, 4, S])
        rec = sb("xa_rec", [P, 4, S])
        oN = sb("xa_on", [P, 4, P])
        mx = sb("xa_mx", [P, 4, 4])
        nmx = sb("xa_nmx", [P, 4])
        nm = sb("xa_nm", [P, 4, 2], f32r)
        kraw = [E[n][:].rearrange("p c n -> p (c n)") for n in ("wk", "wv")]
        wk = [sb(f"xa_wk{j}", [P, CH, D], f32r) for j in range(2)]
        wv = [sb(f"xa_wv{j}", [P, CH, D], f32r) for j in range(2)]
        SC = [ctx.enter_context(nc.psum_tensor(f"xa_sc{j}", [P, 2, 512], f32)) for j in range(2)]
        OP = [ctx.enter_context(nc.psum_tensor(f"xa_op{j}", [P, 512], f32)) for j in range(2)]
        PJ = [ctx.enter_context(nc.psum_tensor(f"xa_pj{j}", [P, 512], f32)) for j in range(2)]

        w_split, bo_added = sem("xa_w_split"), sem("xa_bo_added")
        hi_done, lo_done, csum_done = sem("xa_hi_done"), sem("xa_lo_done"), sem("xa_csum_done")
        full = {k: sem(f"xa_{k}_full") for k in RING}
        free = {k: sem(f"xa_{k}_free") for k in RING if k != "E"}
        khi, klo = sem("xa_khi"), sem("xa_klo")
        kst_in = [sem(f"xa_kst_in{h}") for h in range(2)]
        q_in = sem("xa_q_in")
        sc_full = {k: sem(f"xa_{k}_full") for k in ("mx", "st")}
        mx_done, nm_done, mt_full, mrow = sem("xa_mx_done"), sem("xa_nm_done"), sem("xa_mt_full"), sem("xa_mrow")
        ex_done, pv_done, o_ev = sem("xa_ex_done"), sem("xa_pv_done"), sem("xa_o_ev")
        rec_done, on_done = sem("xa_rec_done"), sem("xa_on_done")
        stats_done = sem("xa_stats")
        pch, qch = sem("xa_pch"), sem("xa_qch")

        PER = {"K": 8, "V": 7, "Q": 2, "E": 1, "W": 2, "mx": 16, "st": 14, "pv": 14, "mt": 2, "cv": 2}
        INNER = {"K": 4, "mx": 8, "st": 7, "pv": 7, "mt": 1}

        def nth(step, i):
            k, b, h, n = step
            if k in ("Q", "W"):
                return PER[k] * (i + b // 2) + (n + 1)
            return (i * (2 * PER[k])) + (PER[k] * b + INNER.get(k, 0) * h + n + 1)

        def z(i):
            return 0 if i is None else i

        def ptslot(step):
            return (nth(step, 0) - 1) % PTN

        START, MIDDLE, END = xattn_order(True, True), xattn_order(False, True), xattn_order(False, False)

        def past(order, n, i, kinds):
            before = []
            if order is not XATTN_FIRST:
                before = [(x, 0) for x in XATTN_FIRST]
            if order is MIDDLE or order is END or order is XATTN_LAST:
                before += [(x, i - 1) for x in START]
            if order is XATTN_LAST:
                before += [(x, i) for x in END]
            return [x for x in before + [(x, z(i)) for x in order[:n]] if x[0][0] in kinds]

        def ring_before(order, kinds, n, i):
            before = past(order, n, i, kinds)
            return before[-2] if len(before) >= 2 else None

        def bank(order, kinds, n, i):
            return len(past(order, n, 1, kinds)) % 2

        def walk(steps, eng):
            steps(XATTN_FIRST, None)
            steps(START, 0)
            with eng.Fori(1, T - 1) as i:
                steps(MIDDLE, i)
            steps(END, T - 1)
            steps(XATTN_LAST, T - 1)

        block = ctx.enter_context(nc.Block())

        @block.sync
        def _(sp):
            def steps(order, i):
                for n, step in enumerate(order):
                    k, b, h, u = step
                    if (k, u) == ("V", 3) and i is None or (k, h, u) == ("st", 1, 1) and order is not END:
                        b_ = 0 if i is None else b + 1
                        ge(sp, csum_done, nth(("cv", b_, 0, 1), z(i)) * 2)
                        ge(sp, lo_done, nth(("cv", b_, 0, 1), z(i)))
                        sp.dma_start(raw[:, :, 0:NK], ctxT[2 * z(i) + (b_ + 1)]).then_inc(raw_in, 16)
                    if k == "K" and u == 3:
                        ge(sp, klo, nth(step, z(i)))
                        for r, src in ((0, kstage_hi), (1, kstage_lo), (2, kstage_hi)):
                            for q in range(4):
                                sp.dma_start(KS[32 * r:32 * r + 32, 4 * h + q, :].bitcast(f32),
                                             src[32 * q:32 * q + 32].bitcast(f32)).then_inc(kst_in[h], 16)

            walk(steps, sp)

        @block.gpsimd
        def _(pool):
            def steps(order, i):
                for n, step in enumerate(order):
                    k, b, h, u = step
                    if k == "cv":
                        ge(pool, hi_done, nth(step, z(i)) * 2)
                        lo, hi = CVCOLS[u]
                        nc.gpsimd.tensor_tensor(ctx_lo[:, :, lo:hi], raw[:, :, lo:hi],
                                                ctx_hi[:, :, lo:hi].bitcast(f32), ALU.subtract).then_inc(lo_done, 1)
                    if k == "K":
                        lo, hi = KCOLS[u]
                        ge(pool, khi, nth(step, z(i)))
                        nc.gpsimd.tensor_tensor(kstage_lo[:, lo:hi], kraw[u % 2][:, 0:hi - lo],
                                                kstage_hi[:, lo:hi].bitcast(f32), ALU.subtract).then_inc(klo, 1)
                    if (k, h, u) == ("mx", 0, 7) or (k, u) == ("Q", 1):
                        if k == "Q":
                            pair, want = 0, nth(step, z(i))
                        elif b == 0:
                            pair, want = 1, nth(("Q", 0, 0, 1), i)
                        else:
                            continue
                        ge(pool, free["Q"], want)
                        if not (i is None or (isinstance(i, int) and i == 0 and pair == 1)):
                            rel = 0 if pair == 0 else -1
                            ge(pool, sc_full["st"], nth(("st", rel, 1, 6), i))
                        for e in range(2):
                            nc.gpsimd.tensor_tensor(QS[pair][0:96, :, e * S:(e + 1) * S],
                                                    Q96[:, :, pair * S:(pair + 1) * S].bitcast(f32),
                                                    c["hmask"][0:96, e:e + 1].unsqueeze(1).to_broadcast([96, 8, S]),
                                                    ALU.mult).then_inc(q_in, 1)
                    if k == "E":
                        ge(pool, rec_done, nth(step, i))
                        if b == 0:
                            ge(pool, full["W"], nth(("W", -2, 0, 1), i))
                        nc.gpsimd.tensor_tensor(o_sb[:], o_sb[:], rec[:], ALU.mult).then_inc(pch, 1)
                        pool.wait_ge(pch, nth(step, i))
                        nc.gpsimd.tensor_tensor(oN[:, :, (b % 2) * S:(b % 2 + 1) * S], o_sb[:],
                                                bvq[:].unsqueeze(2).to_broadcast([P, 4, S]), ALU.add).then_inc(on_done, 1)

            def first_steps(order, i):
                steps(order, i)
                if order is XATTN_FIRST:
                    pool.wait_ge(w_in, 16 * 6)
                    for t in range(T):
                        nc.gpsimd.tensor_tensor(X[:, t], X[:, t], bo[:], ALU.add).then_inc(bo_added, 1)

            walk(first_steps, pool)

        @block.scalar
        def _(act):
            act.wait_ge(w_in, 16 * 6)

            def steps(order, i):
                for n, step in enumerate(order):
                    k, b, h, u = step
                    if k == "K":
                        lo, hi = KCOLS[u]
                        ge(act, full["K"], nth(step, z(i)))
                        if i is not None and u in (0, 2):
                            ph = (b - 1, 1) if h == 0 else (b, 0)
                            done = nth(("E", ph[0], 0, 0), i) * (16 * DMAS_KST)
                            ge(act, kst_in[ph[1]], done)
                        kr = kraw[u % 2]
                        ge(act, klo, nth(step, z(i)) - 2)
                        nc.scalar.activation(kr[:, 0:hi - lo], PJ[bank(order, RING, n, i)][:, 0:hi - lo],
                                             ACT.Identity, bias=bk[:, h:h + 1]).then_inc(free["K"], 1)
                        ge(act, free["K"], nth(step, z(i)))
                        nc.scalar.activation(kstage_hi[:, lo:hi], kr[:, 0:hi - lo], ACT.Copy).then_inc(khi, 1)
                    elif k == "V":
                        nt = 2 if u < 6 else 1
                        rows = P if u < 6 else KLAST
                        ge(act, full["V"], nth(step, z(i)))
                        if u == 0 and i is not None and not (isinstance(i, int) and i == 0 and b == 1):
                            ge(act, pv_done, nth(("pv", b - 2, 1, 6), i))
                        if i is None and u == 0:
                            act.wait_ge(init, 3)
                        vdst = V[b % 2][0:rows, 2 * u:2 * u + nt, 0:H0 * VW].rearrange("p k (h s) -> p k h s", s=VW)[:, :, :, 0:D0]
                        vsrc = PJ[bank(order, RING, n, i)][0:rows, 0:nt * D].rearrange("p (k h s) -> p k h s", k=nt, s=D0)
                        for kk in range(nt):
                            ins = nc.scalar.activation(vdst[:, kk], vsrc[:, kk], ACT.Copy)
                        ins.then_inc(free["V"], 1)
                    elif k == "st":
                        nt = 2 if u < 6 else 1
                        rows = P if u < 6 else KLAST
                        ge(act, sc_full["st"], nth(step, i))
                        ge(act, pv_done, nth(step, i) - PTN)
                        nc.scalar.activation(PT[ptslot(step)][0:rows, 0:nt], SC[bank(order, ("mx", "st"), n, i)][0:rows, 0:nt],
                                             ACT.Exp, scale=float(D0) ** -0.5).then_inc(ex_done, 1)

            walk(steps, act)

        @block.vector
        def _(dve):
            for n, (src, raw_w, dst) in enumerate(((wk_in, E["wk"], wk), (wv_in, E["wv"], wv))):
                dve.wait_ge(src, 16)
                nc.vector.tensor_copy(dst[0][:], raw_w[:]).then_inc(w_split, 1)
                dve.wait_ge(w_split, 2 * n + 1)
                nc.vector.tensor_tensor(dst[1][:], raw_w[:], dst[0][:].bitcast(f32), ALU.subtract).then_inc(w_split, 1)
            dve.wait_ge(w_in, 16 * 6)

            def steps(order, i):
                for n, step in enumerate(order):
                    k, b, h, u = step
                    if k == "cv":
                        lo, hi = CVCOLS[u]
                        ge(dve, raw_in, 16 * (nth(("E", b, 0, 0), z(i))))
                        if i is None:
                            dve.wait_ge(init, 1)
                        else:
                            ge(dve, full["K"], nth(("K", b - 1, 1, 2 * u + 1), i))
                            if u == 1:
                                ge(dve, full["V"], nth(("V", b - 1, 0, 6), i))
                        bat = 0 if i is None else 2 * i + b
                        for ch in range(CH):
                            nc.vector.tensor_copy(ctx_hi[:, ch, lo:hi], raw[:, ch, lo:hi]).then_inc(hi_done, 1)
                        for ch in range(CH):
                            nc.vector.tensor_reduce(csum[:, ch, u, bass.ds(bat, 1)], raw[:, ch, lo:hi], AX.X, ALU.add).then_inc(csum_done, 1)
                    elif k == "mx":
                        ge(dve, sc_full["mx"], nth(step, i))
                        if u == 0:
                            ge(dve, nm_done, nth(("mt", b, h, 0), i) * 3 - 3)
                        nc.vector.tensor_reduce(mx[:, u // 2, 2 * (u % 2):2 * (u % 2) + 2],
                                                SC[bank(order, ("mx", "st"), n, i)][:, :, 0:MXN], AX.X, ALU.max).then_inc(mx_done, 1)
                        if u == 7:
                            n0 = nth(("mt", b, h, 0), i)
                            dve.wait_ge(mx_done, nth(step, i))
                            nc.vector.tensor_reduce(nmx[:], mx[:], AX.X, ALU.max, negate=True).then_inc(nm_done, 1)
                            ge(dve, mt_full, n0 - 1)
                            dve.wait_ge(nm_done, n0 * 3 - 2)
                            nc.vector.tensor_copy(nm[:, :, 0], nmx[:]).then_inc(nm_done, 1)
                            dve.wait_ge(nm_done, n0 * 3 - 1)
                            nc.vector.tensor_tensor(nm[:, :, 1], nmx[:], nm[:, :, 0].bitcast(f32), ALU.subtract).then_inc(nm_done, 1)
                    elif k == "mt":
                        ge(dve, mt_full, nth(step, i))
                        nc.vector.tensor_copy(QS[b % 2][96:98, 4 * h:4 * h + 4, :],
                                              OP[h][96:98].rearrange("p (a n) -> p a n", a=4)).then_inc(mrow, 1)
                    elif k == "Q":
                        ge(dve, full["Q"], nth(step, z(i)))
                        qs = slice(4 * u, 4 * u + 4)
                        q0 = nth(step, z(i))
                        ge(dve, free["Q"], q0 - 1)
                        nc.vector.tensor_tensor(qtmp[:], PJ[bank(order, RING, n, i)][0:96].rearrange("p (a n) -> p a n", a=4),
                                                bq96[:, qs].unsqueeze(2).to_broadcast([96, 4, P]), ALU.add).then_inc(qch, 1)
                        dve.wait_ge(qch, q0 * 2 - 1)
                        if i is not None:
                            ge(dve, q_in, (i + 1) * 4)
                        nc.vector.tensor_copy(Q96[:, qs], qtmp[:]).then_inc(qch, 1)
                        dve.wait_ge(qch, q0 * 2)
                        nc.vector.tensor_tensor(Q96[64:96, qs], qtmp[64:96], Q96[64:96, qs].bitcast(f32), ALU.subtract).then_inc(free["Q"], 1)
                    elif k == "E":
                        ge(dve, full["E"], nth(step, i))
                        ge(dve, on_done, nth(step, i) - 1)
                        nc.vector.reciprocal(rec[:], PJ[bank(order, RING, n, i)][:, 0:4 * S].rearrange("p (a n) -> p a n", a=4)).then_inc(rec_done, 1)
                    elif k == "W":
                        ge(dve, full["W"], nth(step, i))
                        dve.wait_ge(bo_added, T)
                        xs = X[:, bass.ds(i + b // 2, 1), u * P:(u + 1) * P].rearrange("p a n -> p (a n)")
                        nc.vector.tensor_tensor(xs, xs, PJ[bank(order, RING, n, i)][:, 0:P], ALU.add).then_inc(free["W"], 1)
                        if u == 1:
                            ge(dve, free["W"], nth(step, i))
                            tile_ = bass.ds(i + b // 2, 1)
                            nc.vector.bn_stats(stats[:, tile_, :].rearrange("p a n -> p (a n)"),
                                               X[:, tile_, :].rearrange("p a n -> p (a n)")).then_inc(stats_done, 1)
                    elif k == "pv" and u == 6:
                        ge(dve, pv_done, nth(step, i))
                        ge(dve, on_done, nth(("E", b, 0, 0), i) - 1)
                        nc.vector.tensor_copy(o_sb[:, 2 * h:2 * h + 2], OP[h][:, 0:2 * S].rearrange("p (a n) -> p a n", a=2)).then_inc(o_ev, 1)

            walk(steps, dve)

        @block.tensor
        def _(pe):
            mm = nc.tensor.matmul
            pe.wait_ge(w_split, 4)
            pe.wait_ge(w_in, 16 * 6)

            def split_product(out, lh, rh):
                terms = [(a, b_) for a, b_ in zip(lh, rh)]
                todo = []
                for l, r in terms:
                    todo += [(l[0], r[0]), (l[0], r[1]), (l[1], r[0])]
                for n_, (l, r) in enumerate(todo):
                    last = mm(out, l, r, start=n_ == 0, stop=n_ == len(todo) - 1)
                return last

            def steps(order, i):
                for n, step in enumerate(order):
                    k, b, h, u = step
                    if k in RING:
                        before = ring_before(order, RING, n, i)
                        if before:
                            (bk_, j) = before
                            ge(pe, free_of(bk_[0]), nth(bk_, j))
                        dst = PJ[bank(order, RING, n, i)]
                    if k == "K":
                        lo, hi = KCOLS[u]
                        if u in (0, 2) and h == 0:
                            ge(pe, hi_done, nth(("cv", b, 0, u // 2), z(i)) * 2)
                            ge(pe, lo_done, nth(("cv", b, 0, u // 2), z(i)))
                        hs = slice(h * P, (h + 1) * P)
                        split_product(dst[:, 0:hi - lo], [(wk[0][:, ch, hs], wk[1][:, ch, hs]) for ch in range(CH)],
                                      [(ctx_hi[:, ch, lo:hi], ctx_lo[:, ch, lo:hi]) for ch in range(CH)]).then_inc(full["K"], 1)
                    elif k == "V":
                        for kk in range(2 if u < 6 else 1):
                            kt = 2 * u + kk
                            rows = P if kt < KT - 1 else KLAST
                            cs = slice(kt * P, kt * P + rows)
                            last = split_product(dst[0:rows, kk * D:(kk + 1) * D], [(ctx_hi[:, ch, cs], ctx_lo[:, ch, cs]) for ch in range(CH)],
                                                 [(wv[0][:, ch, :], wv[1][:, ch, :]) for ch in range(CH)])
                        last.then_inc(full["V"], 1)
                    elif k == "Q":
                        for a in range(4):
                            for ch in range(CH):
                                tok = bass.ds(0, P) if i is None else bass.ds((i + 1) * P, P)
                                last = mm(dst[0:96, a * P:(a + 1) * P], wq96[:, ch, 4 * u + a], lnT[:, ch, tok], start=ch == 0, stop=ch == CH - 1)
                        last.then_inc(full["Q"], 1)
                    elif k == "E":
                        ge(pe, o_ev, nth(step, i) * 2)
                        mm(dst[:, 0:4 * S], c["spread"][:], o_sb[:].rearrange("p a n -> p (a n)"), start=True, stop=True).then_inc(full["E"], 1)
                    elif k == "W":
                        if u == 0:
                            ge(pe, on_done, nth(("E", b + 1, 0, 0), i))
                        for q in range(4):
                            last = mm(dst[:, 0:P], oN[:, q], wo[:, q, u * P:(u + 1) * P], start=q == 0, stop=q == 3)
                        last.then_inc(full["W"], 1)
                    elif k == "mx":
                        wait_slot(order, n, i)
                        if u == 0:
                            ge(pe, kst_in[h], nth(("E", b, 0, 0), i) * (16 * DMAS_KST))
                            if h == 0:
                                ge(pe, q_in, nth(("E", b, 0, 0), i) * 2)
                        pr = 4 * h + u // 2
                        for kk in range(2):
                            lo = MXCOLS[2 * (u % 2) + kk]
                            last = mm(SC[bank(order, ("mx", "st"), n, i)][:, kk, 0:MXN], QS[b % 2][0:96, pr, :], KS[0:96, pr, lo:lo + MXN], start=True, stop=True)
                        last.then_inc(sc_full["mx"], 1)
                    elif k == "mt":
                        ge(pe, nm_done, nth(step, i) * 3)
                        ge(pe, o_ev, nth(step, i) - 2)
                        for a in range(4):
                            last = mm(OP[h][96:98, a * P:(a + 1) * P], nm[:, a, :].bitcast(f32), c["ident"][:], start=True, stop=True, tile_position=(0, 96))
                        last.then_inc(mt_full, 1)
                    elif k == "st":
                        wait_slot(order, n, i)
                        pe.wait_ge(E["ones"], 2)
                        if u == 0:
                            ge(pe, mrow, nth(("mt", b, h, 0), i))
                        for kk in range(2 if u < 6 else 1):
                            kt = 2 * u + kk
                            rows = P if kt < KT - 1 else KLAST
                            for a in range(4):
                                last = mm(SC[bank(order, ("mx", "st"), n, i)][0:rows, kk, a * P:(a + 1) * P],
                                          KS[:, 4 * h + a, kt * P:kt * P + rows], QS[b % 2][:, 4 * h + a, :], start=True, stop=True)
                        last.then_inc(sc_full["st"], 1)
                    elif k == "pv":
                        ge(pe, ex_done, nth(("st", b, h, u), i))
                        for kk in range(2 if u < 6 else 1):
                            kt = 2 * u + kk
                            rows = P if kt < KT - 1 else KLAST
                            for a in range(2):
                                for j in range(4):
                                    hd = 8 * h + 4 * a + j
                                    last = mm(OP[h][32 * j:32 * j + 32, a * S:(a + 1) * S],
                                              V[b % 2][0:rows, kt, hd * VW:hd * VW + 32],
                                              PT[ptslot(("st", b, h, u))][0:rows, kk, (4 * a + j) * S:(4 * a + j + 1) * S],
                                              start=kt == 0 and a == 0, stop=kt == KT - 1, tile_position=(0, 32 * j), skip_group_check=True)
                        last.then_inc(pv_done, 1)

            def free_of(kind):
                return free[kind] if kind != "E" else rec_done

            def wait_slot(order, n, i):
                before = ring_before(order, ("mx", "st"), n, i)
                if isinstance(i, int) and i == 0 and sum(x[0] in ("mx", "st") for x in order[:n]) < 2:
                    return
                (x, j) = before
                ge(pe, mx_done if x[0] == "mx" else ex_done, nth(x, j))

            walk(steps, pe)


def stage_weights(nc, ctx, tag, sources, **shapes):
    W = {n: ctx.enter_context(nc.sbuf_tensor(f"{tag}_w_{n}", s, f32)) for n, s in shapes.items()}
    w_in = ctx.enter_context(nc.semaphore(f"{tag}_w_in"))
    return W, w_in, [(W[n][:], sources[n], w_in) for n in shapes]


LN_SEMS = ("stat", "var", "std", "norm", "tr", "ev_dve", "ev_act")


def layer_norm(nc, k, sems, X, stats, lnT, c, loads=(), also={}):
    ctx = ExitStack()
    with ctx:
        sb = lambda n, s, d=f32: ctx.enter_context(nc.sbuf_tensor(f"ln{k}_{n}", s, d))
        stat, var_done, std_done, norm, tr, ev_dve, ev_act = [sems[n] for n in LN_SEMS]
        s0, n0, t0 = k * (T + 1) + (T if k else 0), k * T, 4 * k
        a0 = s0 + (0 if k else T)
        mv = sb("mv", [P, T, 2])
        var, std, rstd = sb("var", [P, T]), sb("std", [P, T]), sb("rstd", [P, T])
        y = sb("y", [P, T, D])
        PS = [ctx.enter_context(nc.psum_tensor(f"ln{k}_ps{j}", [P, 512], f32)) for j in range(4)]
        block = ctx.enter_context(nc.Block())

        @block.sync
        def _(sp):
            for dst, src, counted in loads:
                sp.dma_start(dst, src).then_inc(counted, 16)

        @block.vector
        def _(dve):
            if k == 0:
                for t in range(T):
                    nc.vector.bn_stats(stats[:, t], X[:, t]).then_inc(stat, 1)
            for t in range(T):
                if k == 0:
                    dve.wait_ge(stat, s0 + t + 1)
                nc.vector.bn_aggr(mv[:, t], stats[:, t]).then_inc(stat, 1)
            dve.wait_ge(stat, a0 + T)
            nc.vector.tensor_scalar(var[:], mv[:, :, 1], 1e-5, None, ALU.add).then_inc(var_done, 1)
            dve.wait_ge(std_done, k + 1)
            nc.vector.reciprocal(rstd[:], std[:]).then_inc(stat, 1)
            dve.wait_ge(stat, a0 + T + 1)
            for t in range(T):
                nc.vector.tensor_scalar(y[:, t], X[:, t], mv[:, t, 0:1], rstd[:, t:t + 1], ALU.subtract, ALU.mult).then_inc(norm, 1)
            for g in (1, 3):
                dve.wait_ge(tr, t0 + g + 1)
                nc.vector.tensor_copy(lnT[:, g % 2, (g // 2) * 512:(g // 2) * 512 + 512], PS[g][:]).then_inc(ev_dve, 1)

        @block.scalar
        def _(act):
            act.wait_ge(var_done, k + 1)
            nc.scalar.activation(std[:], var[:], ACT.Sqrt).then_inc(std_done, 1)
            if "act" in also:
                also["act"](act)
            for g in (0, 2):
                act.wait_ge(tr, t0 + g + 1)
                nc.scalar.activation(lnT[:, g % 2, (g // 2) * 512:(g // 2) * 512 + 512], PS[g][:], ACT.Copy).then_inc(ev_act, 1)

        @block.tensor
        def _(pe):
            for g in range(4):
                for a in range(4):
                    t = 4 * (g // 2) + a
                    pe.wait_ge(norm, n0 + t + 1)
                    last = nc.tensor.transpose(PS[g][:, a * P:(a + 1) * P], y[:, t, (g % 2) * P:(g % 2 + 1) * P], c["ident"])
                last.then_inc(tr, 1)

        @block.gpsimd
        def _(pool):
            if "pool" in also:
                also["pool"](pool)


def bias_row(nc, ctx, tag, source):
    row, row_in = ctx.enter_context(nc.sbuf_tensor(f"{tag}_brow", [P, D], f32)), ctx.enter_context(nc.semaphore(f"{tag}_row_in"))
    return row, row_in, [(row[:], source.rearrange("(a n) -> a n", a=1).to_broadcast([P, D]), row_in)]


def add_bias(nc, pool, X, row, row_in, added):
    pool.wait_ge(row_in, 16)
    for t in range(T):
        nc.gpsimd.tensor_tensor(X[:, t], X[:, t], row[:], ALU.add).then_inc(added, 1)


def self_attention(nc, tag, X, stats, lnT, c, W, w_in, bias, heads, dk, dv, mask, rope=False, conv_bias=None, loads=()):
    NCH = heads * dk // P
    HC = P // dk
    NP = heads // 2
    VW2 = 2 * (dv + 1)
    ctx = ExitStack()
    with ctx:
        sb = lambda n, s, d=f32: ctx.enter_context(nc.sbuf_tensor(f"{tag}_{n}", s, d))
        sem = lambda n: ctx.enter_context(nc.semaphore(f"{tag}_{n}"))
        names = ["q", "k"] + (["qr", "kr"] if rope else [])
        lnH, lnL = sb("lnH", [P, CH, T * P], f32r), sb("lnL", [P, CH, T * P], f32r)
        WH, WL = [{n: sb(f"{x}_{n}", [P, CH, heads * dk], f32r) for n in names} for x in ("wh", "wl")]
        QT, KTt = sb("QT", [P, NCH, T * P]), sb("KT", [P, NCH, T * P])
        rot = sb("rot", [P, 512])
        Vd = sb("Vd", [P, B, NP, 2, dv + 1])
        Vt = [sb(f"Vt{j}", [P, 2, NP * VW2]) for j in range(2)]
        Qt = [sb(f"Qt{j}", [P, NCH, P]) for j in range(2)]
        Km = [sb(f"Km{j}", [P, NCH, 2, HC, S]) for j in range(2)]
        Sc, Pr = sb("Sc", [P, heads, S]), sb("Pr", [P, heads, S])
        PT = sb("PT", [P, NP, P])
        mxt, rs = sb("mx", [P, heads]), sb("rs", [P, heads])
        oN, oT = sb("oN", [P, heads, dv]), sb("oT", [P, 2, P])
        bank = lambda n, k=1: ctx.enter_context(nc.psum_tensor(f"{tag}_{n}", [P, k, 512], f32))
        SC = ctx.enter_context(nc.psum_tensor(f"{tag}_SC", [P, heads, S], f32))
        TP = ctx.enter_context(nc.psum_tensor(f"{tag}_TP", [P, NP, P], f32))
        OV, WP = bank("OV", 2), bank("WP")
        PJ = [OV[:, 0], OV[:, 1]]
        outs = OV[:, 0, 0:NP * VW2].rearrange("p (h v) -> p h v", v=dv + 1)
        ln_hi, ln_lo, w_hi, w_lo = sem("ln_hi"), sem("ln_lo"), sem("w_hi"), sem("w_lo")
        cb_in, pj, pj_free, rot_done = [sem(x) for x in ("cb_in", "pj", "pj_free", "rot")]
        ones = [sem(f"ones{e}") for e in range(2)]
        bias_added, stats_done = sem("bias_added"), sem("stats")
        q_in, km_pool, km_act, v_in = sem("q_in"), sem("km_pool"), sem("km_act"), sem("v_in")
        s_full, t_full, o_full, ot_full, y_full = [sem(x) for x in ("s_full", "t_full", "o_full", "ot_full", "y_full")]
        bias_done, mx_done, sub_done, exp_done = [sem(x) for x in ("bias", "mx", "sub", "exp")]
        t_ev, rcp_done, norm_done, ot_ev, y_ev = [sem(x) for x in ("t_ev", "rcp", "norm", "ot_ev", "y_ev")]
        if conv_bias is not None:
            conv, scratch = conv_bias
            ext = sb("ext", [heads, 2 * S - 1])
            CB = sb("CB", [P, heads, S])
            ext_done, ext_out = sem("ext_done"), sem("ext_out")
            NPOS = conv.shape[1]
            E0 = S - 1 - NPOS // 2
        turned = ("", "r") if rope else ("",)
        order = [(n + r, ch, g) for g in range(2) for n in "qk" for ch in range(NCH) for r in turned]
        split_order = ["q", "qr", "k", "kr"] if rope else ["q", "k"]
        nproj = len(order)
        KMP = (HC - HC // 4) * NCH
        EA = HC // 4
        block = ctx.enter_context(nc.Block())

        def over_tiles(eng, step, before, after):
            before()
            for t in range(2):
                step(t, t, t > 0, True)
            with eng.Fori(1, T // 2 - 1) as i:
                for j in range(2):
                    step(i * 2 + j, j, True, True)
            for t in range(T - 2, T):
                step(t, t % 2, True, t < T - 1)
            after()

        def projected(eng, half):
            eng.wait_ge(pj_free, T + half * (nproj // 2))
            if rope:
                eng.wait_ge(rot_done, half * (nproj // 4))

        def zeros_and_ones(eng, e):
            rows_ = slice(e * S, (e + 1) * S)
            eng.memset(Vd[rows_, :, :, 1 - e, :], 0.0).then_inc(ones[e], 1)
            eng.memset(Vd[rows_, :, :, e, dv], 1.0).then_inc(ones[e], 1)

        @block.sync
        def _(sp):
            if conv_bias is not None:
                sp.dma_start(ext[:, E0:E0 + NPOS], conv).then_inc(cb_in, 16)
                sp.wait_ge(ext_done, 2)
                L = 2 * S - 1
                sp.dma_start(scratch.rearrange("h (r l) -> h r l", l=L), ext[:].unsqueeze(1).to_broadcast([heads, S, L])).then_inc(ext_out, 16)
                sp.wait_ge(ext_out, 16)
                for b in range(2):
                    src = scratch[:, S - 1:S - 1 + S * (L - 1)].rearrange("h (r l) -> r h l", l=L - 1)[:, :, 0:S]
                    sp.dma_start(CB[b * S:(b + 1) * S], src).then_inc(cb_in, 16)
            for dst, src, counted in loads:
                sp.dma_start(dst, src).then_inc(counted, 16)

        @block.tensor
        def _(pe):
            mm = nc.tensor.matmul
            pe.wait_ge(w_in, 16 * (len(names) + 2))
            for n in range(T):
                ge(pe, pj_free, n - 1)
                for b in range(2):
                    for e in range(2):
                        for k in range(CH):
                            tok = n * P + b * S
                            last = mm(PJ[n % 2][e * S:(e + 1) * S, b * P:(b + 1) * P], lnT[:, k, tok:tok + S], W["v"][:, k, e, :],
                                      start=k == 0, stop=k == CH - 1, tile_position=(0, e * S))
                last.then_inc(pj, 1)
            pe.wait_ge(ln_lo, CH)
            for m, (name, ch, g) in enumerate(order):
                n = T + m
                pe.wait_ge(pj_free, n - 1)
                pe.wait_ge(w_lo, split_order.index(name) + 1)
                cs, ts = slice(ch * P, (ch + 1) * P), slice(g * 512, (g + 1) * 512)
                todo = [x for k in range(CH) for x in ((WH[name][:, k, cs], lnH[:, k, ts]), (WH[name][:, k, cs], lnL[:, k, ts]),
                                                       (WL[name][:, k, cs], lnH[:, k, ts]))]
                for x, (l, r_) in enumerate(todo):
                    last = mm(PJ[n % 2], l, r_, start=x == 0, stop=x == len(todo) - 1)
                last.then_inc(pj, 1)

            def scores(t, j):
                pe.wait_ge(q_in, t + 1)
                if EA:
                    pe.wait_ge(km_act, t * EA + EA)
                ge(pe, sub_done if conv_bias is None else bias_done, t)
                pe.wait_ge(km_pool, t * KMP + KMP)
                for ch in range(NCH):
                    for b in range(2):
                        last = mm(SC[b * S:(b + 1) * S, ch * HC:(ch + 1) * HC, :].rearrange("p h s -> p (h s)"), Qt[j][:, ch, b * S:(b + 1) * S],
                                  Km[j][:, ch, b].rearrange("p e s -> p (e s)"), start=True, stop=True, tile_position=(0, b * S))
                last.then_inc(s_full, 1)

            def turn(t):
                ge(pe, t_ev, t)
                pe.wait_ge(exp_done, t + 1)
                for pr in range(NP):
                    last = nc.tensor.transpose(TP[:, pr, :], Pr[:, 2 * pr:2 * pr + 2].rearrange("p e s -> p (e s)"), c["ident"])
                last.then_inc(t_full, 1)

            def weigh(t, j):
                ge(pe, norm_done, t)
                pe.wait_ge(v_in, t + 1)
                pe.wait_ge(t_ev, t + 1)
                for pr in range(NP):
                    for b in range(2):
                        last = mm(outs[b * S:(b + 1) * S, 2 * pr:2 * pr + 2].rearrange("p h v -> p (h v)"), PT[:, pr, b * S:(b + 1) * S],
                                  Vt[j][:, b, pr * VW2:(pr + 1) * VW2],
                                  start=True, stop=True, tile_position=(0, b * S))
                last.then_inc(o_full, 1)

            def turn_out(t):
                ge(pe, ot_ev, t)
                pe.wait_ge(norm_done, t + 1)
                for k in range(2):
                    last = nc.tensor.transpose(OV[:, 1, k * P:(k + 1) * P], oN[:].rearrange("p h d -> p (h d)")[:, k * P:(k + 1) * P], c["ident"])
                last.then_inc(ot_full, 1)

            def project(t):
                ge(pe, y_ev, t)
                pe.wait_ge(ot_ev, t + 1)
                for k in range(2):
                    last = mm(WP[:, 0, 0:D], oT[:, k, :], W["o"][:, k, :], start=k == 0, stop=k == 1)
                last.then_inc(y_full, 1)

            def step(t, j, behind, ahead):
                turn(t)
                if behind:
                    turn_out(t - 1)
                if ahead:
                    scores(t + 1, 1 - j)
                weigh(t, j)
                if behind:
                    project(t - 1)

            def before():
                pe.wait_ge(pj_free, nproj + T)
                scores(0, 0)

            def after():
                turn_out(T - 1)
                project(T - 1)

            over_tiles(pe, step, before, after)

        @block.gpsimd
        def _(pool):
            zeros_and_ones(nc.gpsimd, 0)
            pool.wait_ge(ones[0], 2)
            for m, name in enumerate(split_order):
                pool.wait_ge(w_hi, m + 1)
                nc.gpsimd.tensor_tensor(WL[name][:], W[name][:], WH[name][:].bitcast(f32), ALU.subtract).then_inc(w_lo, 1)
            add_bias(nc, pool, X, *bias, bias_added)

            def place(t, j):
                tok = bass.ds(t * P, P)
                ge(pool, s_full, t - 1)
                nc.gpsimd.tensor_copy(Qt[j][:], QT[:, :, tok]).then_inc(q_in, 1)
                for e in range(EA, HC):
                    for ch in range(NCH):
                        nc.gpsimd.tensor_tensor(Km[j][:, ch, :, e, :], KTt[:, ch, tok].rearrange("p (b s) -> p b s", b=2),
                                                mask[:, e:e + 1].unsqueeze(1).to_broadcast([P, 2, S]),
                                                ALU.mult).then_inc(km_pool, 1)

            projected(pool, 1)
            for t in range(2):
                place(t, t)
            projected(pool, 2)
            with pool.Fori(1, T // 2) as i:
                for j in range(2):
                    place(i * 2 + j, j)

        @block.vector
        def _(dve):
            if conv_bias is not None:
                dve.wait_ge(cb_in, 16)
                nc.vector.tensor_copy(ext[:, 0:E0], ext[:, E0:E0 + 1].to_broadcast([heads, E0])).then_inc(ext_done, 1)
                nc.vector.tensor_copy(ext[:, E0 + NPOS:], ext[:, E0 + NPOS - 1:E0 + NPOS].to_broadcast([heads, E0])).then_inc(ext_done, 1)
            zeros_and_ones(nc.vector, 1)
            for e in range(2):
                dve.wait_ge(ones[e], 2)
            for n in range(T):
                dve.wait_ge(pj, n + 1)
                for e in range(2):
                    r_ = slice(e * S, (e + 1) * S)
                    last = nc.vector.tensor_copy(Vd[r_, 2 * n:2 * n + 2, :, e, 0:dv],
                                                 PJ[n % 2][r_, 0:D].rearrange("p (b a v) -> p b a v", b=2, v=dv))
                last.then_inc(pj_free, 1)
                if n % 2 and n // 2 < CH:
                    k = n // 2
                    dve.wait_ge(ln_hi, k + 1)
                    nc.vector.tensor_tensor(lnL[:, k], lnT[:, k], lnH[:, k].bitcast(f32), ALU.subtract).then_inc(ln_lo, 1)
            turns = 0
            for m, (name, ch, g) in enumerate(order):
                n = T + m
                dst = (QT if name[0] == "q" else KTt)[:, ch, g * 512:(g + 1) * 512]
                dve.wait_ge(pj, n + 1)
                if not rope:
                    nc.vector.tensor_copy(dst, PJ[n % 2]).then_inc(pj_free, 1)
                    continue
                wide = lambda a: a.rearrange("p (b s) -> p b s", s=S)
                table = c["sin" if name[1:] else "cos"].unsqueeze(1).to_broadcast([P, 512 // S, S])
                if not name[1:]:
                    nc.vector.tensor_tensor(wide(dst), wide(PJ[n % 2]), table, ALU.mult).then_inc(pj_free, 1)
                else:
                    ge(dve, rot_done, turns)
                    nc.vector.tensor_tensor(wide(rot[:]), wide(PJ[n % 2]), table, ALU.mult).then_inc(pj_free, 1)
                    dve.wait_ge(pj_free, n + 1)
                    nc.vector.tensor_tensor(dst, dst, rot[:], ALU.add).then_inc(rot_done, 1)
                    turns += 1
            if conv_bias is not None:
                dve.wait_ge(cb_in, 16 * 3)
            def less_max(t):
                dve.wait_ge(s_full, t + 1)
                ge(dve, exp_done, t)
                src = SC
                if conv_bias is not None:
                    nc.vector.scalar_tensor_tensor(Sc[:], SC[:], float(dk) ** -0.5, CB[:], ALU.mult, ALU.add).then_inc(bias_done, 1)
                    dve.wait_ge(bias_done, t + 1)
                    src = Sc
                nc.vector.tensor_reduce(mxt[:], src[:], AX.X, ALU.max).then_inc(mx_done, 1)
                dve.wait_ge(mx_done, t + 1)
                nc.vector.tensor_tensor(Sc[:], src[:], mxt[:].unsqueeze(2).to_broadcast([P, heads, S]), ALU.subtract).then_inc(sub_done, 1)

            def normalise(t):
                dve.wait_ge(o_full, t + 1)
                ge(dve, norm_done, t)
                ge(dve, ot_full, t)
                nc.vector.reciprocal(rs[:], outs[:, :, dv]).then_inc(rcp_done, 1)
                dve.wait_ge(rcp_done, t + 1)
                nc.vector.tensor_tensor(oN[:], outs[:, :, 0:dv], rs[:].unsqueeze(2).to_broadcast([P, heads, dv]), ALU.mult).then_inc(norm_done, 1)

            def add(t):
                dve.wait_ge(bias_added, T)
                dve.wait_ge(y_full, t + 1)
                xs = X[:, bass.ds(t, 1), :].rearrange("p a n -> p (a n)")
                nc.vector.tensor_tensor(xs, xs, WP[:, 0, 0:D], ALU.add).then_inc(y_ev, 1)
                dve.wait_ge(y_ev, t + 1)
                nc.vector.bn_stats(stats[:, bass.ds(t, 1), :].rearrange("p a n -> p (a n)"), xs).then_inc(stats_done, 1)

            def step(t, j, behind, ahead):
                if ahead:
                    less_max(t + 1)
                normalise(t)
                if behind:
                    add(t - 1)

            over_tiles(dve, step, lambda: less_max(0), lambda: add(T - 1))

        @block.scalar
        def _(act):
            def place(t, j):
                ge(act, o_full, t - 1)
                nc.scalar.activation(Vt[j][:], Vd[:, bass.ds(t * 2, 2)].rearrange("p b a e v -> p b (a e v)"), ACT.Copy).then_inc(v_in, 1)
                for e in range(EA):
                    nc.scalar.activation(Km[j][:, :, :, e, :], KTt[:, :, bass.ds(t * P, P)].rearrange("p c (b s) -> p c b s", b=2),
                                         ACT.Copy, scale=mask[:, e:e + 1]).then_inc(km_act, 1)

            def exps(t):
                act.wait_ge(sub_done, t + 1)
                ge(act, t_full, t)
                nc.scalar.activation(Pr[:], Sc[:], ACT.Exp, scale=float(dk) ** -0.5 if conv_bias is None else 1.0).then_inc(exp_done, 1)

            def turned_in(t):
                act.wait_ge(t_full, t + 1)
                ge(act, o_full, t)
                nc.scalar.activation(PT[:], TP[:], ACT.Copy).then_inc(t_ev, 1)

            def turned_out(t):
                act.wait_ge(ot_full, t + 1)
                ge(act, y_full, t)
                nc.scalar.activation(oT[:], OV[:, 1, 0:2 * P].rearrange("p (k n) -> p k n", k=2), ACT.Copy).then_inc(ot_ev, 1)

            def step(t, j, behind, ahead):
                turned_in(t)
                if behind:
                    turned_out(t - 1)
                if ahead:
                    exps(t + 1)
                    if not (isinstance(t, int) and t == T - 2):
                        place(t + 2, j)

            for k in range(CH):
                nc.scalar.activation(lnH[:, k], lnT[:, k], ACT.Copy).then_inc(ln_hi, 1)
            act.wait_ge(w_in, 16 * (len(names) + 2))
            for name in split_order:
                nc.scalar.activation(WH[name][:], W[name][:], ACT.Copy).then_inc(w_hi, 1)

            def before():
                projected(act, 1)
                for t in range(2):
                    place(t, t)
                projected(act, 2)
                exps(0)

            over_tiles(act, step, before, lambda: turned_out(T - 1))


FE = 352
NE = 8
NX = NE + 2
TOPK = 2
ROUTED_SCALE = 2.5
FCH = [(0, P), (P, 2 * P), (2 * P, FE)]


def expert_buffers(nc, ctx, w):
    sb = lambda n, s: [ctx.enter_context(nc.sbuf_tensor(f"moe_{n}{j}", s, f32)) for j in range(2)]
    sem = lambda n: ctx.enter_context(nc.semaphore("moe_" + n))
    gate, gate_in = ctx.enter_context(nc.sbuf_tensor("moe_gate", [P, CH, NE], f32)), sem("gate_in")
    gu, dn = sb("gu_raw", [P, CH, 2, FE]), sb("dn_raw", [P, 3, D])
    gu_in, dn_in = [[sem(f"{n}{j}") for j in range(2)] for n in ("gu_in", "dn_in")]
    loads = [(gate[:], w["gate"], gate_in)]
    loads += [(gu[j][:], w["gu"][j], gu_in[j]) for j in range(2)] + [(dn[j][:], w["down"][j], dn_in[j]) for j in range(2)]
    return (gate, gate_in, gu, dn, gu_in, dn_in), loads


def experts(nc, tag, X, stats, lnT, c, w, buffers):
    ctx = ExitStack()
    with ctx:
        sb = lambda n, s, d=f32: ctx.enter_context(nc.sbuf_tensor(f"{tag}_{n}", s, d))
        sem = lambda n: ctx.enter_context(nc.semaphore(f"{tag}_{n}"))
        gate, gate_in, gu_raw, dn_raw, gu_in, dn_in = buffers
        lg, sc8, pk, t8 = [sb(n, [P, T, NE]) for n in ("lg", "sc8", "pk", "t8")]
        g1, g2 = sb("g1", [P, T * NE, NE]), sb("g2", [P, T * NE, NE])
        m8, s8 = sb("m8", [P, T]), sb("s8", [P, T])
        comb = sb("comb", [P, T, NX])
        gu = [[sb(f"gu{j}{k}", [P, CH, 2, FE], f32r) for k in range(2)] for j in range(2)]
        dn = [[sb(f"dn{j}{k}", [P, 3, D], f32r) for k in range(2)] for j in range(2)]
        h = [[sb(f"h{j}{k}", [P, 3, T * P], f32r) for k in range(2)] for j in range(2)]
        sg = [sb(f"sg{j}", [P, 512]) for j in range(2)]
        h32 = [sb(f"h32{j}", [P, 512]) for j in range(2)]
        GU = [ctx.enter_context(nc.psum_tensor(f"{tag}_GU{j}", [P, 2, 512], f32)) for j in range(2)]
        DN = [ctx.enter_context(nc.psum_tensor(f"{tag}_DN{j}", [P, 2, D], f32)) for j in range(2)]
        LG = ctx.enter_context(nc.psum_tensor(f"{tag}_LG", [P, T, NE], f32))
        lnH, lnL = sb("lnH", [P, CH, T * P], f32r), sb("lnL", [P, CH, T * P], f32r)
        ln_hi, ln_lo, stats_done = sem("ln_hi"), sem("ln_lo"), sem("stats")
        lg_full, r, rexp = sem("lg_full"), sem("r"), sem("rexp")
        gu_hi, gu_lo, dn_hi, dn_lo = sem("gu_hi"), sem("gu_lo"), sem("dn_hi"), sem("dn_lo")
        gu_full, silu_done, mul_done, hhi_done, hlo_done = [sem(x) for x in ("gu_full", "silu", "mul", "hhi", "hlo")]
        dn_full, dn_read = sem("dn_full"), sem("dn_read")
        UN = [(f, g) for f in range(3) for g in range(2)]
        NU, ND = len(UN), T // 2
        block = ctx.enter_context(nc.Block())

        def over_experts(eng, ahead, behind):
            def two(i):
                ahead(i * 2 + 1, 1)
                behind(i * 2, 0)
                ahead(i * 2 + 2, 0)
                behind(i * 2 + 1, 1)

            ahead(0, 0)
            two(0)
            with eng.Fori(1, NX // 2 - 1) as i:
                two(i)
            ahead(NX - 1, 1)
            behind(NX - 2, 0)
            behind(NX - 1, 1)

        def over_splits(eng, units, split_gu, split_dn, then=lambda: None):
            def two(i, last=False):
                for j in range(2):
                    e = i * 2 + j
                    units(e, j)
                    if not (last and j == 1):
                        split_dn(e + 1, 1 - j)
                    if not last:
                        split_gu(e + 2, j)

            split_gu(0, 0)
            split_gu(1, 1)
            split_dn(0, 0)
            then()
            two(0)
            with eng.Fori(1, NX // 2 - 1) as i:
                two(i)
            two(NX // 2 - 1, last=True)

        @block.sync
        def _(sp):
            def load(e, j):
                ge(sp, gu_lo, e - 1)
                sp.dma_start(gu_raw[j][:], w["gu"][e]).then_inc(gu_in[j], 16)
                ge(sp, dn_lo, e - 1)
                sp.dma_start(dn_raw[j][:], w["down"][e]).then_inc(dn_in[j], 16)

            with sp.Fori(1, NX // 2) as i:
                load(i * 2, 0)
                load(i * 2 + 1, 1)

        @block.tensor
        def _(pe):
            mm = nc.tensor.matmul
            pe.wait_ge(gate_in, 16)
            for t in range(T):
                for k in range(CH):
                    last = mm(LG[:, t, :], lnT[:, k, t * P:(t + 1) * P], gate[:, k, :], start=k == 0, stop=k == CH - 1)
            last.then_inc(lg_full, 1)

            def split_product(out, pairs):
                todo = [x for (lh, ll), (rh, rl) in pairs for x in ((lh, rh), (lh, rl), (ll, rh))]
                for n, (l, r_) in enumerate(todo):
                    last = mm(out, l, r_, start=n == 0, stop=n == len(todo) - 1)
                return last

            def up(e, j):
                pe.wait_ge(gu_lo, e + 1)
                for n, (f, g) in enumerate(UN):
                    lo, hi = FCH[f]
                    ge(pe, mul_done, e * NU + (n - 1))
                    for x in range(2):
                        last = split_product(GU[n % 2][0:hi - lo, x, :], [
                            ((gu[j][0][:, k, x, lo:hi], gu[j][1][:, k, x, lo:hi]),
                             (lnH[:, k, g * 512:(g + 1) * 512], lnL[:, k, g * 512:(g + 1) * 512])) for k in range(CH)])
                    last.then_inc(gu_full, 1)

            def down(e, j):
                pe.wait_ge(hlo_done, e * NU + NU)
                pe.wait_ge(dn_lo, e + 1)
                for n in range(ND):
                    ge(pe, dn_read, e * T + (2 * n - 2))
                    for a in range(2):
                        tok = slice((2 * n + a) * P, (2 * n + a + 1) * P)
                        last = split_product(DN[n % 2][:, a, :], [
                            ((h[j][0][0:hi - lo, f, tok], h[j][1][0:hi - lo, f, tok]), (dn[j][0][0:hi - lo, f, :], dn[j][1][0:hi - lo, f, :]))
                            for f, (lo, hi) in enumerate(FCH)])
                    last.then_inc(dn_full, 1)

            pe.wait_ge(ln_lo, CH)
            over_experts(pe, up, down)

        @block.scalar
        def _(act):
            def split_gu(e, j):
                act.wait_ge(gu_in[j], e * 8 + (16 - 8 * j))
                if not (isinstance(e, int) and e < 2):
                    act.wait_ge(gu_full, e * NU - NU)
                nc.scalar.activation(gu[j][0][:], gu_raw[j][:], ACT.Copy).then_inc(gu_hi, 1)

            def split_dn(e, j):
                act.wait_ge(dn_in[j], e * 8 + (16 - 8 * j))
                if not (isinstance(e, int) and e < 2):
                    act.wait_ge(dn_full, e * ND - ND)
                nc.scalar.activation(dn[j][0][:], dn_raw[j][:], ACT.Copy).then_inc(dn_hi, 1)

            def units(e, j):
                for n, (f, g) in enumerate(UN):
                    lo, hi = FCH[f]
                    act.wait_ge(gu_full, e * NU + (n + 1))
                    ge(act, mul_done, e * NU + (n - 1))
                    nc.scalar.activation(sg[n % 2][0:hi - lo], GU[n % 2][0:hi - lo, 0, :], ACT.Silu).then_inc(silu_done, 1)
                    if n >= 1:
                        hi_part(e, j, n - 1)
                hi_part(e, j, NU - 1)

            def hi_part(e, j, n):
                f, g = UN[n]
                lo, hi = FCH[f]
                act.wait_ge(mul_done, e * NU + (n + 1))
                if n == 0 and not (isinstance(e, int) and e < 2):
                    act.wait_ge(dn_full, e * ND - ND)
                nc.scalar.activation(h[j][0][0:hi - lo, f, g * 512:(g + 1) * 512], h32[n % 2][0:hi - lo], ACT.Copy).then_inc(hhi_done, 1)

            for k in range(CH):
                nc.scalar.activation(lnH[:, k], lnT[:, k], ACT.Copy).then_inc(ln_hi, 1)

            def routing():
                act.wait_ge(r, 2)
                nc.scalar.activation(sc8[:], lg[:], ACT.Exp).then_inc(rexp, 1)

            over_splits(act, units, split_gu, split_dn, routing)

        @block.gpsimd
        def _(pool):
            def lower(e, j, part, raw, hi, lo):
                pool.wait_ge(hi, e + 1)
                nc.gpsimd.tensor_tensor(part[j][1][:], raw[j][:], part[j][0][:].bitcast(f32), ALU.subtract).then_inc(lo, 1)

            def split_gu(e, j):
                lower(e, j, gu, gu_raw, gu_hi, gu_lo)

            def split_dn(e, j):
                lower(e, j, dn, dn_raw, dn_hi, dn_lo)

            def units(e, j):
                for n, (f, g) in enumerate(UN):
                    lo, hi = FCH[f]
                    pool.wait_ge(hhi_done, e * NU + (n + 1))
                    s_ = slice(g * 512, (g + 1) * 512)
                    nc.gpsimd.tensor_tensor(h[j][1][0:hi - lo, f, s_], h32[n % 2][0:hi - lo], h[j][0][0:hi - lo, f, s_].bitcast(f32),
                                            ALU.subtract).then_inc(hlo_done, 1)

            over_splits(pool, units, split_gu, split_dn)

        @block.vector
        def _(dve):
            n_ = [0]

            def step(ins):
                n_[0] += 1
                ins.then_inc(r, 1)
                dve.wait_ge(r, n_[0])

            over8 = lambda a: a.unsqueeze(2).to_broadcast([P, T, NE])
            V = nc.vector
            for k in range(CH):
                dve.wait_ge(ln_hi, k + 1)
                V.tensor_tensor(lnL[:, k], lnT[:, k], lnH[:, k].bitcast(f32), ALU.subtract).then_inc(ln_lo, 1)
            dve.wait_ge(lg_full, 1)
            step(V.tensor_reduce(m8[:], LG[:], AX.X, ALU.max))
            step(V.tensor_tensor(lg[:], LG[:], over8(m8[:]), ALU.subtract))
            dve.wait_ge(rexp, 1)
            step(V.tensor_reduce(s8[:], sc8[:], AX.X, ALU.add))
            step(V.reciprocal(m8[:], s8[:]))
            step(V.tensor_tensor(sc8[:], sc8[:], over8(m8[:]), ALU.mult))
            for t in range(T):
                ts = slice(t * NE, (t + 1) * NE)
                mine = sc8[:, t].unsqueeze(2).to_broadcast([P, NE, NE])
                other = sc8[:, t].unsqueeze(1).to_broadcast([P, NE, NE])
                V.tensor_tensor(g1[:, ts], other, mine, ALU.is_gt).then_inc(r, 1)
                V.tensor_tensor(g2[:, ts], other, mine, ALU.is_equal).then_inc(r, 1)
                n_[0] += 2
            dve.wait_ge(r, n_[0])
            g2v = g2[:].rearrange("p (t e) j -> p t (e j)", t=T)
            step(V.tensor_tensor(g2v, g2v, c["lower"].unsqueeze(1).to_broadcast([P, T, NE * NE]), ALU.mult))
            step(V.tensor_tensor(g1[:], g1[:], g2[:], ALU.add))
            step(V.tensor_reduce(pk[:].rearrange("p t e -> p (t e)"), g1[:], AX.X, ALU.add))
            step(V.tensor_scalar(t8[:], pk[:], float(TOPK), None, ALU.is_lt))
            step(V.tensor_tensor(pk[:], sc8[:], t8[:], ALU.mult))
            step(V.tensor_reduce(s8[:], pk[:], AX.X, ALU.add))
            step(V.tensor_scalar(m8[:], s8[:], 1e-20, None, ALU.add))
            step(V.reciprocal(s8[:], m8[:]))
            step(V.tensor_scalar(m8[:], s8[:], ROUTED_SCALE, None, ALU.mult))
            step(V.tensor_tensor(comb[:, :, 0:NE], pk[:], over8(m8[:]), ALU.mult))
            step(V.memset(comb[:, :, NE:NX], 1.0))

            def units(e, j):
                for n, (f, g) in enumerate(UN):
                    lo, hi = FCH[f]
                    dve.wait_ge(silu_done, e * NU + (n + 1))
                    ge(dve, hlo_done, e * NU + (n - 1))
                    V.tensor_tensor(h32[n % 2][0:hi - lo], sg[n % 2][0:hi - lo], GU[n % 2][0:hi - lo, 1, :], ALU.mult).then_inc(mul_done, 1)

            def add(e, j):
                for n in range(ND):
                    dve.wait_ge(dn_full, e * ND + (n + 1))
                    for a in range(2):
                        t = 2 * n + a
                        ge(dve, dn_read, e * T + (t - T + 1))
                        V.scalar_tensor_tensor(X[:, t], DN[n % 2][:, a, :], comb[:, t, bass.ds(e, 1)], X[:, t], ALU.mult, ALU.add).then_inc(dn_read, 1)
                        if isinstance(e, int) and e == NX - 1:
                            dve.wait_ge(dn_read, e * T + t + 1)
                            V.bn_stats(stats[:, t], X[:, t]).then_inc(stats_done, 1)

            over_experts(dve, units, add)


def context_means(nc, csum, mean, wide, mean_done, wide_done):
    def add_parts(pool):
        nc.gpsimd.tensor_tensor(mean[:], csum[:, :, 0], csum[:, :, 1], ALU.add).then_inc(mean_done, 1)

    def widen(act):
        act.wait_ge(mean_done, 1)
        for k in range(CH):
            nc.scalar.activation(wide[:, k], mean[:, k].unsqueeze(2).to_broadcast([P, B, S]), ACT.Copy, scale=1.0 / NK).then_inc(wide_done, 1)

    return {"pool": add_parts, "act": widen}


def mean_context(nc, tag, X, stats, lnT, W, w_in, bias, wide, wide_done):
    ctx = ExitStack()
    with ctx:
        sem = lambda n: ctx.enter_context(nc.semaphore(f"{tag}_{n}"))
        PS = [ctx.enter_context(nc.psum_tensor(f"{tag}_ps{j}", [P, 512], f32)) for j in range(2)]
        full, read, bias_added, stats_done = [sem(n) for n in ("full", "read", "bias_added", "stats")]
        block = ctx.enter_context(nc.Block())

        @block.gpsimd
        def _(pool):
            add_bias(nc, pool, X, *bias, bias_added)

        @block.tensor
        def _(pe):
            pe.wait_ge(w_in, 32)
            pe.wait_ge(wide_done, CH)
            means = wide[:].rearrange("p c b s -> p c (b s)")
            for t in range(T):
                ge(pe, read, t - 1)
                tok = slice(t * P, (t + 1) * P)
                for n in range(2 * CH):
                    l, r_ = (lnT[:, n, tok], W["w1"][:, n, :]) if n < CH else (means[:, n - CH, tok], W["w2"][:, n - CH, :])
                    last = nc.tensor.matmul(PS[t % 2][:, 0:D], l, r_, start=n == 0, stop=n == 2 * CH - 1)
                last.then_inc(full, 1)

        @block.vector
        def _(dve):
            for t in range(T):
                dve.wait_ge(bias_added, t + 1)
                dve.wait_ge(full, t + 1)
                nc.vector.tensor_tensor(X[:, t], X[:, t], PS[t % 2][:, 0:D], ALU.add).then_inc(read, 1)
                dve.wait_ge(read, t + 1)
                nc.vector.bn_stats(stats[:, t], X[:, t]).then_inc(stats_done, 1)


FG = 1024
NF = FG // P
NG = 3


def group_loads(w, W, t):
    return [(W["w1"][:], w["w1"][t]), (W["w2"][:], w["w2"][t]), (W["b2"][:], w["b2"][t:t + 1, :].to_broadcast([P, D]))]


def grouped_ffn(nc, tag, X, lnT, c, w, W, w_in, out):
    ctx = ExitStack()
    with ctx:
        sb = lambda n, s, d=f32: ctx.enter_context(nc.sbuf_tensor(f"{tag}_{n}", s, d))
        sem = lambda n: ctx.enter_context(nc.semaphore(f"{tag}_{n}"))
        w1, w2, b2 = [[W[j][n] for j in range(NG)] for n in ("w1", "w2", "b2")]
        b1 = sb("b1", [P, T, NF])
        h = [sb(f"h{j}", [P, NF, P]) for j in range(2)]
        xo = [sb(f"xo{j}", [P, D]) for j in range(2)]
        HP = [ctx.enter_context(nc.psum_tensor(f"{tag}_hp{j}", [P, 4, P], f32)) for j in range(4)]
        YP = [ctx.enter_context(nc.psum_tensor(f"{tag}_yp{j}", [P, 512], f32)) for j in range(2)]
        b_in = sem("b_in")
        h_full, h_ev, y_full, y_ev = sem("h_full"), sem("h_ev"), sem("y_full"), sem("y_ev")
        r_done, out_done = sem("r_done"), [sem(f"out_done{j}") for j in range(2)]
        block = ctx.enter_context(nc.Block())

        @block.sync
        def _(sp):
            sp.dma_start(b1[:], w["b1"]).then_inc(b_in, 16)

            for t in range(NG, T):
                sp.wait_ge(y_full, t - NG + 1)
                sp.wait_ge(r_done, t - NG + 1)
                for dst, src in group_loads(w, W[t % NG], t):
                    sp.dma_start(dst, src).then_inc(w_in[t % NG], 16)

        @block.tensor
        def _(pe):
            mm = nc.tensor.matmul

            for t in range(T):
                j, wj = t % 2, t % NG
                pe.wait_ge(w_in[wj], (t // NG + 1) * 48)
                for g in range(2):
                    ge(pe, h_ev, t * 2 + (g - 3))
                    for f in range(4):
                        for k in range(CH):
                            last = mm(HP[2 * j + g][:, f, :], w1[wj][:, k, (4 * g + f) * P:(4 * g + f + 1) * P], lnT[:, k, t * P:(t + 1) * P],
                                      start=k == 0, stop=k == CH - 1)
                    last.then_inc(h_full, 1)
                ge(pe, y_ev, t - 1)
                for g in range(2):
                    pe.wait_ge(h_ev, t * 2 + (g + 1))
                    for f in range(4):
                        last = mm(YP[j][:, 0:D], h[j][:, 4 * g + f, :], w2[wj][:, 4 * g + f, :], start=g + f == 0, stop=g + f == 4)
                last.then_inc(y_full, 1)

        @block.vector
        def _(dve):
            dve.wait_ge(b_in, 16)
            for t in range(T):
                j = t % 2
                for g in range(2):
                    dve.wait_ge(h_full, t * 2 + (g + 1))
                    ge(dve, y_full, t - 1)
                    nc.vector.tensor_tensor(h[j][:, 4 * g:4 * g + 4, :], HP[2 * j + g][:],
                                            b1[:, t, 4 * g:4 * g + 4].unsqueeze(2).to_broadcast([P, 4, P]), ALU.add).then_inc(h_ev, 1)
                dve.wait_ge(y_full, t + 1)
                ge(dve, out_done[j], (t // 2) * 16)
                nc.vector.tensor_tensor(xo[j][:], X[:, t], YP[j][:, 0:D], ALU.add).then_inc(y_ev, 1)
                dve.wait_ge(y_ev, t + 1)
                nc.vector.tensor_tensor(xo[j][:], xo[j][:], b2[t % NG][:], ALU.add).then_inc(r_done, 1)

        @block.scalar
        def _(act):
            for t in range(T):
                act.wait_ge(r_done, t + 1)
                act.dma_start(out[t], xo[t % 2][:]).then_inc(out_done[t % 2], 16)
            for j in range(2):
                act.wait_ge(out_done[j], 16 * (T // 2))


CONST = {"ident": P, "spread": P, "hmask": 2, "cos": S, "sin": S, "lower": NE * NE, "half": 2, "eighth": 8}
H1, DQK1, DV1 = 8, 64, 32


def program(nc, a, out):
    ctx = ExitStack()
    with ctx:
        sb = lambda n, s, d=f32: ctx.enter_context(nc.sbuf_tensor(n, s, d))
        X = sb("X", [P, T, D])
        stats = sb("stats", [P, T, 6])
        lnT = sb("lnT", [P, CH, T * P])
        consts = sb("consts", [P, sum(CONST.values())])
        csum = sb("csum", [P, CH, 2, B])
        first_in = ctx.enter_context(nc.semaphore("first_in"))
        ln = {n: ctx.enter_context(nc.semaphore(f"ln_{n}")) for n in LN_SEMS}
        c, at = {}, 0
        for name, width in CONST.items():
            c[name] = consts[:, at:at + width]
            at += width

        xa_parts = ExitStack()
        E = xattn_buffers(nc, xa_parts)

        with nc.Block() as block:
            @block.sync
            def _(sp):
                sp.dma_start(X[:], a["x"].rearrange("(t p) n -> p t n", p=P)).then_inc(first_in, 16)
                sp.dma_start(consts[:], a["consts"]).then_inc(first_in, 16)
                xattn_loads(sp, E, {k: a["xa_" + k] for k in ("wq", "bq", "wk", "bk", "wv", "bv", "wo", "bo")}, a["ctxT"])
                sp.wait_ge(first_in, 32)

            @block.vector
            def _(dve):
                xattn_ones(nc, nc.vector, E, 0)

            @block.gpsimd
            def _(pool):
                xattn_ones(nc, nc.gpsimd, E, 1)

        layer_norm(nc, 0, ln, X, stats, lnT, c, also={"pool": lambda pool: xattn_fill(nc, pool, E)})
        xattn(nc, X, stats, lnT, c, E, a["ctxT"], csum)
        xa_parts.close()

        later = ctx.enter_context(ExitStack())
        wide = [P, CH, H1 * DQK1]
        W_sb, w_in_sb, loads_sb = stage_weights(nc, later, "sb", {k: a["sb_" + k] for k in ("q", "k", "v", "o")},
                                                q=wide, k=wide, v=[P, CH, 2, P], o=[P, 2, D])
        row_sb, row_in_sb, row_load_sb = bias_row(nc, later, "sb", a["sb_bo"])
        W_mc, w_in_mc, loads_mc = stage_weights(nc, later, "mc", {k: a["mc_" + k] for k in ("w1", "w2")}, w1=[P, CH, D], w2=[P, CH, D])
        row_mc, row_in_mc, row_load_mc = bias_row(nc, later, "mc", a["mc_b"])

        moe_stack = ExitStack()
        moe = {k: a["moe_" + k] for k in ("gate", "gu", "down")}
        expert_parts, expert_loads = expert_buffers(nc, moe_stack, moe)

        with ExitStack() as parts:
            wide = [P, CH, H0 * D0]
            W, w_in, loads = stage_weights(nc, parts, "sa", {k: a["sa_" + k] for k in ("q", "qr", "k", "kr", "v", "o")},
                                           q=wide, qr=wide, k=wide, kr=wide, v=[P, CH, 2, P], o=[P, 2, D])
            row, row_in, row_load = bias_row(nc, parts, "sa", a["sa_bo"])
            layer_norm(nc, 1, ln, X, stats, lnT, c, loads=loads + row_load + expert_loads)
            self_attention(nc, "sa", X, stats, lnT, c, W, w_in, (row, row_in), H0, D0, D0, c["eighth"], rope=True)

        layer_norm(nc, 2, ln, X, stats, lnT, c, loads=loads_mc + row_load_mc + loads_sb + row_load_sb)
        experts(nc, "moe", X, stats, lnT, c, moe, expert_parts)
        moe_stack.close()

        gf_W = [{n: later.enter_context(nc.sbuf_tensor(f"gf_{n}{j}", s_, f32))
                 for n, s_ in (("w1", [P, CH, FG]), ("w2", [P, NF, D]), ("b2", [P, D]))} for j in range(NG)]
        gf_in = [later.enter_context(nc.semaphore(f"gf_w_in{j}")) for j in range(NG)]
        gf_dram = {k: a["gf_" + k] for k in ("w1", "b1", "w2", "b2")}
        gf_loads = [(dst, src, gf_in[t]) for t in range(NG) for dst, src in group_loads(gf_dram, gf_W[t], t)]

        with ExitStack() as parts:
            mean = parts.enter_context(nc.sbuf_tensor("mc_mean", [P, CH, B], f32))
            spread = parts.enter_context(nc.sbuf_tensor("mc_wide", [P, CH, B, S], f32))
            mean_done, wide_done = [parts.enter_context(nc.semaphore(f"mc_{n}_done")) for n in ("mean", "wide")]
            layer_norm(nc, 3, ln, X, stats, lnT, c, also=context_means(nc, csum, mean, spread, mean_done, wide_done))
            mean_context(nc, "mc", X, stats, lnT, W_mc, w_in_mc, (row_mc, row_in_mc), spread, wide_done)

        layer_norm(nc, 4, ln, X, stats, lnT, c)
        scratch = nc.dram_tensor("bias_scratch", (H1, S * (2 * S - 1)), f32, kind="Internal").ap()
        self_attention(nc, "sb", X, stats, lnT, c, W_sb, w_in_sb, (row_sb, row_in_sb), H1, DQK1, DV1, c["half"],
                       conv_bias=(a["sb_conv"], scratch), loads=gf_loads)

        layer_norm(nc, 5, ln, X, stats, lnT, c)
        grouped_ffn(nc, "gf", X, lnT, c, gf_dram, gf_W, gf_in, out)


def shape_constants():
    import numpy as np

    p = np.arange(P)
    d = p % D0
    spread = np.zeros((P, P), np.float32)
    spread[32 * (p // 32) + D0, p] = 1.0
    freqs = (np.float32(10000.0) ** (-np.arange(0, D0, 2, dtype=np.float32) / np.float32(D0))).astype(np.float32)
    angles = (np.arange(S, dtype=np.float32)[:, None] * freqs).astype(np.float32)
    sign = np.where(d < D0 // 2, -1.0, 1.0).astype(np.float32)[:, None]
    e, j = np.divmod(np.arange(NE * NE), NE)
    parts = {
        "ident": np.eye(P),
        "spread": spread,
        "hmask": np.stack([(p % 32) // D0 == h for h in range(2)], 1),
        "cos": np.cos(angles)[:, d // 2].T,
        "sin": np.sin(angles)[:, d // 2].T * sign,
        "lower": np.tile((j < e)[None], (P, 1)),
        "eighth": np.stack([p // D0 == h for h in range(8)], 1),
        "half": np.stack([p // (P // 2) == h for h in range(2)], 1),
    }
    return np.ascontiguousarray(np.concatenate([parts[k] for k in CONST], 1).astype(np.float32))


def kernel(**inputs):
    import numpy as np
    import concourse.bacc as bacc
    from concourse.bass_utils import run_bass_kernel_spmd

    i = {k: np.asarray(v) for k, v in inputs.items()}

    def rows(w):
        return w.reshape(-1, P, w.shape[-1]).transpose(1, 0, 2)

    def quads(w):
        n = w.size // D
        o = np.zeros((4, 32, 4, n), w.dtype)
        o[:, :D0] = w.reshape(4, 4, D0, n).transpose(1, 2, 0, 3)
        return o.reshape(P, 4, n)

    def by_head_of_pair(w, heads):
        return rows(w.reshape(D, heads // 2, 2, -1).transpose(0, 2, 1, 3).reshape(D, D)).reshape(P, CH, 2, P)

    wq, wkv, bkv = i["L0_xattn_Wq"], i["L0_xattn_Wkv"], i["L0_xattn_bkv"]
    pairs = rows(wq).reshape(P, CH, 8, 1, 32)
    w_q, w_k, w_v = np.split(i["L0_attn_w_qkv"], 3, axis=1)
    turn = (np.arange(H0)[:, None] * D0 + np.concatenate([np.arange(1, D0, 2), np.arange(0, D0, 2)])).ravel()
    qk = i["L1_attn_W_qk"]
    halves = lambda w: w.reshape(D, 2, FE).transpose(1, 0, 2)
    gate_w = np.concatenate([i["L0_ffn_w_gate"], halves(i["L0_ffn_sw_gate"])])
    up_w = np.concatenate([i["L0_ffn_w_up"], halves(i["L0_ffn_sw_up"])])
    down_w = np.concatenate([i["L0_ffn_w_down"], i["L0_ffn_sw_down"].reshape(2, FE, D)])
    down = np.zeros((NX, 3 * P, D), down_w.dtype)
    down[:, :FE] = down_w
    W = i["L1_xattn_W"]
    arrays = {
        "x": i["x"].reshape(T * P, D),
        "consts": shape_constants(),
        "ctxT": i["ctx_1024"].transpose(0, 2, 1).reshape(B, CH, P, NK).transpose(0, 2, 1, 3),
        "xa_wq": np.broadcast_to(pairs, (P, CH, 8, 3, 32)).reshape(P, CH, 8, 96),
        "xa_bq": np.tile(i["L0_xattn_bq"].reshape(8, 32).T, (3, 1)),
        "xa_wk": rows(wkv[:, 0::2]),
        "xa_bk": bkv[0::2].reshape(CH, P).T,
        "xa_wv": rows(wkv[:, 1::2]),
        "xa_bv": quads(bkv[1::2])[:, :, 0],
        "xa_wo": quads(i["L0_xattn_Wout"]),
        "xa_bo": i["L0_xattn_bout"],
        "sa_q": rows(w_q), "sa_qr": rows(w_q[:, turn]), "sa_k": rows(w_k), "sa_kr": rows(w_k[:, turn]),
        "sa_v": by_head_of_pair(w_v, H0), "sa_o": rows(i["L0_attn_w_out"]), "sa_bo": i["L0_attn_b_out"],
        "moe_gate": rows(i["L0_ffn_gate_w"].T),
        "moe_gu": np.stack([gate_w, up_w], 2).reshape(NX, CH, P, 2, FE).transpose(0, 2, 1, 3, 4),
        "moe_down": down.reshape(NX, 3, P, D).transpose(0, 2, 1, 3),
        "mc_w1": rows(W[:, :D].T), "mc_w2": rows(W[:, D:].T), "mc_b": i["L1_xattn_b"],
        "sb_q": rows(qk[:, :H1 * DQK1]), "sb_k": rows(qk[:, H1 * DQK1:]), "sb_v": by_head_of_pair(i["L1_attn_W_v"], H1),
        "sb_o": rows(i["L1_attn_W_out"]), "sb_bo": i["L1_attn_b_out"], "sb_conv": i["L1_attn_conv"],
        "gf_w1": i["L1_ffn_W1"].transpose(0, 2, 1).reshape(T, CH, P, 1024).transpose(0, 2, 1, 3),
        "gf_b1": i["L1_ffn_b1"].reshape(T, 8, P).transpose(2, 0, 1),
        "gf_w2": i["L1_ffn_W2"].transpose(0, 2, 1).reshape(T, 8, P, D).transpose(0, 2, 1, 3),
        "gf_b2": i["L1_ffn_b2"],
    }
    arrays = {k: np.ascontiguousarray(v) for k, v in arrays.items()}
    nc = bacc.Bacc("TRN2", target_bir_lowering=False, num_devices=1)
    a = {k: nc.dram_tensor("in_" + k, v.shape, mybir.dt.from_np(v.dtype), kind="ExternalInput").ap() for k, v in arrays.items()}
    out = nc.dram_tensor("out_x", (T, P, D), f32, kind="ExternalOutput").ap()
    program(nc, a, out)
    done = run_bass_kernel_spmd(nc, [{"in_" + k: v for k, v in arrays.items()}], core_ids=[0])
    return done.results[0]["out_x"].reshape(B, S, D)
```
